# Optimizing a Trainium2 kernel written in Bass

```python
import numpy as np
import jax
import jax.numpy as jnp

def _softmax(x, axis=-1):
    return jax.nn.softmax(x, axis=axis)

def _gelu(x):
    return jax.nn.gelu(x, approximate=True)

def _silu(x):
    return jax.nn.silu(x)

def _sigmoid(x):
    return jax.nn.sigmoid(x)

def _layernorm(x, axis=-1, eps=1e-05):
    m = jnp.mean(x, axis=axis, keepdims=True)
    v = jnp.var(x, axis=axis, keepdims=True)
    return (x - m) / jnp.sqrt(v + eps)

def _scatter_add(tgt, idx, src, axis=0):
    return tgt.at[idx].add(src)

def _segment_sum(src, seg, n):
    return jax.ops.segment_sum(src, seg, n)
kernel_name = 'mk_early_fusion_embed_d1_tok_img1024_r4_e29e15'

def setup_inputs(seed: int=0):
    np.random.seed(seed)
    _w = jnp.asarray

    def _rec_inputs():
        import jax
        import jax.numpy as jnp
        _rk = jax.random.key(seed)
        x = -0.00016672 + 0.999947 * jax.random.normal(jax.random.fold_in(_rk, 1), (32, 3, 96, 96), jnp.float32)
        x_txt = jax.random.randint(jax.random.fold_in(_rk, 51), (32, 77), 0, 12564, jnp.int32)
        return (x, x_txt)
    x, x_txt = _rec_inputs()

    def _L0_tok_setup():
        import jax, jax.numpy as jnp
        import numpy as np
        PATCH = 16

        def _patchify(x, p):
            B, C, H, W = x.shape
            nh, nw = (H // p, W // p)
            x = x.reshape(B, C, nh, p, nw, p)
            x = x.transpose(0, 2, 4, 1, 3, 5)
            return x.reshape(B, nh * nw, C * p * p)
        key = jax.random.key(seed)
        k1, k2, k3, k4, k5 = jax.random.split(key, 5)
        B, C, H = (64, 3, 96)
        d_model = 256
        p = PATCH
        num_patches = (H // p) ** 2
        in_dim = p * p * C
        x = jax.random.normal(k1, (B, C, H, H), dtype=jnp.float32)
        bound = 1.0 / np.sqrt(in_dim)
        W = jax.random.uniform(k2, (d_model, in_dim), dtype=jnp.float32, minval=-bound, maxval=bound)
        b = jax.random.uniform(k3, (d_model,), dtype=jnp.float32, minval=-bound, maxval=bound)
        cls_token = jax.random.normal(k4, (1, 1, d_model), dtype=jnp.float32)
        pos_enc = jax.random.normal(k5, (1, num_patches + 1, d_model), dtype=jnp.float32)
        return {'x': x, 'W': W, 'b': b, 'cls_token': cls_token, 'pos_enc': pos_enc}
    _L0_tok_all = _L0_tok_setup()
    _L0_tok_in = {k: v for k, v in _L0_tok_all.items() if k in ('W', 'b', 'cls_token', 'pos_enc')}
    del _L0_tok_all

    def _L0_txt_setup():
        import jax, jax.numpy as jnp
        import numpy as np
        B, T, D, INNER, N, V, L, P = (4, 1024, 256, 512, 64, 50257, 4, 5000)
        DECAY, INP = (0.95, 0.05)

        def _silu(x):
            return x * jax.nn.sigmoid(x)

        def _layer(x, W_in_l, cw, cb, WB, WC, Dv, Wo, g, b):
            xp = x @ W_in_l.T
            x_in, x_gate = jnp.split(xp, 2, axis=-1)
            xc = jnp.transpose(x_in, (0, 2, 1))
            xc = jnp.pad(xc, ((0, 0), (0, 0), (3, 0)))
            xc = jax.lax.conv_general_dilated(xc, cw, window_strides=(1,), padding='VALID', dimension_numbers=('NCH', 'OIH', 'NCH'), feature_group_count=INNER)
            xc = xc + cb[None, :, None]
            u = _silu(jnp.transpose(xc, (0, 2, 1)))
            Bu = u @ WB.T

            def step(h, bu):
                h = DECAY * h + INP * bu
                return (h, h)
            h0 = jnp.zeros((x.shape[0], Bu.shape[-1]), x.dtype)
            _, hs = jax.lax.scan(step, h0, jnp.swapaxes(Bu, 0, 1))
            hs = jnp.swapaxes(hs, 0, 1)
            y = hs @ WC.T + Dv * u
            y = y * _silu(x_gate)
            y = y @ Wo.T
            z = y + x
            mu = jnp.mean(z, axis=-1, keepdims=True)
            var = jnp.var(z, axis=-1, keepdims=True)
            return (z - mu) * jax.lax.rsqrt(var + 1e-05) * g + b
        key = jax.random.key(seed)
        ks = jax.random.split(key, 10)
        s = 0.02
        return {'tokens': jax.random.randint(ks[0], (B, T), 0, V), 'tok_emb': jax.random.normal(ks[1], (V, D), jnp.float32) * s, 'pos_emb': jax.random.normal(ks[2], (P, D), jnp.float32) * s, 'W_in': jax.random.normal(ks[3], (L, 2 * INNER, D), jnp.float32) * s, 'conv_w': jax.random.normal(ks[4], (L, INNER, 1, 4), jnp.float32) * s, 'conv_b': jnp.zeros((L, INNER), jnp.float32), 'W_B': jax.random.normal(ks[5], (L, N, INNER), jnp.float32) * s, 'W_C': jax.random.normal(ks[6], (L, INNER, N), jnp.float32) * s, 'D_vec': jax.random.normal(ks[7], (L, INNER), jnp.float32) * s, 'W_out': jax.random.normal(ks[8], (L, D, INNER), jnp.float32) * s, 'ln_g': jnp.ones((L, D), jnp.float32), 'ln_b': jnp.zeros((L, D), jnp.float32)}
    _L0_txt_all = _L0_txt_setup()
    _L0_txt_in = {k: v for k, v in _L0_txt_all.items() if k in ('tok_emb', 'pos_emb', 'W_in', 'conv_w', 'conv_b', 'W_B', 'W_C', 'D_vec', 'W_out', 'ln_g', 'ln_b')}
    del _L0_txt_all

    def _L0_attn_setup():
        import jax, jax.numpy as jnp
        import numpy as np
        import math
        DIM, DIM_QK, DIM_V = (256, 128, 256)
        NUM_BUCKETS, MAX_DISTANCE = (32, 128)

        def silu(x):
            return x * jax.nn.sigmoid(x)

        def laplacian_attn_fn(x):
            mu = math.sqrt(0.5)
            std = math.sqrt(0.25 * math.pi)
            return (1.0 + jax.lax.erf((x - mu) / (std * math.sqrt(2.0)))) * 0.5

        def rel_pos_bias(seq_len, table, scale):
            q_pos = jnp.arange(seq_len)
            k_pos = jnp.arange(seq_len)
            rel_pos = k_pos[None, :] - q_pos[:, None]
            n = jnp.maximum(-rel_pos, 0)
            max_exact = NUM_BUCKETS // 2
            is_small = n < max_exact
            n_safe = jnp.maximum(n, 1).astype(jnp.float32)
            val_if_large = max_exact + (jnp.log(n_safe / max_exact) / math.log(MAX_DISTANCE / max_exact) * (NUM_BUCKETS - max_exact)).astype(jnp.int32)
            val_if_large = jnp.minimum(val_if_large, NUM_BUCKETS - 1)
            bucket = jnp.where(is_small, n, val_if_large)
            return table[bucket] * scale
        key = jax.random.key(seed)
        ks = jax.random.split(key, 8)
        B, S = (4, 512)
        lin_std_qk = 1.0 / math.sqrt(DIM)
        return {'x': jax.random.normal(ks[0], (B, S, DIM), dtype=jnp.float32), 'wqk': jax.random.uniform(ks[1], (DIM, DIM_QK), minval=-lin_std_qk, maxval=lin_std_qk, dtype=jnp.float32), 'bqk': jnp.zeros((DIM_QK,), dtype=jnp.float32), 'gamma': 1.0 + 0.02 * jax.random.normal(ks[2], (2, DIM_QK), dtype=jnp.float32), 'beta': jnp.zeros((2, DIM_QK), dtype=jnp.float32), 'wv': jax.random.uniform(ks[3], (DIM, DIM_V), minval=-lin_std_qk, maxval=lin_std_qk, dtype=jnp.float32), 'bv': jnp.zeros((DIM_V,), dtype=jnp.float32), 'rel_bias': jax.random.normal(ks[4], (NUM_BUCKETS,), dtype=jnp.float32)}
    _L0_attn_all = _L0_attn_setup()
    _L0_attn_in = {k: v for k, v in _L0_attn_all.items() if k in ('wqk', 'bqk', 'gamma', 'beta', 'wv', 'bv', 'rel_bias')}
    del _L0_attn_all

    def _L0_ffn_setup():
        import jax, jax.numpy as jnp
        import numpy as np
        D_MODEL = 256
        D_FFN = 512
        N_EXPERTS = 8
        TOP_K = 2
        B, S = (2, 512)
        LN_EPS = 1e-05
        key = jax.random.key(seed)
        ks = jax.random.split(key, 6)
        scale = 0.02
        x = jax.random.normal(ks[0], (B, S, D_MODEL), dtype=jnp.float32)
        w_router = jax.random.normal(ks[1], (N_EXPERTS, D_MODEL), dtype=jnp.float32) * scale
        w_gate = jax.random.normal(ks[2], (N_EXPERTS, D_FFN, D_MODEL), dtype=jnp.float32) * scale
        w_up = jax.random.normal(ks[3], (N_EXPERTS, D_FFN, D_MODEL), dtype=jnp.float32) * scale
        w_down = jax.random.normal(ks[4], (N_EXPERTS, D_MODEL, D_FFN), dtype=jnp.float32) * scale
        ln_gamma = jnp.ones((D_MODEL,), dtype=jnp.float32)
        ln_beta = jnp.zeros((D_MODEL,), dtype=jnp.float32)
        return {'x': x, 'w_router': w_router, 'w_gate': w_gate, 'w_up': w_up, 'w_down': w_down, 'ln_gamma': ln_gamma, 'ln_beta': ln_beta}
    _L0_ffn_all = _L0_ffn_setup()
    _L0_ffn_in = {k: v for k, v in _L0_ffn_all.items() if k in ('w_router', 'w_gate', 'w_up', 'w_down', 'ln_gamma', 'ln_beta')}
    del _L0_ffn_all
    return {'x': x, 'x_txt': x_txt, 'L0_tok_W': _L0_tok_in['W'], 'L0_tok_b': _L0_tok_in['b'], 'L0_tok_cls_token': _L0_tok_in['cls_token'], 'L0_tok_pos_enc': _L0_tok_in['pos_enc'], 'L0_txt_tok_emb': _L0_txt_in['tok_emb'], 'L0_txt_pos_emb': _L0_txt_in['pos_emb'], 'L0_txt_W_in': _L0_txt_in['W_in'], 'L0_txt_conv_w': _L0_txt_in['conv_w'], 'L0_txt_conv_b': _L0_txt_in['conv_b'], 'L0_txt_W_B': _L0_txt_in['W_B'], 'L0_txt_W_C': _L0_txt_in['W_C'], 'L0_txt_D_vec': _L0_txt_in['D_vec'], 'L0_txt_W_out': _L0_txt_in['W_out'], 'L0_txt_ln_g': _L0_txt_in['ln_g'], 'L0_txt_ln_b': _L0_txt_in['ln_b'], 'L0_attn_wqk': _L0_attn_in['wqk'], 'L0_attn_bqk': _L0_attn_in['bqk'], 'L0_attn_gamma': _L0_attn_in['gamma'], 'L0_attn_beta': _L0_attn_in['beta'], 'L0_attn_wv': _L0_attn_in['wv'], 'L0_attn_bv': _L0_attn_in['bv'], 'L0_attn_rel_bias': _L0_attn_in['rel_bias'], 'L0_ffn_w_router': _L0_ffn_in['w_router'], 'L0_ffn_w_gate': _L0_ffn_in['w_gate'], 'L0_ffn_w_up': _L0_ffn_in['w_up'], 'L0_ffn_w_down': _L0_ffn_in['w_down'], 'L0_ffn_ln_gamma': _L0_ffn_in['ln_gamma'], 'L0_ffn_ln_beta': _L0_ffn_in['ln_beta']}

def reference(x, x_txt, L0_tok_W, L0_tok_b, L0_tok_cls_token, L0_tok_pos_enc, L0_txt_tok_emb, L0_txt_pos_emb, L0_txt_W_in, L0_txt_conv_w, L0_txt_conv_b, L0_txt_W_B, L0_txt_W_C, L0_txt_D_vec, L0_txt_W_out, L0_txt_ln_g, L0_txt_ln_b, L0_attn_wqk, L0_attn_bqk, L0_attn_gamma, L0_attn_beta, L0_attn_wv, L0_attn_bv, L0_attn_rel_bias, L0_ffn_w_router, L0_ffn_w_gate, L0_ffn_w_up, L0_ffn_w_down, L0_ffn_ln_gamma, L0_ffn_ln_beta):
    import jax
    import jax.numpy as jnp

    def _L0_tok_ref(x, W, b, cls_token, pos_enc):
        import jax, jax.numpy as jnp
        import numpy as np
        PATCH = 16

        def _patchify(x, p):
            B, C, H, W = x.shape
            nh, nw = (H // p, W // p)
            x = x.reshape(B, C, nh, p, nw, p)
            x = x.transpose(0, 2, 4, 1, 3, 5)
            return x.reshape(B, nh * nw, C * p * p)
        B = x.shape[0]
        patches = _patchify(x, PATCH)
        proj = jnp.einsum('bnf,df->bnd', patches, W) + b
        cls = jnp.broadcast_to(cls_token, (B, 1, cls_token.shape[-1]))
        out = jnp.concatenate([cls, proj], axis=1) + pos_enc
        return out

    def _L0_txt_ref(tokens, tok_emb, pos_emb, W_in, conv_w, conv_b, W_B, W_C, D_vec, W_out, ln_g, ln_b):
        import jax, jax.numpy as jnp
        import numpy as np
        B, T, D, INNER, N, V, L, P = (4, 1024, 256, 512, 64, 50257, 4, 5000)
        DECAY, INP = (0.95, 0.05)

        def _silu(x):
            return x * jax.nn.sigmoid(x)

        def _layer(x, W_in_l, cw, cb, WB, WC, Dv, Wo, g, b):
            xp = x @ W_in_l.T
            x_in, x_gate = jnp.split(xp, 2, axis=-1)
            xc = jnp.transpose(x_in, (0, 2, 1))
            xc = jnp.pad(xc, ((0, 0), (0, 0), (3, 0)))
            xc = jax.lax.conv_general_dilated(xc, cw, window_strides=(1,), padding='VALID', dimension_numbers=('NCH', 'OIH', 'NCH'), feature_group_count=INNER)
            xc = xc + cb[None, :, None]
            u = _silu(jnp.transpose(xc, (0, 2, 1)))
            Bu = u @ WB.T

            def step(h, bu):
                h = DECAY * h + INP * bu
                return (h, h)
            h0 = jnp.zeros((x.shape[0], Bu.shape[-1]), x.dtype)
            _, hs = jax.lax.scan(step, h0, jnp.swapaxes(Bu, 0, 1))
            hs = jnp.swapaxes(hs, 0, 1)
            y = hs @ WC.T + Dv * u
            y = y * _silu(x_gate)
            y = y @ Wo.T
            z = y + x
            mu = jnp.mean(z, axis=-1, keepdims=True)
            var = jnp.var(z, axis=-1, keepdims=True)
            return (z - mu) * jax.lax.rsqrt(var + 1e-05) * g + b
        x = tok_emb[tokens] + pos_emb[jnp.arange(tokens.shape[1])][None]
        for l in range(L):
            x = _layer(x, W_in[l], conv_w[l], conv_b[l], W_B[l], W_C[l], D_vec[l], W_out[l], ln_g[l], ln_b[l])
        return x

    def _L0_attn_ref(x, wqk, bqk, gamma, beta, wv, bv, rel_bias):
        import jax, jax.numpy as jnp
        import numpy as np
        import math
        DIM, DIM_QK, DIM_V = (256, 128, 256)
        NUM_BUCKETS, MAX_DISTANCE = (32, 128)

        def silu(x):
            return x * jax.nn.sigmoid(x)

        def laplacian_attn_fn(x):
            mu = math.sqrt(0.5)
            std = math.sqrt(0.25 * math.pi)
            return (1.0 + jax.lax.erf((x - mu) / (std * math.sqrt(2.0)))) * 0.5

        def rel_pos_bias(seq_len, table, scale):
            q_pos = jnp.arange(seq_len)
            k_pos = jnp.arange(seq_len)
            rel_pos = k_pos[None, :] - q_pos[:, None]
            n = jnp.maximum(-rel_pos, 0)
            max_exact = NUM_BUCKETS // 2
            is_small = n < max_exact
            n_safe = jnp.maximum(n, 1).astype(jnp.float32)
            val_if_large = max_exact + (jnp.log(n_safe / max_exact) / math.log(MAX_DISTANCE / max_exact) * (NUM_BUCKETS - max_exact)).astype(jnp.int32)
            val_if_large = jnp.minimum(val_if_large, NUM_BUCKETS - 1)
            bucket = jnp.where(is_small, n, val_if_large)
            return table[bucket] * scale
        B, S, _ = x.shape
        qk = silu(x @ wqk + bqk)
        q = qk * gamma[0] + beta[0]
        k = qk * gamma[1] + beta[1]
        v = silu(x @ wv + bv)
        scale = 1.0 / S
        sim = jnp.einsum('bid,bjd->bij', q, k) * scale
        sim = sim + rel_pos_bias(S, rel_bias, DIM_QK ** 0.5)[None, :, :]
        attn = laplacian_attn_fn(sim)
        causal_mask = jnp.triu(jnp.ones((S, S), dtype=bool), k=1)
        attn = jnp.where(causal_mask[None, :, :], 0.0, attn)
        return jnp.einsum('bij,bjd->bid', attn, v)

    def _L0_ffn_ref(x, w_router, w_gate, w_up, w_down, ln_gamma, ln_beta):
        import jax, jax.numpy as jnp
        import numpy as np
        D_MODEL = 256
        D_FFN = 512
        N_EXPERTS = 8
        TOP_K = 2
        B, S = (2, 512)
        LN_EPS = 1e-05
        logits = jnp.einsum('bsd,ed->bse', x, w_router)
        top_vals, top_idx = jax.lax.top_k(logits, TOP_K)
        rw = jax.nn.softmax(top_vals, axis=-1)
        gate = jnp.einsum('bsd,efd->ebsf', x, w_gate)
        up = jnp.einsum('bsd,efd->ebsf', x, w_up)
        h = jax.nn.silu(gate) * up
        y = jnp.einsum('ebsf,edf->bsed', h, w_down)
        sel = jnp.take_along_axis(y, top_idx[..., None], axis=2)
        out = jnp.sum(rw[..., None] * sel, axis=2)
        mu = jnp.mean(out, axis=-1, keepdims=True)
        var = jnp.mean(jnp.square(out - mu), axis=-1, keepdims=True)
        out = (out - mu) * jax.lax.rsqrt(var + LN_EPS)
        return out * ln_gamma + ln_beta
    h = _L0_tok_ref(x, L0_tok_W, L0_tok_b, L0_tok_cls_token, L0_tok_pos_enc)
    h = jnp.concatenate([h, _L0_txt_ref(x_txt, L0_txt_tok_emb, L0_txt_pos_emb, L0_txt_W_in, L0_txt_conv_w, L0_txt_conv_b, L0_txt_W_B, L0_txt_W_C, L0_txt_D_vec, L0_txt_W_out, L0_txt_ln_g, L0_txt_ln_b)], axis=1)
    h = h + _L0_attn_ref(_layernorm(h, axis=-1), L0_attn_wqk, L0_attn_bqk, L0_attn_gamma, L0_attn_beta, L0_attn_wv, L0_attn_bv, L0_attn_rel_bias)
    h = h + _L0_ffn_ref(_layernorm(h, axis=-1), L0_ffn_w_router, L0_ffn_w_gate, L0_ffn_w_up, L0_ffn_w_down, L0_ffn_ln_gamma, L0_ffn_ln_beta)
    return h

_drawn_inputs = setup_inputs


def setup_inputs(seed=0):
    import zlib

    import numpy as np

    out = dict(_drawn_inputs(seed))
    spreads = {'L0_txt_conv_b': (0.0, 0.8),
     'L0_txt_ln_g': (1.0, 0.2),
     'L0_txt_ln_b': (0.0, 0.1),
     'L0_attn_bqk': (0.0, 2.0),
     'L0_attn_beta': (0.0, 2.0),
     'L0_attn_bv': (0.0, 0.1),
     'L0_ffn_ln_gamma': (1.0, 0.6),
     'L0_ffn_ln_beta': (0.0, 0.836)}
    factors = {'L0_txt_W_in': 8.0,
     'L0_txt_conv_w': 8.0,
     'L0_txt_W_B': 8.0,
     'L0_txt_W_C': 8.0,
     'L0_txt_D_vec': 8.0,
     'L0_txt_W_out': 8.0,
     'L0_attn_wqk': 44.064,
     'L0_attn_gamma': 64.0,
     'L0_attn_rel_bias': 8.0}
    for name, (base, spread) in spreads.items():
        noise = np.random.default_rng([zlib.crc32(name.encode()), seed]).standard_normal(out[name].shape)
        drawn = base * np.exp(spread * noise) if base else spread * noise
        out[name] = jnp.asarray(drawn.astype(out[name].dtype))
    for name, factor in factors.items():
        out[name] = (out[name] * factor).astype(out[name].dtype)
    return out
```

```python
from contextlib import ExitStack

import concourse.bass as bass
from concourse import mybir

F32 = mybir.dt.float32
I32 = mybir.dt.int32
U32 = mybir.dt.uint32
ACT = mybir.ActivationFunctionType
ALU = mybir.AluOpType
AX = mybir.AxisListType.X

P = 128
BATCH, TXT, PATCHES = 32, 77, 36
SEQ = 1 + PATCHES + TXT
D = 256
DC = D // P
IN_CH = 768
INNER, STATE, LAYERS = 512, 64, 4
FC = INNER // P
GB = 4
GROUPS = BATCH // GB
GT = GB * TXT
TILE_ROWS = (104, 104, 100)
TILE_AT = (0, 104, 208)
TR = TILE_ROWS[0]
NT = len(TILE_ROWS)
PADT = TXT + 3
PT_SEQS = 3
PT = PT_SEQS * PATCHES
PT_FULL = BATCH // PT_SEQS
PT_TAIL = (BATCH - PT_FULL * PT_SEQS) * PATCHES
QK = 128
GS = GB * SEQ
EXPERTS, FFN = 8, 512
TOKENS = BATCH * SEQ
REGION = TOKENS + P + (-TOKENS) % P
FULL_BLOCKS = 2 * TOKENS // P
BLOCKS = FULL_BLOCKS + EXPERTS - 1
BLOCKS += BLOCKS % 2
SPARE = BLOCKS - FULL_BLOCKS
XROWS = EXPERTS * REGION + SPARE * P
YROWS = 2 * TOKENS + (EXPERTS + SPARE) * P
ROW = D + 2
COUNT_STEPS = -(-TOKENS // P)
EPS = 1e-5
LAP_MU = 0.5 ** 0.5
LAP_STD = (0.25 * 3.141592653589793) ** 0.5
TINY = 1e-30

C_ID = 0
C_TRI = C_ID + P
C_ONE = C_TRI + P
C_BUCKET = C_ONE + P
C_EXP = C_BUCKET + P
C_BASE = C_EXP + EXPERTS
C_PADROW = C_BASE + EXPERTS
C_PADDEST = C_PADROW + EXPERTS
C_TOK = C_PADDEST + EXPERTS + SPARE
C_STEPS = C_TOK + BATCH
C_BLOCK = C_STEPS + COUNT_STEPS
C_B32 = C_BLOCK + BLOCKS
CONSTS = C_B32 + 32

W_CONV = 0
W_CB = W_CONV + LAYERS * FC * 4
W_D = W_CB + LAYERS * FC
W_LN = W_D + LAYERS * FC
W_QK = W_LN + LAYERS * DC * 2
W_R = W_QK + 5
SMALL = W_R + DC * EXPERTS


class Chain:

    def __init__(self, eng, sem, per, iteration):
        self.eng, self.sem, self.base, self.n, self.per = eng, sem, iteration * per, 0, per

    def inc(self, instruction):
        instruction.then_inc(self.sem, 1)
        self.n += 1
        assert self.n <= self.per
        return self.n

    def wait(self, n):
        self.eng.wait_ge(self.sem, self.base + n)

    def done(self):
        assert self.n == self.per, self.n


def wait(eng, sem, value):
    if not (isinstance(value, int) and value <= 0):
        eng.wait_ge(sem, value)


def settled(eng, sem):
    eng.sem_inc(sem, 1)


def text_steps(eng, body):
    for layer in range(LAYERS):
        body(layer, 0)
        body(layer, 1)
        with eng.Fori(2, GROUPS) as g:
            body(layer, g)
    body(LAYERS, 0)
    body(LAYERS, 1)


def back(layer, g, k):
    if isinstance(g, int) and g < k:
        return layer - 1, g + GROUPS - k
    return layer, g - k


def pairs_after_first(eng, n, body):
    body(1, 1)
    with eng.Fori(1, n // 2) as pair:
        for k in range(2):
            body(pair * 2 + k, k)


def build(nc, patches, patches_tail, tokens, tok_w, tok_b, cls, pos_enc, tok_emb, pos_emb, w_in, w_b, w_c, w_out,
          small, ln_gb, wqk, wv, bv, rel_bias, w_gate, w_up, w_down, ffn_gb, consts, out):
    ctx = ExitStack()
    with ctx:
        def sb(name, shape, dt=F32):
            return ctx.enter_context(nc.sbuf_tensor(name, shape, dt))

        def sem(name):
            return ctx.enter_context(nc.semaphore(name))

        seq = nc.dram_tensor("seq", (TOKENS, D), F32, kind="Internal").ap()
        xrows = nc.dram_tensor("xrows", (XROWS, ROW), F32, kind="Internal").ap()
        yrows = nc.dram_tensor("yrows", (YROWS, D), F32, kind="Internal").ap()

        cst = sb("cst", [P, CONSTS])
        sml = sb("sml", [P, SMALL])
        h_all = sb("h_all", [SEQ, BATCH, D])
        ident = cst[:, C_ID:C_ID + P]
        tri = cst[0:SEQ, C_TRI:C_TRI + SEQ]
        ones = cst[0:SEQ, C_ONE:C_ONE + SEQ]
        expert_no = cst[0:SEQ, C_EXP:C_EXP + EXPERTS]
        bias_t = sb("bias_t", [SEQ, SEQ])
        wqk_s = sb("wqk_s", [P, DC, QK])
        wv_s = sb("wv_s", [P, DC, D])
        minus_half = sb("minus_half", [P, GB])
        tab_s = sb("tab_s", [SEQ, 32])
        base_m = sb("base_m", [SEQ, EXPERTS])
        dest_i = sb("dest_i", [P, 2], I32)
        row_wt = sb("row_wt", [P, 2])

        FFN_COLS = DC * EXPERTS * FFN * 2 + FC * EXPERTS * D
        TEXT_COLS = LAYERS * (DC * 2 * INNER + FC * STATE + INNER + FC * D) + DC * BATCH * TXT + GROUPS * NT * D
        arena_a = sb("arena_a", [P, max(FFN_COLS, TEXT_COLS)])
        at = [0]

        def part(arena, cols, shape=None, rows=P):
            v = arena[0:rows, at[0]:at[0] + cols]
            at[0] += cols
            assert at[0] <= arena.shape[1], (at[0], arena.shape)
            return v

        win_s = part(arena_a, LAYERS * DC * 2 * INNER).rearrange("p (l c n) -> p l c n", l=LAYERS, c=DC)
        wb_s = part(arena_a, LAYERS * FC * STATE).rearrange("p (l c n) -> p l c n", l=LAYERS, c=FC)
        wc_s = part(arena_a, LAYERS * INNER, rows=STATE).rearrange("p (l n) -> p l n", l=LAYERS)
        wo_s = part(arena_a, LAYERS * FC * D).rearrange("p (l c n) -> p l c n", l=LAYERS, c=FC)
        xt = part(arena_a, DC * BATCH * TXT).rearrange("p (c t) -> p c t", c=DC)
        xtok = part(arena_a, GROUPS * NT * D, rows=TR)
        at[0] = 0
        wg_s = part(arena_a, DC * EXPERTS * FFN).rearrange("p (c n) -> p c n", c=DC)
        wu_s = part(arena_a, DC * EXPERTS * FFN).rearrange("p (c n) -> p c n", c=DC)
        wd_s = part(arena_a, FC * EXPERTS * D).rearrange("p (c n) -> p c n", c=FC)
        a_vb = part(arena_a, GB * D, rows=SEQ).rearrange("p (k d) -> p k d", k=GB)
        ffn_s = part(arena_a, 2 * D, rows=SEQ).rearrange("p (s d) -> p s d", s=2)
        bv_s = part(arena_a, D, rows=SEQ)

        arena_b = sb("arena_b", [P, 11264])
        at[0] = 0
        xin = part(arena_b, FC * GB * PADT).rearrange("p (c b t) -> p c b t", c=FC, b=GB)
        acc = part(arena_b, FC * GT).rearrange("p (c t) -> p c t", c=FC)
        u = part(arena_b, FC * GT).rearrange("p (c t) -> p c t", c=FC)
        sg = part(arena_b, FC * GT).rearrange("p (c t) -> p c t", c=FC)
        yt = part(arena_b, FC * GT).rearrange("p (c t) -> p c t", c=FC)
        bu = part(arena_b, GT, rows=STATE)
        hs = part(arena_b, GT, rows=STATE)
        decay = part(arena_b, GT, rows=STATE)
        z = part(arena_b, NT * D, rows=TR).rearrange("p (j d) -> p j d", j=NT)
        n = part(arena_b, NT * D, rows=TR).rearrange("p (j d) -> p j d", j=NT)
        ng = part(arena_b, NT * D, rows=TR).rearrange("p (j d) -> p j d", j=NT)
        stats = part(arena_b, NT * 6, rows=TR).rearrange("p (j s) -> p j s", j=NT)
        mv = part(arena_b, NT * 2, rows=TR).rearrange("p (j s) -> p j s", j=NT)
        rstd = part(arena_b, 2 * NT, rows=TR).rearrange("p (k j) -> p k j", k=2)
        emb = [part(arena_b, NT * D, rows=TR).rearrange("p (j d) -> p j d", j=NT) for _ in range(2)]
        tokens_s = sb("tokens_s", [TR, GROUPS * NT], I32)
        tok_now = sb("tok_now", [TR, 2, NT], I32)
        arena_c = sb("arena_c", [P, (EXPERTS + SPARE) * ROW])
        padbuf = arena_c[:, :].rearrange("p (k d) -> p k d", d=ROW)
        at[0] = 0
        pos_s = part(arena_c, NT * D, rows=TR).rearrange("p (j d) -> p j d", j=NT)
        gb_s = part(arena_c, LAYERS * 2 * D, rows=TR).rearrange("p (l s d) -> p l s d", l=LAYERS, s=2)
        h_flat = h_all[:, :, :].rearrange("p b d -> p (b d)")
        at[0] = FC * GB * PADT
        tokw_s = part(arena_b, IN_CH // P * D).rearrange("p (c d) -> p c d", c=IN_CH // P)
        pat = [part(arena_b, IN_CH // P * PT).rearrange("p (c t) -> p c t", c=IN_CH // P) for _ in range(2)]
        pat_out = [h_flat[0:PT, k * D:(k + 1) * D] for k in range(2)]
        posb = h_flat[0:PT, 2 * D:3 * D]
        tokb = h_flat[0:PT, 3 * D:4 * D]
        cls_s = h_flat[0:BATCH, 4 * D:5 * D]
        pos0 = h_flat[0:BATCH, 5 * D:6 * D]
        oh = h_flat[:, 8 * D:8 * D + 114 * 32 // 2]

        at[0] = 0
        a_n = part(arena_b, GB * D, rows=SEQ).rearrange("p (k d) -> p k d", k=GB)
        a_nt = part(arena_b, DC * GS).rearrange("p (c t) -> p c t", c=DC)
        a_qk = part(arena_b, GS)
        a_q = [part(arena_b, GS) for _ in range(2)]
        a_k = [part(arena_b, GS) for _ in range(2)]
        a_v = [part(arena_b, GB * D, rows=SEQ).rearrange("p (k d) -> p k d", k=GB) for _ in range(2)]
        a_arg = part(arena_b, GS, rows=SEQ)
        a_rc = sb("a_rc", [SEQ, GS])[:, :]
        a_w = part(arena_b, GS, rows=SEQ)
        a_x = [part(arena_b, GB * ROW, rows=SEQ).rearrange("p (k d) -> p k d", k=GB) for _ in range(2)]
        m_t = part(arena_b, DC * GS).rearrange("p (c t) -> p c t", c=DC)
        a_st = part(arena_b, GB * 6, rows=SEQ).rearrange("p (k s) -> p k s", k=GB)
        a_mv = part(arena_b, GB * 2, rows=SEQ).rearrange("p (k s) -> p k s", k=GB)
        a_rs = part(arena_b, GB * 2, rows=SEQ).rearrange("p (s k) -> p s k", s=2)
        m_st = part(arena_b, GB * 6, rows=SEQ).rearrange("p (k s) -> p k s", k=GB)
        m_mv = part(arena_b, GB * 2, rows=SEQ).rearrange("p (k s) -> p k s", k=GB)
        m_rs = part(arena_b, GB * 2, rows=SEQ).rearrange("p (s k) -> p s k", s=2)
        lg = part(arena_b, GB * 8, rows=SEQ).rearrange("p (k e) -> p k e", k=GB)
        top = part(arena_b, GB * 8, rows=SEQ).rearrange("p (k e) -> p k e", k=GB)
        idx_f = part(arena_b, GB * 8, rows=SEQ).rearrange("p (k e) -> p k e", k=GB)
        one = [part(arena_b, GB * 8, rows=SEQ).rearrange("p (k e) -> p k e", k=GB) for _ in range(2)]
        both = part(arena_b, GB * 8, rows=SEQ).rearrange("p (k e) -> p k e", k=GB)
        before = part(arena_b, GB * 8, rows=SEQ).rearrange("p (k e) -> p k e", k=GB)
        place = part(arena_b, GB * 8, rows=SEQ).rearrange("p (k e) -> p k e", k=GB)
        picked = [part(arena_b, GB * 8, rows=SEQ).rearrange("p (k e) -> p k e", k=GB) for _ in range(2)]
        slot_f = part(arena_b, 2 * GB, rows=SEQ).rearrange("p (r k) -> p r k", r=2)
        gap = part(arena_b, GB, rows=SEQ)
        gap_tanh = part(arena_b, GB, rows=SEQ)
        at[0] = 0
        cnt = part(arena_b, EXPERTS)
        padrow_f = part(arena_b, EXPERTS)
        steps_b = part(arena_b, EXPERTS * COUNT_STEPS).rearrange("p (e k) -> p e k", e=EXPERTS)
        ntile = part(arena_b, EXPERTS)
        ends = part(arena_b, EXPERTS)
        delta = part(arena_b, EXPERTS)
        passed = part(arena_b, BLOCKS * EXPERTS).rearrange("p (j e) -> p j e", e=EXPERTS)
        shifts = part(arena_b, BLOCKS * EXPERTS).rearrange("p (j e) -> p j e", e=EXPERTS)
        expert_f = part(arena_b, BLOCKS)
        row_f = part(arena_b, BLOCKS)
        idx_u = sb("idx_u", [SEQ, GB, 8], U32)
        slot_i = sb("slot_i", [SEQ, 2, GB], I32)
        padrow_i = sb("padrow_i", [P, EXPERTS], I32)
        expert_i = sb("expert_i", [P, BLOCKS], I32)
        row_i = sb("row_i", [P, BLOCKS], I32)

        at[0] = 0
        x_g = [part(arena_b, ROW) for _ in range(2)]
        x_gt = [part(arena_b, DC * P).rearrange("p (c t) -> p c t", c=DC) for _ in range(2)]
        f_sg = part(arena_b, FFN)
        f_h = part(arena_b, FFN)
        f_ht = [part(arena_b, FFN).rearrange("p (c t) -> p c t", c=FC) for _ in range(2)]
        f_y = [part(arena_b, D) for _ in range(2)]
        at[0] = 0
        y12 = [part(arena_a, GB * 2 * D, rows=SEQ).rearrange("p (k d) -> p k d", k=GB) for _ in range(2)]
        y_sum = part(arena_a, GB * D, rows=SEQ).rearrange("p (k d) -> p k d", k=GB)
        y_n = part(arena_a, GB * D, rows=SEQ).rearrange("p (k d) -> p k d", k=GB)
        y_g = part(arena_a, GB * D, rows=SEQ).rearrange("p (k d) -> p k d", k=GB)
        y_out = [part(arena_a, GB * D, rows=SEQ).rearrange("p (k d) -> p k d", k=GB) for _ in range(2)]
        y_st = part(arena_a, GB * 6, rows=SEQ).rearrange("p (k s) -> p k s", k=GB)
        y_mv = part(arena_a, GB * 2, rows=SEQ).rearrange("p (k s) -> p k s", k=GB)
        y_rs = part(arena_a, GB * 2, rows=SEQ).rearrange("p (s k) -> p s k", s=2)

        bank = [ctx.enter_context(nc.psum_tensor(f"bank{k}", [P, 512], F32)) for k in range(8)]

        ld_cst = sem("ld_cst")
        ld_text = sem("ld_text")
        ld_tokw = sem("ld_tokw")
        ld_attn = sem("ld_attn")
        ld_pos = sem("ld_pos")
        ld_late = sem("ld_late")
        ld_toks = sem("ld_toks")
        ld_pat = [sem(f"ld_pat{k}") for k in range(2)]
        ld_ffn = sem("ld_ffn")
        ld_h = [sem(f"ld_h{k}") for k in range(2)]
        seq_stored = [sem(f"seq_stored{k}") for k in range(3)]
        posb_ready = sem("posb_ready")
        cls_ready = sem("cls_ready")
        pat_mm = sem("pat_mm")
        pat_ready = sem("pat_ready")
        zeroed = sem("zeroed")
        bias_seq = sem("bias_seq")
        tok_copied = sem("tok_copied")
        emb_ready = [sem(f"emb_ready{k}") for k in range(2)]
        pe_x, act_x = sem("pe_x"), sem("act_x")
        pe_g, act_g = sem("pe_g"), sem("act_g")
        pe_b, act_b = sem("pe_b"), sem("act_b")
        pe_c, dve_c, dve_y = sem("pe_c"), sem("dve_c"), sem("dve_y")
        dve_scan, act_u, dve_conv = sem("dve_scan"), sem("act_u"), sem("dve_conv")
        pe_o, dve_z, dve_bn, dve_stats = sem("pe_o"), sem("dve_z"), sem("dve_bn"), sem("dve_stats")
        pool_var, pool_rstd, dve_n = sem("pool_var"), sem("pool_rstd"), sem("dve_n")
        pe_t, act_xt, pool_ng, pool_x = sem("pe_t"), sem("act_xt"), sem("pool_ng"), sem("pool_x")
        dve_passed, pool_passed = sem("dve_passed"), sem("pool_passed")
        at_dve, a_var, m_var, m_seq = sem("at_dve"), sem("a_var"), sem("m_var"), sem("m_seq")
        a_stats, a_rstd, a_norm = sem("a_stats"), sem("a_rstd"), sem("a_norm")
        a_tr, a_trc, a_qkm, a_qks, a_qkd = sem("a_tr"), sem("a_trc"), sem("a_qkm"), sem("a_qks"), sem("a_qkd")
        a_vm, a_va, a_vs = sem("a_vm"), sem("a_va"), sem("a_vs")
        a_sm, a_sa, a_er, a_at = sem("a_sm"), sem("a_sa"), sem("a_er"), sem("a_at")
        a_rec, a_sel = sem("a_rec"), sem("a_sel")
        a_om, a_h2 = sem("a_om"), sem("a_h2")
        m_stats, m_rstd, m_norm, m_tr, m_trc = sem("m_stats"), sem("m_rstd"), sem("m_norm"), sem("m_tr"), sem("m_trc")
        m_lm, m_lg, m_gap, m_wt, m_both, m_rk = sem("m_lm"), sem("m_lg"), sem("m_gap"), sem("m_wt"), sem("m_both"), sem("m_rk")
        m_slot, m_row2, pad_zero = sem("m_slot"), sem("m_row2"), sem("pad_zero")
        x_sent = [sem(f"x_sent{k}") for k in range(2)]
        cnt_mm, tb, tbl_ready, pad_ready, pad_sent, spare_sent = (
            sem("cnt_mm"), sem("tb"), sem("tbl_ready"), sem("pad_ready"), sem("pad_sent"), sem("spare_sent"))
        x_in = [sem(f"x_in{k}") for k in range(2)]
        f_tr, f_trc, f_gm, f_um, f_silu, f_hh = sem("f_tr"), sem("f_trc"), sem("f_gm"), sem("f_um"), sem("f_silu"), sem("f_hh")
        f_hm, f_htc, f_dm, f_yc, f_dest = sem("f_hm"), sem("f_htc"), sem("f_dm"), sem("f_yc"), sem("f_dest")
        y_sent = [sem(f"y_sent{k}") for k in range(2)]
        h2b = sem("h2b")
        y_in = [sem(f"y_in{k}") for k in range(2)]
        yf, y_stats, y_rstd, y_normed, y_gained, y_done = (
            sem("yf"), sem("y_stats"), sem("y_rstd"), sem("y_normed"), sem("y_gained"), sem("y_done"))
        y_var = sem("y_var")
        out_sent = [sem(f"out_sent{k}") for k in range(2)]

        SML = lambda at_, *_: sml[:, at_:at_ + 1]
        seq_b = seq.rearrange("(b s) d -> b s d", s=SEQ)

        def conv_w(layer, c, tap):
            return SML(W_CONV + (layer * FC + c) * 4 + tap)

        def group_rows(tile, g):
            return tile[:, bass.ds(g * (NT * D), NT * D)].rearrange("p (j d) -> p j d", j=NT)

        N_STEPS = LAYERS * GROUPS
        ALL_T = 2 * N_STEPS
        pieces = []
        for j in range(NT):
            t = TILE_AT[j]
            while t < TILE_AT[j] + TILE_ROWS[j]:
                b, p = divmod(t, TXT)
                m = min(TXT - p, TILE_AT[j] + TILE_ROWS[j] - t)
                pieces.append((j, t - TILE_AT[j], m, b, p))
                t += m
        PIECES = len(pieces)

        block = ctx.enter_context(nc.Block())

        def store_out(sp, g):
            sp.wait_ge(y_done, g + 1)
            sp.dma_start(out[g * GB:(g + 1) * GB].rearrange("b s d -> s b d"), y_out[g % 2]).then_inc(out_sent[g % 2], 16)

        @block.sync
        def _(sp):
            sp.dma_start(tokw_s[:, :, :], tok_w).then_inc(ld_tokw, 16)
            for k in range(2):
                sp.dma_start(pat[k][:, :, :], patches[k]).then_inc(ld_pat[k], 16)
            sp.dma_start(cst[:, :], consts).then_inc(ld_cst, 16)
            sp.dma_start(sml[:, :], small).then_inc(ld_cst, 16)
            sp.dma_start(win_s, w_in).then_inc(ld_text, 16)
            sp.dma_start(wb_s, w_b).then_inc(ld_text, 16)
            sp.dma_start(wc_s, w_c).then_inc(ld_text, 16)
            sp.dma_start(wo_s, w_out).then_inc(ld_text, 16)
            sp.dma_start(gb_s[:, :, :, :], ln_gb.partition_broadcast(TR)).then_inc(ld_text, 16)

            def store_patches(i, k, seqs=PT_SEQS):
                sp.wait_ge(pat_ready, i + 1)
                for q in range(seqs):
                    sp.dma_start(seq_b[bass.ds(i * PT_SEQS + q, 1), 1:1 + PATCHES, :].rearrange("b s d -> (b s) d"),
                                 pat_out[k][q * PATCHES:(q + 1) * PATCHES, :]).then_inc(seq_stored[k], 16)

            with sp.Fori(0, PT_FULL // 2 - 1) as pair:
                for k in range(2):
                    i = pair * 2 + k
                    sp.wait_ge(pat_mm, i + 1)
                    sp.dma_start(pat[k][:, :, :], patches[bass.ds(i + 2, 1)].rearrange("a p c t -> (a p) c t"))\
                        .then_inc(ld_pat[k], 16)
                    store_patches(i, k)
            sp.wait_ge(pat_mm, PT_FULL - 1)
            sp.dma_start(pat[0][:, :, 0:PT_TAIL], patches_tail).then_inc(ld_pat[0], 16)
            store_patches(PT_FULL - 2, 0)
            store_patches(PT_FULL - 1, 1)
            store_patches(PT_FULL, 0, PT_TAIL // PATCHES)
            sp.wait_ge(cls_ready, 1)
            sp.dma_start(seq_b[:, 0, :], cls_s).then_inc(seq_stored[1], 16)

            with sp.Fori(0, GROUPS) as g:
                sp.wait_ge(pool_x, g + (LAYERS * GROUPS + 1))
                rows = group_rows(xtok, g)
                for j, r0, m, b, p in pieces:
                    sp.dma_start(seq_b[bass.ds(g * GB + b, 1), 1 + PATCHES + p:1 + PATCHES + p + m, :]
                                 .rearrange("b s d -> (b s) d"), rows[r0:r0 + m, j, :]).then_inc(seq_stored[2], 16)
            sp.wait_ge(seq_stored[0], 16 * (PT_SEQS * (PT_FULL // 2) + PT_TAIL // PATCHES))
            sp.wait_ge(seq_stored[1], 16 * (PT_SEQS * (PT_FULL // 2) + 1))
            sp.wait_ge(seq_stored[2], 16 * PIECES * GROUPS)
            sp.wait_ge(bias_seq, 6)
            for dst, src in ((ffn_s, ffn_gb), (bv_s, bv)):
                sp.dma_start(dst, src.partition_broadcast(SEQ)).then_inc(ld_late, 16)
            for g in range(GROUPS):
                if g >= 2:
                    sp.wait_ge(ld_h[g % 2], 16 * (g // 2))
                sp.dma_start(h_all[:, g * GB:(g + 1) * GB, :],
                             seq_b[g * GB:(g + 1) * GB].rearrange("b s d -> s b d")).then_inc(ld_h[g % 2], 16)
            for dst, src in ((wg_s, w_gate), (wu_s, w_up), (wd_s, w_down)):
                sp.dma_start(dst, src).then_inc(ld_ffn, 16)

            sp.wait_ge(pad_sent, 16 * EXPERTS)
            sp.wait_ge(spare_sent, 16)
            for k in range(2):
                sp.wait_ge(x_sent[k], 16 * 2 * GB * (GROUPS // 2))
            sp.wait_ge(tbl_ready, 2)

            def load_block(j, k):
                row = sp.value_load(row_i[0:1, bass.ds(j, 1)], min_val=0, max_val=XROWS - P)
                sp.dma_start(x_g[k], xrows[bass.ds(row, P), :]).then_inc(x_in[k], 16)

            load_block(0, 0)
            load_block(1, 1)
            with sp.Fori(1, BLOCKS // 2) as pair:
                for k in range(2):
                    j = pair * 2 + k
                    sp.wait_ge(f_tr, j - 1)
                    sp.wait_ge(f_dest, j - 1)
                    load_block(j, k)

            for k in range(2):
                sp.wait_ge(y_sent[k], 16 * (BLOCKS // 2))
            for g in range(GROUPS):
                k = g % 2
                if g >= 2:
                    sp.wait_ge(yf, 10 * (g - 2) + 1)
                sp.dma_start(y12[k], yrows[g * GS * 2:(g + 1) * GS * 2].rearrange("(b s r) d -> s b (r d)", s=SEQ, r=2))\
                    .then_inc(y_in[k], 16)
                if g >= 1:
                    store_out(sp, g - 1)
            store_out(sp, GROUPS - 1)
            for k in range(2):
                sp.wait_ge(out_sent[k], 16 * (GROUPS // 2))

        @block.scalar
        def _(act):
            act.dma_start(tokens_s[:, :], tokens).then_inc(ld_toks, 16)
            act.dma_start(tokb, tok_b.partition_broadcast(PT)).then_inc(ld_pos, 16)
            for q in range(PT_SEQS):
                act.dma_start(posb[q * PATCHES:(q + 1) * PATCHES, :], pos_enc[1:1 + PATCHES, :]).then_inc(ld_pos, 16)
            act.dma_start(cls_s, cls.partition_broadcast(BATCH)).then_inc(ld_pos, 16)
            act.dma_start(pos0, pos_enc[0].partition_broadcast(BATCH)).then_inc(ld_pos, 16)
            for j, r0, m, b, p in pieces:
                act.dma_start(pos_s[r0:r0 + m, j, :], pos_emb[p:p + m, :]).then_inc(ld_pos, 16)
            act.dma_start(wqk_s[:, :, :], wqk).then_inc(ld_attn, 16)
            act.dma_start(wv_s[:, :, :], wv).then_inc(ld_attn, 16)
            act.dma_start(tab_s[:, :], rel_bias.partition_broadcast(SEQ)).then_inc(ld_attn, 16)
            act.wait_ge(ld_cst, 32)

            def xt_copy(t, g, layer, d):
                act.wait_ge(pe_t, t * 2 + (d + 1))
                dst = xt[:, d, bass.ds(g * GT, GT)]
                if layer < 0:
                    act.activation(dst, bank[7][:, 0:GT], ACT.Copy).then_inc(act_xt, 1)
                else:
                    at_ = W_LN + (layer * DC + d) * 2
                    act.activation(dst, bank[7][:, 0:GT], ACT.Identity, bias=SML(at_ + 1), scale=SML(at_))\
                        .then_inc(act_xt, 1)

            with act.Fori(0, GROUPS) as g:
                for d in range(DC):
                    xt_copy(g, g, -1, d)

            def text_step(layer, g):
                s = layer * GROUPS + g
                lb, gb = back(layer, g, 1)
                lt, gt = back(layer, g, 2)
                sb_, st_ = lb * GROUPS + gb, (lt + 1) * GROUPS + gt
                if layer < LAYERS:
                    for c in range(FC):
                        act.wait_ge(pe_x, s * 4 + (c + 1))
                        wait(act, dve_conv, s * 12)
                        wait(act, act_u, s * 4)
                        act.activation(xin[:, c, :, 3:PADT], bank[c][:, 0:GT].rearrange("p (b t) -> p b t", b=GB), ACT.Copy)
                        act.activation(acc[:, c, :], bank[c][:, 0:GT], ACT.Identity,
                                       bias=SML(W_CB + layer * FC + c), scale=conv_w(layer, c, 3)).then_inc(act_x, 1)
                if 0 <= lt < LAYERS - 1:
                    xt_copy(st_, gt, lt, 0)
                if 0 <= lb < LAYERS:
                    act.wait_ge(pe_b, sb_ + 1)
                    wait(act, dve_scan, sb_)
                    act.activation(bu, bank[4][0:STATE, 0:GT], ACT.Copy, scale=0.05).then_inc(act_b, 1)
                if 0 <= lt < LAYERS - 1:
                    xt_copy(st_, gt, lt, 1)
                if 0 <= lb < LAYERS:
                    for c in range(FC):
                        act.wait_ge(pe_g, sb_ * 4 + (c + 1))
                        wait(act, dve_y, sb_ * 4)
                        act.activation(sg[:, c, :], bank[(0, 1, 1, 2)[c]][:, 0:GT], ACT.Silu).then_inc(act_g, 1)
                if layer < LAYERS:
                    for c in range(FC):
                        act.wait_ge(dve_conv, s * 12 + (9 + c))
                        wait(act, dve_y, s * 4)
                        act.activation(u[:, c, :], acc[:, c, :], ACT.Silu).then_inc(act_u, 1)

            text_steps(act, text_step)

            act.wait_ge(pool_x, (LAYERS + 1) * GROUPS)
            act.wait_ge(ld_attn, 48)

            def project(g, k):
                for d in range(DC):
                    act.wait_ge(a_tr, g * 2 + (d + 1))
                    wait(act, a_vm, (g) * 2)
                    act.activation(a_nt[:, d, :], bank[d][:, 0:GS], ACT.Copy).then_inc(a_trc, 1)
                act.wait_ge(a_qkm, g + 1)
                wait(act, a_qkd, g)
                act.activation(a_qk, bank[2][:, 0:GS], ACT.Silu, bias=SML(W_QK)).then_inc(a_qks, 1)
                act.wait_ge(a_va, g * 2 + 2)
                wait(act, a_om, g * 2 - 2)
                act.activation(a_v[k], a_vb, ACT.Silu).then_inc(a_vs, 1)

            def score(g):
                act.wait_ge(a_sa, g + 1)
                wait(act, a_om, g * 2)
                act.activation(a_w, a_arg, ACT.Gelu).then_inc(a_er, 1)
                for d in range(DC):
                    act.wait_ge(m_tr, g * 2 + (d + 1))
                    wait(act, m_lm, g)
                    act.activation(m_t[:, d, :], bank[6][:, 0:GS], ACT.Copy).then_inc(m_trc, 1)
                act.wait_ge(m_gap, g + 1)
                act.activation(gap_tanh, gap, ACT.Tanh, scale=0.5).then_inc(m_wt, 1)

            def attn_step(g, k):
                project(g, k)
                score(g - 1)

            project(0, 0)
            pairs_after_first(act, GROUPS, attn_step)
            score(GROUPS - 1)

            def turn(j, k):
                act.wait_ge(f_tr, j + 1)
                wait(act, f_um, j - 1)
                act.activation(x_gt[k], bank[2][:, 0:DC * P].rearrange("p (c t) -> p c t", c=DC), ACT.Copy)\
                    .then_inc(f_trc, 1)

            def gate(j):
                act.wait_ge(f_gm, j + 1)
                wait(act, f_hh, j)
                act.activation(f_sg, bank[0][:, :], ACT.Silu).then_inc(f_silu, 1)

            def back_half(j, k):
                act.wait_ge(f_dm, j + 1)
                wait(act, y_sent[k], (j - k) * 8)
                act.wait_ge(f_dest, j + 1)
                act.activation(f_y[k], bank[4 + k][:, 0:D], ACT.Copy, scale=row_wt[:, k:k + 1]).then_inc(f_yc, 1)

            def expert_step(j, k):
                gate(j)
                turn(j + 1, 1 - k)
                back_half(j - 1, 1 - k)

            act.wait_ge(tbl_ready, 2)
            turn(0, 0)
            gate(0)
            turn(1, 1)
            expert_step(1, 1)
            expert_step(2, 0)
            with act.Fori(1, BLOCKS // 2 - 1) as pair:
                expert_step(pair * 2 + 1, 1)
                expert_step(pair * 2 + 2, 0)
            gate(BLOCKS - 1)
            back_half(BLOCKS - 2, 0)
            back_half(BLOCKS - 1, 1)

        @block.gpsimd
        def _(pool):
            pool.memset(xin, 0.0).then_inc(zeroed, 1)
            pool.memset(decay, 0.95).then_inc(zeroed, 1)
            for t in (z, n, mv, emb[0], emb[1], minus_half[:, :]):
                pool.memset(t, 1.0).then_inc(zeroed, 1)
            pool.wait_ge(zeroed, 8)
            pool.memset(decay.rearrange("p (b t) -> p b t", b=GB)[:, :, 0:1], 0.0).then_inc(zeroed, 1)
            pool.memset(minus_half[:, :], -0.5).then_inc(zeroed, 1)
            pool.memset(base_m[:, :], 0.0).then_inc(zeroed, 1)
            pool.wait_ge(ld_toks, 16)
            pool.wait_ge(zeroed, 11)

            def gather(g, k, turn_):
                wait(pool, dve_n, (g - 1) * NT)
                settled(pool, pool_passed)
                pool.tensor_copy(tok_now[:, k, :], tokens_s[:, bass.ds(g * NT, NT)]).then_inc(tok_copied, 1)
                pool.wait_ge(tok_copied, g + 1)
                for j in range(NT):
                    m = TILE_ROWS[j]
                    settled(pool, pool_passed)
                    pool.indirect_dma_start(emb[k][0:m, j, :], None, tok_emb,
                                            bass.IndirectOffsetOnAxis(ap=tok_now[0:m, k, j:j + 1], axis=0))\
                        .then_inc(emb_ready[k], 16)

            def keep_embedding(g):
                pool.wait_ge(dve_n, g * NT + NT)
                settled(pool, pool_passed)
                pool.tensor_copy(group_rows(xtok, g), n).then_inc(pool_x, 1)

            gather(0, 0, 0)
            gather(1, 1, 0)
            with pool.Fori(1, GROUPS // 2) as pair:
                for k in range(2):
                    keep_embedding(pair * 2 + (k - 2))
                    pool.wait_ge(emb_ready[k], pair * (NT * 16))
                    gather(pair * 2 + k, k, pair)
            keep_embedding(GROUPS - 2)
            keep_embedding(GROUPS - 1)
            pool.wait_ge(ld_text, 80)

            def text_step(layer, g):
                lt, gt = back(layer, g, 2)
                if not 0 <= lt < LAYERS:
                    return
                s = lt * GROUPS + gt
                pool.wait_ge(dve_stats, s + 1)
                settled(pool, pool_passed)
                pool.tensor_scalar(rstd[:, 1, :], mv[:, :, 1], EPS, None, ALU.add).then_inc(pool_var, 1)
                pool.wait_ge(pool_var, s + 1)
                pool.tensor_tensor(rstd[:, 0, :], rstd[:, 1, :], minus_half[0:TR, 0:NT], ALU.pow).then_inc(pool_rstd, 1)
                pool.wait_ge(dve_n, (s + GROUPS) * NT + NT)
                gain = gb_s[:, lt, 0:1, :].broadcast_to([TR, NT, D])
                bias = gb_s[:, lt, 1:2, :].broadcast_to([TR, NT, D])
                pool.tensor_tensor(ng, n, gain, ALU.mult).then_inc(pool_ng, 1)
                pool.wait_ge(pool_ng, s + 1)
                pool.tensor_tensor(group_rows(xtok, gt), ng, bias, ALU.add).then_inc(pool_x, 1)

            text_steps(pool, text_step)

            def rsqrt(mv_, rs, stats_sem, count, chain, rstd_sem):
                pool.wait_ge(stats_sem, count)
                settled(pool, pool_passed)
                v = chain.inc(pool.tensor_scalar(rs[:, 1, :], mv_[:, :, 1], EPS, None, ALU.add))
                chain.wait(v)
                pool.tensor_tensor(rs[:, 0, :], rs[:, 1, :], minus_half[0:SEQ, 0:GB], ALU.pow).then_inc(rstd_sem, 1)

            def project(g):
                rsqrt(a_mv, a_rs, a_stats, g + 1, Chain(pool, a_var, 1, g), a_rstd)

            def route(g, k):
                rsqrt(m_mv, m_rs, m_stats, g + 1, Chain(pool, m_var, 1, g), m_rstd)
                pool.wait_ge(m_norm, g + 1)
                settled(pool, pool_passed)
                pool.tensor_copy(a_x[1][:, :, 0:D], a_x[0][:, :, 0:D]).then_inc(m_row2, 1)
                pool.wait_ge(m_row2, g + 1)
                pool.wait_ge(m_slot, g + 1)
                for r in range(2):
                    for b in range(GB):
                        settled(pool, pool_passed)
                        pool.indirect_dma_start(xrows, bass.IndirectOffsetOnAxis(ap=slot_i[:, r, b:b + 1], axis=0),
                                                a_x[r][:, b, :], None).then_inc(x_sent[k], 16)

            def causal(g):
                pool.wait_ge(a_er, g + 1)
                w = a_w.rearrange("p (k i) -> p k i", k=GB)
                settled(pool, pool_passed)
                pool.affine_select(out=w, in_=w, compare_op=ALU.is_ge, fill=0.0, base=0, pattern=[[0, GB], [1, SEQ]],
                                   channel_multiplier=-1).then_inc(a_sel, 1)

            def attn_step(g, k):
                project(g)
                causal(g - 1)
                route(g - 1, 1 - k)

            pool.wait_ge(pool_x, (LAYERS + 1) * GROUPS)
            pool.memset(padbuf, 0.0).then_inc(pad_zero, 1)
            project(0)
            pairs_after_first(pool, GROUPS, attn_step)
            causal(GROUPS - 1)
            route(GROUPS - 1, 1)

            pool.wait_ge(pad_ready, 2)
            for e in range(EXPERTS):
                pool.indirect_dma_start(xrows, bass.IndirectOffsetOnAxis(ap=padrow_i[:, e:e + 1], axis=0),
                                        padbuf[:, e, :], None).then_inc(pad_sent, 16)
            pool.dma_start(xrows[EXPERTS * REGION:XROWS, :].rearrange("(k p) d -> p k d", p=P),
                           padbuf[:, EXPERTS:EXPERTS + SPARE, :]).then_inc(spare_sent, 16)

            def send(j, k):
                pool.wait_ge(f_yc, j + 1)
                pool.wait_ge(f_dest, j + 1)
                settled(pool, pool_passed)
                pool.indirect_dma_start(yrows, bass.IndirectOffsetOnAxis(ap=dest_i[:, k:k + 1], axis=0), f_y[k], None)\
                    .then_inc(y_sent[k], 16)

            assert BLOCKS // 2 == BATCH
            pool.wait_ge(ld_late, 32)
            with pool.Fori(0, BATCH) as pair:
                for k in range(2):
                    send(pair * 2 + k, k)
                one_h = h_all[:, bass.ds(pair, 1), :]
                pool.tensor_tensor(one_h, one_h, ffn_s[:, 1:2, :], ALU.add).then_inc(h2b, 1)

            for g in range(GROUPS):
                pool.wait_ge(y_stats, g + 1)
                pool.tensor_scalar(y_rs[:, 1, :], y_mv[:, :, 1], EPS, None, ALU.add).then_inc(y_var, 1)
                pool.wait_ge(y_var, g + 1)
                pool.tensor_tensor(y_rs[:, 0, :], y_rs[:, 1, :], minus_half[0:SEQ, 0:GB], ALU.pow).then_inc(y_rstd, 1)

        @block.tensor
        def _(pe):
            def patch_tile(i, k, m, turn_):
                pe.wait_ge(ld_pat[k], turn_ * 16 + 16)
                wait(pe, pat_ready, i - 1)
                for c in range(IN_CH // P):
                    mm = pe.matmul(bank[k][0:m, 0:D], pat[k][:, c, 0:m], tokw_s[:, c, :], start=(c == 0),
                                   stop=(c == IN_CH // P - 1))
                mm.then_inc(pat_mm, 1)

            pe.wait_ge(ld_tokw, 16)
            patch_tile(0, 0, PT, 0)
            patch_tile(1, 1, PT, 0)
            with pe.Fori(1, PT_FULL // 2) as pair:
                for k in range(2):
                    patch_tile(pair * 2 + k, k, PT, pair)
            patch_tile(PT_FULL, 0, PT_TAIL, PT_FULL // 2)

            pe.wait_ge(ld_cst, 32)

            def turn(t, d):
                pe.wait_ge(dve_n, t * NT + NT)
                wait(pe, act_xt, t * 2 + d)
                for j in range(NT):
                    m = TILE_ROWS[j]
                    mm = pe.transpose(bank[7][:, TILE_AT[j]:TILE_AT[j] + m], n[0:m, j, d * P:(d + 1) * P],
                                      ident[0:m, 0:m])
                mm.then_inc(pe_t, 1)

            for d in range(DC):
                turn(0, d)
            with pe.Fori(1, GROUPS) as g:
                for d in range(DC):
                    turn(g, d)
            pe.wait_ge(ld_text, 80)

            def text_step(layer, g):
                s = layer * GROUPS + g
                lb, gb = back(layer, g, 1)
                lt, gt = back(layer, g, 2)
                sb_, st_ = lb * GROUPS + gb, (lt + 1) * GROUPS + gt
                late = 0 <= lb < LAYERS

                def in_product(l, group, c, out_):
                    for d in range(DC):
                        mm = pe.matmul(out_, win_s[:, l, d, c * P:(c + 1) * P], xt[:, d, bass.ds(group * GT, GT)],
                                       start=(d == 0), stop=(d == DC - 1))
                    return mm

                def gate_product(c, b):
                    in_product(lb, gb, FC + c, bank[b][:, 0:GT]).then_inc(pe_g, 1)

                if layer < LAYERS:
                    pe.wait_ge(act_xt, s * 2 + 2)
                    for c, (q, v) in enumerate(((dve_c, (s - 1) * 4), (act_g, (s - 2) * 4 + 3), (act_g, (s - 1) * 4),
                                                (dve_c, (s - 2) * 4 + 2))):
                        wait(pe, q, v)
                        if isinstance(s, int) and s == 1:
                            pe.wait_ge(act_x, c + 1)
                        in_product(layer, g, c, bank[c][:, 0:GT]).then_inc(pe_x, 1)
                if 0 <= lt < LAYERS - 1:
                    turn(st_, 0)
                if late:
                    for c in range(FC):
                        pe.wait_ge(act_u, sb_ * 4 + (c + 1))
                        wait(pe, dve_c, (sb_ - 1) * 4 + 3)
                        mm = pe.matmul(bank[4][0:STATE, 0:GT], wb_s[:, lb, c, :], u[:, c, :], start=(c == 0),
                                       stop=(c == FC - 1))
                    mm.then_inc(pe_b, 1)
                if 0 <= lt < LAYERS - 1:
                    turn(st_, 1)
                if late:
                    if layer < LAYERS:
                        pe.wait_ge(act_x, s * 4 + 2)
                    gate_product(0, 0)
                    gate_product(1, 1)
                    if layer < LAYERS:
                        pe.wait_ge(act_x, s * 4 + 4)
                    pe.wait_ge(dve_scan, sb_ + 1)
                    for c, b in enumerate((2, 3, 4, 0)):
                        if c == 2:
                            pe.wait_ge(act_b, sb_ + 1)
                        if c == 3:
                            pe.wait_ge(act_g, sb_ * 4 + 1)
                        pe.matmul(bank[b][:, 0:GT], wc_s[:, lb, c * P:(c + 1) * P], hs, start=True, stop=True)\
                            .then_inc(pe_c, 1)
                    pe.wait_ge(act_g, sb_ * 4 + 2)
                    gate_product(2, 1)
                    pe.wait_ge(dve_c, sb_ * 4 + 1)
                    gate_product(3, 2)
                    for j in range(NT):
                        m = TILE_ROWS[j]
                        wait(pe, dve_z, (sb_ * 3, (sb_ - 1) * 3 + 2, sb_ * 3 + 1)[j])
                        for c in range(FC):
                            if j == 0:
                                pe.wait_ge(dve_y, sb_ * 4 + (c + 1))
                            mm = pe.matmul(bank[5 + j % 2][0:m, 0:D], yt[:, c, TILE_AT[j]:TILE_AT[j] + m],
                                           wo_s[:, lb, c, :], start=(c == 0), stop=(c == FC - 1))
                        mm.then_inc(pe_o, 1)

            text_steps(pe, text_step)

            pe.wait_ge(pool_x, (LAYERS + 1) * GROUPS)
            pe.wait_ge(ld_attn, 48)

            def project(g, k):
                pe.wait_ge(a_norm, g + 1)
                for d in range(DC):
                    wait(pe, a_trc, g * 2 + (d - 1))
                    for b in range(GB):
                        mm = pe.transpose(bank[d][:, b * SEQ:(b + 1) * SEQ], a_n[:, b, d * P:(d + 1) * P],
                                          ident[0:SEQ, 0:SEQ])
                    mm.then_inc(a_tr, 1)
                pe.wait_ge(a_trc, g * 2 + 2)
                wait(pe, a_qks, g)
                for d in range(DC):
                    mm = pe.matmul(bank[2][:, 0:GS], wqk_s[:, d, :], a_nt[:, d, :], start=(d == 0), stop=(d == DC - 1))
                mm.then_inc(a_qkm, 1)

            def values(g):
                for half in range(2):
                    wait(pe, a_va, g * 2 + half)
                    for b in range(2 * half, 2 * half + 2):
                        for d in range(DC):
                            mm = pe.matmul(bank[3][0:SEQ, (b % 2) * D:(b % 2 + 1) * D], a_nt[:, d, b * SEQ:(b + 1) * SEQ],
                                           wv_s[:, d, :], start=(d == 0), stop=(d == DC - 1))
                    mm.then_inc(a_vm, 1)

            def similar(g, k):
                pe.wait_ge(a_qkd, g + 1)
                wait(pe, a_sa, g)
                for b in range(GB):
                    cut = slice(b * SEQ, (b + 1) * SEQ)
                    mm = pe.matmul(bank[4][0:SEQ, cut], a_k[k][:, cut], a_q[k][:, cut], start=True, stop=True)
                mm.then_inc(a_sm, 1)

            def score(g, k):
                pe.wait_ge(a_at, g + 1)
                pe.wait_ge(a_vs, g + 1)
                for half in range(2):
                    wait(pe, a_h2, g * 2 + half)
                    for b in range(2 * half, 2 * half + 2):
                        mm = pe.matmul(bank[5][0:SEQ, (b % 2) * D:(b % 2 + 1) * D], a_w[:, b * SEQ:(b + 1) * SEQ],
                                       a_v[k][:, b, :], start=True, stop=True)
                    mm.then_inc(a_om, 1)
                pe.wait_ge(m_norm, g + 1)
                for d in range(DC):
                    wait(pe, m_trc, g * 2 + d)
                    for b in range(GB):
                        mm = pe.transpose(bank[6][:, b * SEQ:(b + 1) * SEQ], a_x[0][:, b, d * P:(d + 1) * P],
                                          ident[0:SEQ, 0:SEQ])
                    mm.then_inc(m_tr, 1)
                pe.wait_ge(m_trc, g * 2 + 2)
                wait(pe, m_slot, g)
                for b in range(GB):
                    for d in range(DC):
                        at_ = W_R + d * EXPERTS
                        mm = pe.matmul(bank[7][0:SEQ, b * 8:(b + 1) * 8], m_t[:, d, b * SEQ:(b + 1) * SEQ],
                                       sml[:, at_:at_ + EXPERTS], start=(d == 0), stop=(d == DC - 1))
                mm.then_inc(m_lm, 1)
                pe.wait_ge(m_both, g + 1)
                pe.matmul(bank[7][0:SEQ, 0:GB * 8], tri, both.rearrange("p k e -> p (k e)"), start=True, stop=False)
                pe.matmul(bank[7][0:SEQ, 0:GB * 8], ones, before.rearrange("p k e -> p (k e)"), start=False, stop=True)\
                    .then_inc(m_rk, 1)

            def attn_step(g, k):
                project(g, k)
                similar(g - 1, 1 - k)
                values(g)
                score(g - 1, 1 - k)

            project(0, 0)
            values(0)
            pairs_after_first(pe, GROUPS, attn_step)
            similar(GROUPS - 1, 1)
            score(GROUPS - 1, 1)
            pe.wait_ge(m_slot, GROUPS)
            pe.matmul(bank[7][:, 0:EXPERTS], cst[0:SEQ, C_ONE:C_ONE + P], base_m[:, :], start=True, stop=True)\
                .then_inc(cnt_mm, 1)

            pe.wait_ge(tbl_ready, 2)
            pe.wait_ge(ld_ffn, 48)

            def turn_block(j, k, turn_):
                pe.wait_ge(x_in[k], turn_ * 16 + 16)
                wait(pe, f_trc, j)
                for d in range(DC):
                    mm = pe.transpose(bank[2][:, d * P:(d + 1) * P], x_g[k][:, d * P:(d + 1) * P], ident)
                mm.then_inc(f_tr, 1)

            def gate_up(j, k):
                e = pe.value_load(expert_i[0:1, bass.ds(j, 1)], min_val=0, max_val=EXPERTS - 1)
                pe.wait_ge(f_trc, j + 1)
                for q, w, sig, free in ((0, wg_s, f_gm, f_silu), (1, wu_s, f_um, f_hh)):
                    wait(pe, free, j)
                    for d in range(DC):
                        mm = pe.matmul(bank[q][:, :], x_gt[k][:, d, :], w[:, d, bass.ds(e * FFN, FFN)], start=(d == 0),
                                       stop=(d == DC - 1))
                    mm.then_inc(sig, 1)

            def turn_hidden(j, k):
                pe.wait_ge(f_hh, j + 1)
                wait(pe, f_htc, j)
                for c in range(FC):
                    mm = pe.transpose(bank[3][:, c * P:(c + 1) * P], f_h[:, c * P:(c + 1) * P], ident)
                mm.then_inc(f_hm, 1)

            def down(j, k):
                e = pe.value_load(expert_i[0:1, bass.ds(j, 1)], min_val=0, max_val=EXPERTS - 1)
                pe.wait_ge(f_htc, j + 1)
                wait(pe, f_yc, j - 1)
                for c in range(FC):
                    mm = pe.matmul(bank[4 + k][:, 0:D], f_ht[k][:, c, :], wd_s[:, c, bass.ds(e * D, D)], start=(c == 0),
                                   stop=(c == FC - 1))
                mm.then_inc(f_dm, 1)

            def expert_step(j, k, turn_):
                gate_up(j, k)
                turn_block(j + 1, 1 - k, turn_)
                down(j - 1, 1 - k)
                turn_hidden(j, k)

            turn_block(0, 0, 0)
            gate_up(0, 0)
            turn_block(1, 1, 0)
            turn_hidden(0, 0)
            expert_step(1, 1, 1)
            expert_step(2, 0, 1)
            with pe.Fori(1, BLOCKS // 2 - 1) as pair:
                expert_step(pair * 2 + 1, 1, pair + 1)
                expert_step(pair * 2 + 2, 0, pair + 1)
            gate_up(BLOCKS - 1, 1)
            down(BLOCKS - 2, 0)
            turn_hidden(BLOCKS - 1, 1)
            down(BLOCKS - 1, 1)

        @block.vector
        def _(dve):
            dve.wait_ge(ld_pos, 16 * (3 + PT_SEQS + PIECES))
            dve.tensor_tensor(posb, posb, tokb, ALU.add).then_inc(posb_ready, 1)
            dve.tensor_tensor(cls_s, cls_s, pos0, ALU.add).then_inc(cls_ready, 1)
            dve.wait_ge(posb_ready, 1)

            def patch_tile(i, k, m, turn_):
                dve.wait_ge(pat_mm, i + 1)
                wait(dve, seq_stored[k], turn_ * (16 * PT_SEQS))
                dve.tensor_tensor(pat_out[k][0:m, :], bank[k][0:m, 0:D], posb[0:m, :], ALU.add).then_inc(pat_ready, 1)

            patch_tile(0, 0, PT, 0)
            patch_tile(1, 1, PT, 0)
            with dve.Fori(1, PT_FULL // 2) as pair:
                for k in range(2):
                    patch_tile(pair * 2 + k, k, PT, pair)
            patch_tile(PT_FULL, 0, PT_TAIL, PT_FULL // 2)

            dve.wait_ge(zeroed, 11)

            def embed(g, k, turn_):
                dve.wait_ge(emb_ready[k], turn_ * (16 * NT) + 16 * NT)
                wait(dve, pe_t, g * 2)
                wait(dve, pool_x, g)
                dve.tensor_tensor(n[:, 0:2, :], emb[k][:, 0:2, :], pos_s[:, 0:2, :], ALU.add).then_inc(dve_n, 2)
                dve.tensor_tensor(n[0:TILE_ROWS[2], 2, :], emb[k][0:TILE_ROWS[2], 2, :], pos_s[0:TILE_ROWS[2], 2, :],
                                  ALU.add).then_inc(dve_n, 1)

            embed(0, 0, 0)
            embed(1, 1, 0)
            with dve.Fori(1, GROUPS // 2) as pair:
                for k in range(2):
                    embed(pair * 2 + k, k, pair)
            dve.wait_ge(ld_cst, 32)
            dve.wait_ge(ld_attn, 48)

            HALF = SEQ // 2
            ohv = oh.rearrange("p (i b) -> p i b", b=32)
            c = Chain(dve, bias_seq, 6, 0)
            bucket = cst[0:SEQ, C_BUCKET:C_BUCKET + SEQ]
            numbers = cst[0:SEQ, C_B32:C_B32 + 32].unsqueeze(1).broadcast_to([SEQ, HALF, 32])
            for half in range(2):
                cut = slice(half * HALF, (half + 1) * HALF)
                if half:
                    c.wait(3)
                v = c.inc(dve.tensor_tensor(ohv, bucket[:, cut].unsqueeze(2).broadcast_to([SEQ, HALF, 32]), numbers,
                                            ALU.is_equal))
                c.wait(v)
                v = c.inc(dve.tensor_tensor(ohv, ohv, tab_s[:, :].unsqueeze(1).broadcast_to([SEQ, HALF, 32]), ALU.mult))
                c.wait(v)
                v = c.inc(dve.tensor_reduce(bias_t[:, cut], ohv, AX, ALU.add))
            c.wait(v)
            dve.tensor_scalar(bias_t[:, :], bias_t[:, :], QK ** 0.5 / LAP_STD, -LAP_MU / LAP_STD, ALU.mult, ALU.add)\
                .then_inc(bias_seq, 1)

            def text_step(layer, g):
                s = layer * GROUPS + g
                lb, gb = back(layer, g, 1)
                lt, gt = back(layer, g, 2)
                sb_, st_ = lb * GROUPS + gb, lt * GROUPS + gt
                late = 0 <= lb < LAYERS
                if 0 <= lt < LAYERS:
                    rows = group_rows(xtok, gt)
                    dve.wait_ge(pool_x, st_ + 1)
                    for j in range(NT):
                        m = TILE_ROWS[j]
                        dve.wait_ge(pe_o, st_ * 3 + (j + 1))
                        dve.tensor_tensor(z[0:m, j, :], bank[5 + j % 2][0:m, 0:D], rows[0:m, j, :], ALU.add)\
                            .then_inc(dve_z, 1)
                    for j in range(NT):
                        m = TILE_ROWS[j]
                        dve.wait_ge(dve_z, st_ * 3 + (j + 1))
                        settled(dve, dve_passed)
                        dve.bn_stats(stats[0:m, j, :], z[0:m, j, :]).then_inc(dve_bn, 1)
                    for j in range(NT):
                        m = TILE_ROWS[j]
                        dve.wait_ge(dve_bn, st_ * 3 + (j + 1))
                        settled(dve, dve_passed)
                        i = dve.bn_aggr(mv[0:m, j, :], stats[0:m, j, :])
                    i.then_inc(dve_stats, 1)
                if layer < LAYERS:
                    taps(layer, s, (2, 1), 0)
                if 0 <= lt < LAYERS:
                    dve.wait_ge(pool_rstd, st_ + 1)
                    dve.wait_ge(dve_stats, st_ + 1)
                    idx = st_ + GROUPS
                    dve.wait_ge(pe_t, idx * 2 if lt < LAYERS - 1 else ALL_T)
                    dve.wait_ge(pool_x, idx)
                    for j in range(NT):
                        m = TILE_ROWS[j]
                        dve.tensor_scalar(n[0:m, j, :], z[0:m, j, :], mv[0:m, j, 0:1], rstd[0:m, 0, j:j + 1],
                                          ALU.subtract, ALU.mult).then_inc(dve_n, 1)
                if late:
                    dve.wait_ge(act_b, sb_ + 1)
                    wait(dve, pe_c, sb_ * 4)
                    dve.tensor_tensor_scan(hs, decay, bu, 0.0, ALU.mult, ALU.add).then_inc(dve_scan, 1)
                if layer < LAYERS:
                    taps(layer, s, (0,), 8)
                if late:
                    for c in range(FC):
                        dve.wait_ge(pe_c, sb_ * 4 + (c + 1))
                        dve.wait_ge(pe_b, sb_ + 1)
                        dve.scalar_tensor_tensor(u[:, c, :], u[:, c, :], SML(W_D + lb * FC + c),
                                                 bank[(2, 3, 4, 0)[c]][:, 0:GT], ALU.mult, ALU.add).then_inc(dve_c, 1)
                    for c in range(FC):
                        dve.wait_ge(dve_c, sb_ * 4 + (c + 1))
                        dve.wait_ge(act_g, sb_ * 4 + (c + 1))
                        wait(dve, pe_o, sb_ * 3)
                        dve.tensor_tensor(yt[:, c, :], u[:, c, :], sg[:, c, :], ALU.mult).then_inc(dve_y, 1)

            def taps(layer, s, which, first):
                v = first
                for tap in which:
                    for c in range(FC):
                        if v < 4:
                            dve.wait_ge(act_x, s * 4 + (c + 1))
                        else:
                            dve.wait_ge(dve_conv, s * 12 + (v - 3))
                        a = acc[:, c, :].rearrange("p (b t) -> p b t", b=GB)
                        dve.scalar_tensor_tensor(a, xin[:, c, :, tap:tap + TXT], conv_w(layer, c, tap), a,
                                                 ALU.mult, ALU.add).then_inc(dve_conv, 1)
                        v += 1

            text_steps(dve, text_step)

            dve.wait_ge(pool_x, (LAYERS + 1) * GROUPS)
            rows_of = lambda g: h_all[:, bass.ds(g * GB, GB), :]

            def norm_stats(src, st, mv_, chain, stats_sem):
                for b in range(GB):
                    settled(dve, dve_passed)
                    v = chain.inc(dve.bn_stats(st[:, b, :], src[:, b, :]))
                for b in range(GB):
                    chain.wait(v - GB + 1 + b)
                    settled(dve, dve_passed)
                    i = dve.bn_aggr(mv_[:, b, :], st[:, b, :])
                i.then_inc(stats_sem, 1)

            def project(g, k):
                chain = Chain(dve, at_dve, 4, g)
                dve.wait_ge(ld_h[k], g * 8 + (16 - 8 * k))
                h = rows_of(g)
                norm_stats(h, a_st, a_mv, chain, a_stats)
                dve.wait_ge(a_rstd, g + 1)
                dve.wait_ge(a_stats, g + 1)
                wait(dve, a_tr, g * 2)
                for b in range(GB):
                    i = dve.tensor_scalar(a_n[:, b, :], h[:, b, :], a_mv[:, b, 0:1], a_rs[:, 0, b:b + 1],
                                          ALU.subtract, ALU.mult)
                i.then_inc(a_norm, 1)

            def value_bias(g):
                for half in range(2):
                    dve.wait_ge(a_vm, g * 2 + (half + 1))
                    wait(dve, a_vs, g)
                    dve.tensor_tensor(a_vb[:, 2 * half:2 * half + 2, :],
                                      bank[3][0:SEQ, :].rearrange("p (k d) -> p k d", k=2),
                                      bv_s.unsqueeze(1).broadcast_to([SEQ, 2, D]), ALU.add).then_inc(a_va, 1)

            def query_key(g, k):
                dve.wait_ge(a_qks, g + 1)
                wait(dve, a_sm, g - 1)
                dve.tensor_scalar(a_q[k], a_qk, SML(W_QK + 1), SML(W_QK + 3), ALU.mult, ALU.add)
                dve.tensor_scalar(a_k[k], a_qk, SML(W_QK + 2), SML(W_QK + 4), ALU.mult, ALU.add).then_inc(a_qkd, 1)

            v3 = lambda t: t.rearrange("p (k i) -> p k i", k=GB)
            wide = lambda t: t.unsqueeze(1).broadcast_to([SEQ, GB, SEQ])

            def scale_scores(g):
                dve.wait_ge(a_sm, g + 1)
                wait(dve, a_er, g)
                wait(dve, a_at, g)
                dve.scalar_tensor_tensor(v3(a_arg), v3(bank[4][0:SEQ, 0:GS]), 1.0 / (SEQ * LAP_STD), wide(bias_t[:, :]),
                                         ALU.mult, ALU.add).then_inc(a_rec, 1)
                dve.wait_ge(a_rec, g * 2 + 1)
                dve.tensor_scalar(a_arg, a_arg, TINY, None, ALU.add).then_inc(a_sa, 1)
                dve.wait_ge(a_sa, g + 1)
                dve.reciprocal(a_rc, a_arg).then_inc(a_rec, 1)

            def score(g):
                h = rows_of(g)
                dve.wait_ge(a_sel, g + 1)
                dve.wait_ge(a_rec, g * 2 + 2)
                dve.tensor_tensor(a_w, a_w, a_rc, ALU.mult).then_inc(a_at, 1)
                for half in range(2):
                    dve.wait_ge(a_om, g * 2 + (half + 1))
                    two = h[:, 2 * half:2 * half + 2, :]
                    dve.tensor_tensor(two, bank[5][0:SEQ, :].rearrange("p (k d) -> p k d", k=2), two, ALU.add)\
                        .then_inc(a_h2, 1)

            def route(g, k):
                h = rows_of(g)
                chain = Chain(dve, m_seq, 26, g)
                dve.wait_ge(a_h2, g * 2 + 2)
                norm_stats(h, m_st, m_mv, chain, m_stats)
                dve.wait_ge(m_rstd, g + 1)
                dve.wait_ge(m_stats, g + 1)
                if isinstance(g, int):
                    if g >= 1:
                        dve.wait_ge(x_sent[1 - k], 16 * 2 * GB * ((g - 1) // 2 + 1))
                else:
                    dve.wait_ge(x_sent[1 - k], (g + k) * (16 * GB))
                for b in range(GB):
                    i = dve.tensor_scalar(a_x[0][:, b, 0:D], h[:, b, :], m_mv[:, b, 0:1], m_rs[:, 0, b:b + 1],
                                          ALU.subtract, ALU.mult)
                i.then_inc(m_norm, 1)
                dve.wait_ge(m_lm, g + 1)
                v = chain.inc(dve.tensor_copy(lg, bank[7][0:SEQ, 0:GB * 8].rearrange("p (k e) -> p k e", k=GB)))
                chain.wait(v)
                for b in range(GB):
                    settled(dve, dve_passed)
                    v = chain.inc(dve.max(top[:, b, :], lg[:, b, :]))
                for b in range(GB):
                    chain.wait(v - GB + 1 + b)
                    settled(dve, dve_passed)
                    vi = chain.inc(dve.max_index(idx_u[:, b, :], top[:, b, :], lg[:, b, :]))
                wait(dve, m_wt, g)
                dve.tensor_tensor(gap, top[:, :, 0], top[:, :, 1], ALU.subtract).then_inc(m_gap, 1)
                chain.wait(vi)
                v = chain.inc(dve.tensor_copy(idx_f, idx_u[:, :, :]))
                chain.wait(v)
                numbers = expert_no.unsqueeze(1).broadcast_to([SEQ, GB, 8])
                for r in range(2):
                    v = chain.inc(dve.tensor_tensor(one[r], idx_f[:, :, r:r + 1].broadcast_to([SEQ, GB, 8]), numbers,
                                                    ALU.is_equal))
                chain.wait(v)
                v = chain.inc(dve.tensor_tensor(both, one[0], one[1], ALU.add))
                v2 = chain.inc(dve.tensor_copy(before[:, 0, :], base_m[:, :]))
                for b in range(1, GB):
                    chain.wait(v2)
                    v2 = chain.inc(dve.tensor_tensor(before[:, b, :], before[:, b - 1, :], both[:, b - 1, :], ALU.add))
                chain.wait(v2)
                dve.tensor_tensor(base_m[:, :], before[:, GB - 1, :], both[:, GB - 1, :], ALU.add).then_inc(m_both, 1)
                dve.wait_ge(m_rk, g + 1)
                v = chain.inc(dve.tensor_tensor(place, bank[7][0:SEQ, 0:GB * 8].rearrange("p (k e) -> p k e", k=GB),
                                                cst[0:SEQ, C_BASE:C_BASE + 8].unsqueeze(1).broadcast_to([SEQ, GB, 8]),
                                                ALU.add))
                chain.wait(v)
                for r in range(2):
                    v = chain.inc(dve.tensor_tensor(picked[r], place, one[r], ALU.mult))
                for r in range(2):
                    chain.wait(v - 1 + r)
                    v3_ = chain.inc(dve.tensor_reduce(slot_f[:, r, :], picked[r], AX, ALU.add))
                chain.wait(v3_)
                dve.tensor_copy(slot_i[:, :, :], slot_f)
                toks = cst[0:SEQ, bass.ds(g * GB + C_TOK, GB)]
                for r in range(2):
                    dve.tensor_scalar(a_x[r][:, :, D], toks, float(r), None, ALU.add)
                dve.wait_ge(m_wt, g + 1)
                for r in range(2):
                    i = dve.tensor_scalar(a_x[r][:, :, D + 1], gap_tanh, 0.5 - r, 0.5, ALU.mult, ALU.add)
                i.then_inc(m_slot, 1)
                chain.done()

            def attn_step(g, k):
                project(g, k)
                scale_scores(g - 1)
                value_bias(g)
                score(g - 1)
                query_key(g, k)
                route(g - 1, 1 - k)

            dve.wait_ge(ld_late, 32)
            project(0, 0)
            value_bias(0)
            query_key(0, 0)
            pairs_after_first(dve, GROUPS, attn_step)
            scale_scores(GROUPS - 1)
            score(GROUPS - 1)
            route(GROUPS - 1, 1)

            c = Chain(dve, tb, 13, 0)
            dve.wait_ge(pad_zero, 1)
            dve.tensor_copy(padbuf[:, :, D], cst[:, C_PADDEST:C_PADDEST + EXPERTS + SPARE]).then_inc(pad_ready, 1)
            dve.wait_ge(cnt_mm, 1)
            v = c.inc(dve.tensor_copy(cnt, bank[7][:, 0:EXPERTS]))
            c.wait(v)
            v = c.inc(dve.tensor_tensor(padrow_f, cnt, cst[:, C_PADROW:C_PADROW + EXPERTS], ALU.add))
            v2 = c.inc(dve.tensor_tensor(steps_b, cnt.unsqueeze(2).broadcast_to([P, EXPERTS, COUNT_STEPS]),
                                         cst[:, C_STEPS:C_STEPS + COUNT_STEPS].unsqueeze(1)
                                         .broadcast_to([P, EXPERTS, COUNT_STEPS]), ALU.is_gt))
            c.wait(v)
            dve.tensor_copy(padrow_i[:, :], padrow_f).then_inc(pad_ready, 1)
            c.wait(v2)
            v = c.inc(dve.tensor_reduce(ntile, steps_b, AX, ALU.add))
            c.wait(v)
            v = c.inc(dve.tensor_tensor_scan(ends, cst[:, C_ONE:C_ONE + EXPERTS], ntile, 0.0, ALU.mult, ALU.add))
            v = c.inc(dve.tensor_scalar(delta, ntile, -float(P), float(REGION), ALU.mult, ALU.add))
            c.wait(v)
            v = c.inc(dve.tensor_scalar(delta[:, EXPERTS - 1:], ends[:, EXPERTS - 2:EXPERTS - 1], float(P),
                                        float(REGION - FULL_BLOCKS * P), ALU.mult, ALU.add))
            v2 = c.inc(dve.tensor_tensor(passed, cst[:, C_BLOCK:C_BLOCK + BLOCKS].unsqueeze(2)
                                         .broadcast_to([P, BLOCKS, EXPERTS]),
                                         ends.unsqueeze(1).broadcast_to([P, BLOCKS, EXPERTS]), ALU.is_ge))
            c.wait(v2)
            v = c.inc(dve.tensor_tensor(shifts, passed, delta.unsqueeze(1).broadcast_to([P, BLOCKS, EXPERTS]), ALU.mult))
            v2 = c.inc(dve.tensor_reduce(expert_f, passed, AX, ALU.add))
            c.wait(v)
            v = c.inc(dve.tensor_reduce(row_f, shifts, AX, ALU.add))
            c.wait(v)
            v = c.inc(dve.scalar_tensor_tensor(row_f, cst[:, C_BLOCK:C_BLOCK + BLOCKS], float(P), row_f, ALU.mult, ALU.add))
            v2 = c.inc(dve.tensor_scalar(expert_f, expert_f, float(EXPERTS - 1), None, ALU.min))
            c.wait(v2)
            dve.tensor_copy(row_i[:, :], row_f).then_inc(tbl_ready, 1)
            dve.tensor_copy(expert_i[:, :], expert_f).then_inc(tbl_ready, 1)
            c.done()
            dve.wait_ge(tbl_ready, 2)

            def hidden(j, k):
                dve.wait_ge(f_silu, j + 1)
                dve.wait_ge(f_um, j + 1)
                wait(dve, f_hm, j)
                dve.tensor_tensor(f_h, bank[1][:, :], f_sg, ALU.mult).then_inc(f_hh, 1)

            def destinations(j, k):
                dve.wait_ge(f_tr, j + 1)
                wait(dve, f_yc, j - 1)
                wait(dve, y_sent[k], (j - k) * 8)
                dve.tensor_copy(row_wt[:, k:k + 1], x_g[k][:, D + 1:D + 2])
                dve.tensor_copy(dest_i[:, k:k + 1], x_g[k][:, D:D + 1]).then_inc(f_dest, 1)

            def hidden_turned(j, k):
                dve.wait_ge(f_hm, j + 1)
                wait(dve, f_dm, j - 1)
                dve.tensor_copy(f_ht[k], bank[3][:, :].rearrange("p (c t) -> p c t", c=FC)).then_inc(f_htc, 1)

            for j in range(2):
                hidden(j, j)
                destinations(j, j)
                hidden_turned(j, j)
            with dve.Fori(1, BLOCKS // 2) as pair:
                for k in range(2):
                    hidden(pair * 2 + k, k)
                    destinations(pair * 2 + k, k)
                    hidden_turned(pair * 2 + k, k)

            for g in range(GROUPS):
                k = g % 2
                c = Chain(dve, yf, 10, g)
                dve.wait_ge(y_in[k], 16 * (g // 2 + 1))
                v = c.inc(dve.tensor_tensor(y_sum, y12[k][:, :, 0:D], y12[k][:, :, D:2 * D], ALU.add))
                c.wait(v)
                norm_stats(y_sum, y_st, y_mv, c, y_stats)
                dve.wait_ge(y_rstd, g + 1)
                dve.wait_ge(y_stats, g + 1)
                for b in range(GB):
                    v = c.inc(dve.tensor_scalar(y_n[:, b, :], y_sum[:, b, :], y_mv[:, b, 0:1], y_rs[:, 0, b:b + 1],
                                                ALU.subtract, ALU.mult))
                c.wait(v)
                v = c.inc(dve.tensor_tensor(y_g, y_n, ffn_s[0:SEQ, 0:1, :].broadcast_to([SEQ, GB, D]), ALU.mult))
                wait(dve, out_sent[k], 16 * (g // 2))
                dve.wait_ge(h2b, BATCH)
                c.wait(v)
                dve.tensor_tensor(y_out[k], y_g, h_all[:, g * GB:(g + 1) * GB, :], ALU.add).then_inc(y_done, 1)
                c.done()


def constants():
    import math

    import numpy as np
    c = np.zeros((P, CONSTS), np.float32)
    p = np.arange(P)[:, None]
    i = np.arange(P)[None, :]
    c[:, C_ID:C_ID + P] = p == i
    c[:, C_TRI:C_TRI + P] = p < i
    c[:, C_ONE:C_ONE + P] = 1
    dist = np.maximum(i - p, 0)
    large = 16 + (np.log(np.maximum(dist, 1).astype(np.float32) / 16) / math.log(128 / 16) * 16).astype(np.int32)
    c[:, C_BUCKET:C_BUCKET + P] = np.where(dist < 16, dist, np.minimum(large, 31))
    e = np.arange(EXPERTS)
    c[:, C_EXP:C_EXP + EXPERTS] = e
    c[:, C_BASE:C_BASE + EXPERTS] = e * REGION
    c[:, C_PADROW:C_PADROW + EXPERTS] = e * REGION + p
    k = np.arange(EXPERTS + SPARE)
    c[:, C_PADDEST:C_PADDEST + EXPERTS + SPARE] = 2 * TOKENS + k * P + p
    c[:, C_TOK:C_TOK + BATCH] = 2 * (np.arange(BATCH) * SEQ + p)
    c[:, C_STEPS:C_STEPS + COUNT_STEPS] = P * np.arange(COUNT_STEPS)
    c[:, C_BLOCK:C_BLOCK + BLOCKS] = np.arange(BLOCKS)
    c[:, C_B32:C_B32 + 32] = np.arange(32)
    return c


def kernel(**inputs):
    import concourse.bacc as bacc
    import numpy as np
    from concourse.bass_utils import run_bass_kernel_spmd

    a = {k: np.asarray(v) for k, v in inputs.items()}
    rows = lambda w, chunks: w.reshape(chunks, P, -1).transpose(1, 0, 2)

    x = a["x"].reshape(BATCH, 3, 6, 16, 6, 16).transpose(1, 3, 5, 0, 2, 4).reshape(IN_CH // P, P, BATCH * PATCHES)
    full = PT_FULL * PT
    patches = x[:, :, :full].reshape(IN_CH // P, P, PT_FULL, PT).transpose(2, 1, 0, 3)
    tail = x[:, :, full:].transpose(1, 0, 2)
    toks = a["x_txt"].reshape(GROUPS, GT)
    tokens = np.zeros((TR, GROUPS * NT), np.int32)
    for j, (t, m) in enumerate(zip(TILE_AT, TILE_ROWS)):
        tokens[:m, j::NT] = toks[:, t:t + m].T

    per_layer = lambda w, chunks: np.stack([rows(w[l].T, chunks) for l in range(LAYERS)], 1)
    small = np.zeros((P, SMALL), np.float32)
    small[:, W_CONV:W_CB] = a["L0_txt_conv_w"].reshape(LAYERS, FC, P, 4).transpose(2, 0, 1, 3).reshape(P, -1)
    small[:, W_CB:W_D] = a["L0_txt_conv_b"].reshape(LAYERS * FC, P).T
    small[:, W_D:W_LN] = a["L0_txt_D_vec"].reshape(LAYERS * FC, P).T
    small[:, W_LN:W_QK:2] = a["L0_txt_ln_g"].reshape(LAYERS * DC, P).T
    small[:, W_LN + 1:W_QK:2] = a["L0_txt_ln_b"].reshape(LAYERS * DC, P).T
    small[:, W_QK] = a["L0_attn_bqk"]
    small[:, W_QK + 1:W_QK + 3] = a["L0_attn_gamma"].T
    small[:, W_QK + 3:W_QK + 5] = a["L0_attn_beta"].T
    small[:, W_R:] = rows(a["L0_ffn_w_router"].T, DC).reshape(P, -1)

    experts = lambda w, chunks: w.transpose(2, 0, 1).reshape(chunks, P, -1).transpose(1, 0, 2)
    arrays = {
        "patches": patches, "patches_tail": tail, "tokens": tokens,
        "tok_w": rows(a["L0_tok_W"].T, IN_CH // P), "tok_b": a["L0_tok_b"], "cls": a["L0_tok_cls_token"].reshape(D),
        "pos_enc": a["L0_tok_pos_enc"].reshape(1 + PATCHES, D), "tok_emb": a["L0_txt_tok_emb"],
        "pos_emb": a["L0_txt_pos_emb"], "w_in": per_layer(a["L0_txt_W_in"], DC),
        "w_b": per_layer(a["L0_txt_W_B"], FC), "w_c": a["L0_txt_W_C"].transpose(2, 0, 1),
        "w_out": per_layer(a["L0_txt_W_out"], FC), "small": small,
        "ln_gb": np.stack([a["L0_txt_ln_g"], a["L0_txt_ln_b"]], 1),
        "wqk": rows(a["L0_attn_wqk"], DC), "wv": rows(a["L0_attn_wv"], DC), "bv": a["L0_attn_bv"],
        "rel_bias": a["L0_attn_rel_bias"],
        "w_gate": experts(a["L0_ffn_w_gate"], DC), "w_up": experts(a["L0_ffn_w_up"], DC),
        "w_down": experts(a["L0_ffn_w_down"], FC),
        "ffn_gb": np.stack([a["L0_ffn_ln_gamma"], a["L0_ffn_ln_beta"]]), "consts": constants(),
    }
    nc = bacc.Bacc("TRN2", target_bir_lowering=False, num_devices=1)
    arrays = {f"in_{k}": np.ascontiguousarray(v) for k, v in arrays.items()}
    aps = [nc.dram_tensor(k, v.shape, mybir.dt.from_np(v.dtype), kind="ExternalInput").ap() for k, v in arrays.items()]
    aps.append(nc.dram_tensor("out_0", (BATCH, SEQ, D), F32, kind="ExternalOutput").ap())
    build(nc, *aps)
    r = run_bass_kernel_spmd(nc, [arrays], core_ids=[0])
    return r.results[0]["out_0"]
```

```python
from contextlib import ExitStack

import concourse.bass as bass
from concourse import mybir

F32 = mybir.dt.float32
I32 = mybir.dt.int32
U32 = mybir.dt.uint32
ACT = mybir.ActivationFunctionType
ALU = mybir.AluOpType
AX = mybir.AxisListType.X

P = 128
BATCH, TXT, PATCHES = 32, 77, 36
SEQ = 1 + PATCHES + TXT
D = 256
DC = D // P
IN_CH = 768
INNER, STATE, LAYERS = 512, 64, 4
FC = INNER // P
GB = 4
GROUPS = BATCH // GB
GT = GB * TXT
TILE_ROWS = (104, 104, 100)
TILE_AT = (0, 104, 208)
TR = TILE_ROWS[0]
NT = len(TILE_ROWS)
PADT = TXT + 3
PT_SEQS = 3
PT = PT_SEQS * PATCHES
PT_FULL = BATCH // PT_SEQS
PT_TAIL = (BATCH - PT_FULL * PT_SEQS) * PATCHES
QK = 128
GS = GB * SEQ
EXPERTS, FFN = 8, 512
TOKENS = BATCH * SEQ
REGION = TOKENS + P + (-TOKENS) % P
FULL_BLOCKS = 2 * TOKENS // P
BLOCKS = FULL_BLOCKS + EXPERTS - 1
BLOCKS += BLOCKS % 2
SPARE = BLOCKS - FULL_BLOCKS
XROWS = EXPERTS * REGION + SPARE * P
YROWS = 2 * TOKENS + (EXPERTS + SPARE) * P
ROW = D + 2
COUNT_STEPS = -(-TOKENS // P)
EPS = 1e-5
LAP_MU = 0.5 ** 0.5
LAP_STD = (0.25 * 3.141592653589793) ** 0.5
TINY = 1e-30

C_ID = 0
C_TRI = C_ID + P
C_CAUSAL = C_TRI + P
C_ONE = C_CAUSAL + P
C_BUCKET = C_ONE + P
C_EXP = C_BUCKET + P
C_BASE = C_EXP + EXPERTS
C_PADROW = C_BASE + EXPERTS
C_PADDEST = C_PADROW + EXPERTS
C_TOK = C_PADDEST + EXPERTS + SPARE
C_STEPS = C_TOK + BATCH
C_BLOCK = C_STEPS + COUNT_STEPS
C_B32 = C_BLOCK + BLOCKS
CONSTS = C_B32 + 32

W_CONV = 0
W_CB = W_CONV + LAYERS * FC * 4
W_D = W_CB + LAYERS * FC
W_LN = W_D + LAYERS * FC
W_QK = W_LN + LAYERS * DC * 2
W_R = W_QK + 5
SMALL = W_R + DC * EXPERTS


class Chain:

    def __init__(self, eng, sem, per, iteration):
        self.eng, self.sem, self.base, self.n, self.per = eng, sem, iteration * per, 0, per

    def inc(self, instruction):
        instruction.then_inc(self.sem, 1)
        self.n += 1
        assert self.n <= self.per
        return self.n

    def wait(self, n):
        self.eng.wait_ge(self.sem, self.base + n)

    def done(self):
        assert self.n == self.per, self.n


def wait(eng, sem, value):
    if not (isinstance(value, int) and value <= 0):
        eng.wait_ge(sem, value)


def settled(eng, sem):
    eng.sem_inc(sem, 1)


def text_steps(eng, body):
    for layer in range(LAYERS):
        body(layer, 0)
        body(layer, 1)
        with eng.Fori(2, GROUPS) as g:
            body(layer, g)
    body(LAYERS, 0)
    body(LAYERS, 1)


def back(layer, g, k):
    if isinstance(g, int) and g < k:
        return layer - 1, g + GROUPS - k
    return layer, g - k


def attention_steps(eng, body):
    body(0, 0)
    body(1, 1)
    with eng.Fori(1, GROUPS // 2 - 1) as pair:
        for k in range(2):
            body(pair * 2 + k, k)
    for g in range(GROUPS - 2, GROUPS + 2):
        body(g, g % 2)


def has(g):
    return not isinstance(g, int) or 0 <= g < GROUPS


def build(nc, patches, patches_tail, tokens, tok_w, tok_b, cls, pos_enc, tok_emb, pos_emb, w_in, w_b, w_c, w_out,
          small, ln_gb, wqk, wv, bv, rel_bias, w_gate, w_up, w_down, ffn_gb, consts, out):
    ctx = ExitStack()
    with ctx:
        def sb(name, shape, dt=F32):
            return ctx.enter_context(nc.sbuf_tensor(name, shape, dt))

        def sem(name):
            return ctx.enter_context(nc.semaphore(name))

        seq = nc.dram_tensor("seq", (TOKENS, D), F32, kind="Internal").ap()
        xrows = nc.dram_tensor("xrows", (XROWS, ROW), F32, kind="Internal").ap()
        yrows = nc.dram_tensor("yrows", (YROWS, D), F32, kind="Internal").ap()

        cst = sb("cst", [P, CONSTS])
        sml = sb("sml", [P, SMALL])
        h_all = sb("h_all", [SEQ, BATCH, D])
        ident = cst[:, C_ID:C_ID + P]
        tri = cst[0:SEQ, C_TRI:C_TRI + SEQ]
        causal = cst[0:SEQ, C_CAUSAL:C_CAUSAL + SEQ]
        ones = cst[0:SEQ, C_ONE:C_ONE + SEQ]
        expert_no = cst[0:SEQ, C_EXP:C_EXP + EXPERTS]
        bias_t = sb("bias_t", [SEQ, SEQ])
        wqk_s = sb("wqk_s", [P, DC, QK])
        wv_s = sb("wv_s", [P, DC, D])
        minus_half = sb("minus_half", [P, GB])
        tab_s = sb("tab_s", [SEQ, 32])
        base_m = sb("base_m", [SEQ, EXPERTS])
        dest_i = sb("dest_i", [P, 2], I32)
        row_wt = sb("row_wt", [P, 2])

        FFN_COLS = DC * EXPERTS * FFN * 2 + FC * EXPERTS * D
        TEXT_COLS = LAYERS * (DC * 2 * INNER + FC * STATE + INNER + FC * D) + DC * BATCH * TXT + GROUPS * NT * D
        arena_a = sb("arena_a", [P, max(FFN_COLS, TEXT_COLS)])
        at = [0]

        def part(arena, cols, shape=None, rows=P):
            v = arena[0:rows, at[0]:at[0] + cols]
            at[0] += cols
            assert at[0] <= arena.shape[1], (at[0], arena.shape)
            return v

        win_s = part(arena_a, LAYERS * DC * 2 * INNER).rearrange("p (l c n) -> p l c n", l=LAYERS, c=DC)
        wb_s = part(arena_a, LAYERS * FC * STATE).rearrange("p (l c n) -> p l c n", l=LAYERS, c=FC)
        wc_s = part(arena_a, LAYERS * INNER, rows=STATE).rearrange("p (l n) -> p l n", l=LAYERS)
        wo_s = part(arena_a, LAYERS * FC * D).rearrange("p (l c n) -> p l c n", l=LAYERS, c=FC)
        xt = part(arena_a, DC * BATCH * TXT).rearrange("p (c t) -> p c t", c=DC)
        xtok = part(arena_a, GROUPS * NT * D, rows=TR)
        at[0] = 0
        wg_s = part(arena_a, DC * EXPERTS * FFN).rearrange("p (c n) -> p c n", c=DC)
        wu_s = part(arena_a, DC * EXPERTS * FFN).rearrange("p (c n) -> p c n", c=DC)
        wd_s = part(arena_a, FC * EXPERTS * D).rearrange("p (c n) -> p c n", c=FC)
        a_vb = part(arena_a, GB * D, rows=SEQ).rearrange("p (k d) -> p k d", k=GB)
        ffn_s = part(arena_a, 2 * D, rows=SEQ).rearrange("p (s d) -> p s d", s=2)
        bv_s = part(arena_a, D, rows=SEQ)

        arena_b = sb("arena_b", [P, 11264])
        at[0] = 0
        xin = part(arena_b, FC * GB * PADT).rearrange("p (c b t) -> p c b t", c=FC, b=GB)
        acc = part(arena_b, FC * GT).rearrange("p (c t) -> p c t", c=FC)
        u = part(arena_b, FC * GT).rearrange("p (c t) -> p c t", c=FC)
        sg = part(arena_b, FC * GT).rearrange("p (c t) -> p c t", c=FC)
        yt = part(arena_b, FC * GT).rearrange("p (c t) -> p c t", c=FC)
        bu = part(arena_b, GT, rows=STATE)
        hs = part(arena_b, GT, rows=STATE)
        decay = part(arena_b, GT, rows=STATE)
        z = part(arena_b, NT * D, rows=TR).rearrange("p (j d) -> p j d", j=NT)
        n = part(arena_b, NT * D, rows=TR).rearrange("p (j d) -> p j d", j=NT)
        ng = part(arena_b, NT * D, rows=TR).rearrange("p (j d) -> p j d", j=NT)
        stats = part(arena_b, NT * 6, rows=TR).rearrange("p (j s) -> p j s", j=NT)
        mv = part(arena_b, NT * 2, rows=TR).rearrange("p (j s) -> p j s", j=NT)
        rstd = part(arena_b, 2 * NT, rows=TR).rearrange("p (k j) -> p k j", k=2)
        emb = [part(arena_b, NT * D, rows=TR).rearrange("p (j d) -> p j d", j=NT) for _ in range(2)]
        tokens_s = sb("tokens_s", [TR, GROUPS * NT], I32)
        tok_now = sb("tok_now", [TR, 2, NT], I32)
        arena_c = sb("arena_c", [P, (EXPERTS + SPARE) * ROW])
        padbuf = arena_c[:, :].rearrange("p (k d) -> p k d", d=ROW)
        at[0] = 0
        pos_s = part(arena_c, NT * D, rows=TR).rearrange("p (j d) -> p j d", j=NT)
        gb_s = part(arena_c, LAYERS * 2 * D, rows=TR).rearrange("p (l s d) -> p l s d", l=LAYERS, s=2)
        h_flat = h_all[:, :, :].rearrange("p b d -> p (b d)")
        at[0] = FC * GB * PADT
        tokw_s = part(arena_b, IN_CH // P * D).rearrange("p (c d) -> p c d", c=IN_CH // P)
        pat = [part(arena_b, IN_CH // P * PT).rearrange("p (c t) -> p c t", c=IN_CH // P) for _ in range(2)]
        pat_out = [h_flat[0:PT, k * D:(k + 1) * D] for k in range(2)]
        posb = h_flat[0:PT, 2 * D:3 * D]
        tokb = h_flat[0:PT, 3 * D:4 * D]
        cls_s = h_flat[0:BATCH, 4 * D:5 * D]
        pos0 = h_flat[0:BATCH, 5 * D:6 * D]
        oh = h_flat[:, 8 * D:8 * D + 114 * 32 // 2]

        at[0] = 0
        a_n = part(arena_b, GB * D, rows=SEQ).rearrange("p (k d) -> p k d", k=GB)
        a_nt = part(arena_b, DC * GS).rearrange("p (c t) -> p c t", c=DC)
        a_qk = part(arena_b, GS)
        a_q = part(arena_b, GS)
        a_k = part(arena_b, GS)
        a_v = part(arena_b, GB * D, rows=SEQ).rearrange("p (k d) -> p k d", k=GB)
        a_arg = part(arena_b, GS, rows=SEQ)
        a_rc = sb("a_rc", [SEQ, GS])[:, :]
        a_w = part(arena_b, GS, rows=SEQ)
        a_x = [[part(arena_b, GB * ROW, rows=SEQ).rearrange("p (k d) -> p k d", k=GB) for _ in range(2)]
               for _ in range(2)]
        m_t = part(arena_b, DC * GS).rearrange("p (c t) -> p c t", c=DC)
        a_st = part(arena_b, GB * 6, rows=SEQ).rearrange("p (k s) -> p k s", k=GB)
        a_mv = part(arena_b, GB * 2, rows=SEQ).rearrange("p (k s) -> p k s", k=GB)
        a_rs = part(arena_b, GB * 2, rows=SEQ).rearrange("p (s k) -> p s k", s=2)
        m_st = part(arena_b, GB * 6, rows=SEQ).rearrange("p (k s) -> p k s", k=GB)
        m_mv = part(arena_b, GB * 2, rows=SEQ).rearrange("p (k s) -> p k s", k=GB)
        m_rs = part(arena_b, GB * 2, rows=SEQ).rearrange("p (s k) -> p s k", s=2)
        lg = part(arena_b, GB * 8, rows=SEQ).rearrange("p (k e) -> p k e", k=GB)
        top = part(arena_b, GB * 8, rows=SEQ).rearrange("p (k e) -> p k e", k=GB)
        idx_f = part(arena_b, GB * 8, rows=SEQ).rearrange("p (k e) -> p k e", k=GB)
        one = [part(arena_b, GB * 8, rows=SEQ).rearrange("p (k e) -> p k e", k=GB) for _ in range(2)]
        both = part(arena_b, GB * 8, rows=SEQ).rearrange("p (k e) -> p k e", k=GB)
        before = part(arena_b, GB * 8, rows=SEQ).rearrange("p (k e) -> p k e", k=GB)
        place = part(arena_b, GB * 8, rows=SEQ).rearrange("p (k e) -> p k e", k=GB)
        picked = [part(arena_b, GB * 8, rows=SEQ).rearrange("p (k e) -> p k e", k=GB) for _ in range(2)]
        slot_f = part(arena_b, 2 * GB, rows=SEQ).rearrange("p (r k) -> p r k", r=2)
        gap = part(arena_b, GB, rows=SEQ)
        gap_tanh = part(arena_b, GB, rows=SEQ)
        at[0] = 0
        cnt = part(arena_b, EXPERTS)
        padrow_f = part(arena_b, EXPERTS)
        steps_b = part(arena_b, EXPERTS * COUNT_STEPS).rearrange("p (e k) -> p e k", e=EXPERTS)
        ntile = part(arena_b, EXPERTS)
        ends = part(arena_b, EXPERTS)
        delta = part(arena_b, EXPERTS)
        passed = part(arena_b, BLOCKS * EXPERTS).rearrange("p (j e) -> p j e", e=EXPERTS)
        shifts = part(arena_b, BLOCKS * EXPERTS).rearrange("p (j e) -> p j e", e=EXPERTS)
        expert_f = part(arena_b, BLOCKS)
        row_f = part(arena_b, BLOCKS)
        idx_u = sb("idx_u", [SEQ, GB, 8], U32)
        slot_i = [sb(f"slot_i{k}", [SEQ, 2, GB], I32) for k in range(2)]
        padrow_i = sb("padrow_i", [P, EXPERTS], I32)
        expert_i = sb("expert_i", [P, BLOCKS], I32)
        row_i = sb("row_i", [P, BLOCKS], I32)

        at[0] = 0
        x_g = [part(arena_b, ROW) for _ in range(2)]
        x_gt = [part(arena_b, DC * P).rearrange("p (c t) -> p c t", c=DC) for _ in range(2)]
        f_sg = part(arena_b, FFN)
        f_h = part(arena_b, FFN)
        f_ht = [part(arena_b, FFN).rearrange("p (c t) -> p c t", c=FC) for _ in range(2)]
        f_y = [part(arena_b, D) for _ in range(2)]
        at[0] = 0
        y12 = [part(arena_a, GB * 2 * D, rows=SEQ).rearrange("p (k d) -> p k d", k=GB) for _ in range(2)]
        y_sum = part(arena_a, GB * D, rows=SEQ).rearrange("p (k d) -> p k d", k=GB)
        y_n = part(arena_a, GB * D, rows=SEQ).rearrange("p (k d) -> p k d", k=GB)
        y_g = part(arena_a, GB * D, rows=SEQ).rearrange("p (k d) -> p k d", k=GB)
        y_out = [part(arena_a, GB * D, rows=SEQ).rearrange("p (k d) -> p k d", k=GB) for _ in range(2)]
        y_st = part(arena_a, GB * 6, rows=SEQ).rearrange("p (k s) -> p k s", k=GB)
        y_mv = part(arena_a, GB * 2, rows=SEQ).rearrange("p (k s) -> p k s", k=GB)
        y_rs = part(arena_a, GB * 2, rows=SEQ).rearrange("p (s k) -> p s k", s=2)

        bank = [ctx.enter_context(nc.psum_tensor(f"bank{k}", [P, 512], F32)) for k in range(8)]

        ld_cst = sem("ld_cst")
        ld_text = sem("ld_text")
        ld_tokw = sem("ld_tokw")
        ld_attn = sem("ld_attn")
        ld_pos = sem("ld_pos")
        ld_late = sem("ld_late")
        ld_toks = sem("ld_toks")
        ld_pat = [sem(f"ld_pat{k}") for k in range(2)]
        ld_ffn = sem("ld_ffn")
        ld_h = sem("ld_h")
        seq_stored = [sem(f"seq_stored{k}") for k in range(3)]
        posb_ready = sem("posb_ready")
        cls_ready = sem("cls_ready")
        pat_mm = sem("pat_mm")
        pat_ready = sem("pat_ready")
        zeroed = sem("zeroed")
        bias_seq = sem("bias_seq")
        tok_copied = sem("tok_copied")
        emb_ready = [sem(f"emb_ready{k}") for k in range(2)]
        pe_x, act_x = sem("pe_x"), sem("act_x")
        pe_g, act_g = sem("pe_g"), sem("act_g")
        pe_b, act_b = sem("pe_b"), sem("act_b")
        pe_c, dve_c, dve_y = sem("pe_c"), sem("dve_c"), sem("dve_y")
        dve_scan, act_u, dve_conv = sem("dve_scan"), sem("act_u"), sem("dve_conv")
        pe_o, dve_z, dve_bn, dve_stats = sem("pe_o"), sem("dve_z"), sem("dve_bn"), sem("dve_stats")
        pool_var, pool_rstd, dve_n = sem("pool_var"), sem("pool_rstd"), sem("dve_n")
        pe_t, act_xt, pool_ng, pool_x = sem("pe_t"), sem("act_xt"), sem("pool_ng"), sem("pool_x")
        dve_passed, pool_passed, sp_passed = sem("dve_passed"), sem("pool_passed"), sem("sp_passed")
        a_bn, a_var, m_bn, m_var, m_seq = sem("a_bn"), sem("a_var"), sem("m_bn"), sem("m_var"), sem("m_seq")
        a_stats, a_rstd, a_norm = sem("a_stats"), sem("a_rstd"), sem("a_norm")
        a_tr, a_trc, a_qkm, a_qks, a_qkd = sem("a_tr"), sem("a_trc"), sem("a_qkm"), sem("a_qks"), sem("a_qkd")
        a_vm, a_va, a_vs = sem("a_vm"), sem("a_va"), sem("a_vs")
        a_sm, a_sa, a_er, a_at = sem("a_sm"), sem("a_sa"), sem("a_er"), sem("a_at")
        a_rec = sem("a_rec")
        a_om, a_h2 = sem("a_om"), sem("a_h2")
        m_stats, m_rstd, m_norm, m_tr, m_trc = sem("m_stats"), sem("m_rstd"), sem("m_norm"), sem("m_tr"), sem("m_trc")
        m_lm, m_lg, m_gap, m_wt, m_both, m_rk = sem("m_lm"), sem("m_lg"), sem("m_gap"), sem("m_wt"), sem("m_both"), sem("m_rk")
        m_slot, m_row2, pad_zero = sem("m_slot"), sem("m_row2"), sem("pad_zero")
        x_sent = [sem(f"x_sent{k}") for k in range(2)]
        cnt_mm, tb, tbl_ready, pad_ready, pad_sent, spare_sent = (
            sem("cnt_mm"), sem("tb"), sem("tbl_ready"), sem("pad_ready"), sem("pad_sent"), sem("spare_sent"))
        x_in = [sem(f"x_in{k}") for k in range(2)]
        f_tr, f_trc, f_gm, f_um, f_silu, f_hh = sem("f_tr"), sem("f_trc"), sem("f_gm"), sem("f_um"), sem("f_silu"), sem("f_hh")
        f_hm, f_htc, f_dm, f_yc, f_dest = sem("f_hm"), sem("f_htc"), sem("f_dm"), sem("f_yc"), sem("f_dest")
        y_sent = [sem(f"y_sent{k}") for k in range(2)]
        h2b = sem("h2b")
        y_in = [sem(f"y_in{k}") for k in range(2)]
        yf, y_stats, y_rstd, y_normed, y_gained, y_done = (
            sem("yf"), sem("y_stats"), sem("y_rstd"), sem("y_normed"), sem("y_gained"), sem("y_done"))
        y_var = sem("y_var")
        out_sent = [sem(f"out_sent{k}") for k in range(2)]

        SML = lambda at_, *_: sml[:, at_:at_ + 1]
        seq_b = seq.rearrange("(b s) d -> b s d", s=SEQ)

        def conv_w(layer, c, tap):
            return SML(W_CONV + (layer * FC + c) * 4 + tap)

        def group_rows(tile, g):
            return tile[:, bass.ds(g * (NT * D), NT * D)].rearrange("p (j d) -> p j d", j=NT)

        N_STEPS = LAYERS * GROUPS
        ALL_T = 2 * N_STEPS
        pieces = []
        for j in range(NT):
            t = TILE_AT[j]
            while t < TILE_AT[j] + TILE_ROWS[j]:
                b, p = divmod(t, TXT)
                m = min(TXT - p, TILE_AT[j] + TILE_ROWS[j] - t)
                pieces.append((j, t - TILE_AT[j], m, b, p))
                t += m
        PIECES = len(pieces)

        block = ctx.enter_context(nc.Block())

        def store_out(sp, g):
            sp.wait_ge(y_done, g + 1)
            sp.dma_start(out[g * GB:(g + 1) * GB].rearrange("b s d -> s b d"), y_out[g % 2]).then_inc(out_sent[g % 2], 16)

        @block.sync
        def _(sp):
            sp.dma_start(tokw_s[:, :, :], tok_w).then_inc(ld_tokw, 16)
            for k in range(2):
                sp.dma_start(pat[k][:, :, :], patches[k]).then_inc(ld_pat[k], 16)
            sp.dma_start(cst[:, :], consts).then_inc(ld_cst, 16)
            sp.dma_start(sml[:, :], small).then_inc(ld_cst, 16)
            sp.dma_start(win_s, w_in).then_inc(ld_text, 16)
            sp.dma_start(wb_s, w_b).then_inc(ld_text, 16)
            sp.dma_start(wc_s, w_c).then_inc(ld_text, 16)
            sp.dma_start(wo_s, w_out).then_inc(ld_text, 16)
            sp.dma_start(gb_s[:, :, :, :], ln_gb.partition_broadcast(TR)).then_inc(ld_text, 16)

            def store_patches(i, k, seqs=PT_SEQS):
                sp.wait_ge(pat_ready, i + 1)
                for q in range(seqs):
                    sp.dma_start(seq_b[bass.ds(i * PT_SEQS + q, 1), 1:1 + PATCHES, :].rearrange("b s d -> (b s) d"),
                                 pat_out[k][q * PATCHES:(q + 1) * PATCHES, :]).then_inc(seq_stored[k], 16)

            with sp.Fori(0, PT_FULL // 2 - 1) as pair:
                for k in range(2):
                    i = pair * 2 + k
                    sp.wait_ge(pat_mm, i + 1)
                    sp.dma_start(pat[k][:, :, :], patches[bass.ds(i + 2, 1)].rearrange("a p c t -> (a p) c t"))\
                        .then_inc(ld_pat[k], 16)
                    store_patches(i, k)
            sp.wait_ge(pat_mm, PT_FULL - 1)
            sp.dma_start(pat[0][:, :, 0:PT_TAIL], patches_tail).then_inc(ld_pat[0], 16)
            store_patches(PT_FULL - 2, 0)
            store_patches(PT_FULL - 1, 1)
            store_patches(PT_FULL, 0, PT_TAIL // PATCHES)
            sp.wait_ge(cls_ready, 1)
            sp.dma_start(seq_b[:, 0, :], cls_s).then_inc(seq_stored[1], 16)

            def store_text(g):
                sp.wait_ge(pool_x, g + (LAYERS * GROUPS + 1))
                settled(sp, sp_passed)
                rows = group_rows(xtok, g)
                for j, r0, m, b, p in pieces:
                    sp.dma_start(seq_b[bass.ds(g * GB + b, 1), 1 + PATCHES + p:1 + PATCHES + p + m, :]
                                 .rearrange("b s d -> (b s) d"), rows[r0:r0 + m, j, :]).then_inc(seq_stored[2], 16)

            def load_fused(g):
                sp.wait_ge(seq_stored[2], g * (16 * PIECES) + 16 * PIECES)
                settled(sp, sp_passed)
                wait(sp, ld_h, g * 16)
                settled(sp, sp_passed)
                sp.dma_start(h_all[:, bass.ds(g * GB, GB), :],
                             seq_b[bass.ds(g * GB, GB)].rearrange("b s d -> s b d")).then_inc(ld_h, 16)

            sp.wait_ge(seq_stored[0], 16 * (PT_SEQS * (PT_FULL // 2) + PT_TAIL // PATCHES))
            sp.wait_ge(seq_stored[1], 16 * (PT_SEQS * (PT_FULL // 2) + 1))
            sp.wait_ge(bias_seq, 6)
            store_text(0)
            load_fused(0)
            with sp.Fori(1, GROUPS) as g:
                store_text(g)
                load_fused(g)
            for dst, src in ((ffn_s, ffn_gb), (bv_s, bv)):
                sp.dma_start(dst, src.partition_broadcast(SEQ)).then_inc(ld_late, 16)
            for dst, src in ((wg_s, w_gate), (wu_s, w_up), (wd_s, w_down)):
                sp.dma_start(dst, src).then_inc(ld_ffn, 16)

            sp.wait_ge(pad_sent, 16 * EXPERTS)
            sp.wait_ge(spare_sent, 16)
            for k in range(2):
                sp.wait_ge(x_sent[k], 16 * 2 * GB * (GROUPS // 2))
            sp.wait_ge(tbl_ready, 2)

            def load_block(j, k):
                row = sp.value_load(row_i[0:1, bass.ds(j, 1)], min_val=0, max_val=XROWS - P)
                sp.dma_start(x_g[k], xrows[bass.ds(row, P), :]).then_inc(x_in[k], 16)

            load_block(0, 0)
            load_block(1, 1)
            with sp.Fori(1, BLOCKS // 2) as pair:
                for k in range(2):
                    j = pair * 2 + k
                    sp.wait_ge(f_tr, j - 1)
                    sp.wait_ge(f_dest, j - 1)
                    load_block(j, k)

            for k in range(2):
                sp.wait_ge(y_sent[k], 16 * (BLOCKS // 2))
            for g in range(GROUPS):
                k = g % 2
                if g >= 2:
                    sp.wait_ge(yf, 10 * (g - 2) + 1)
                sp.dma_start(y12[k], yrows[g * GS * 2:(g + 1) * GS * 2].rearrange("(b s r) d -> s b (r d)", s=SEQ, r=2))\
                    .then_inc(y_in[k], 16)
                if g >= 1:
                    store_out(sp, g - 1)
            store_out(sp, GROUPS - 1)
            for k in range(2):
                sp.wait_ge(out_sent[k], 16 * (GROUPS // 2))

        @block.scalar
        def _(act):
            act.dma_start(tokens_s[:, :], tokens).then_inc(ld_toks, 16)
            act.dma_start(tokb, tok_b.partition_broadcast(PT)).then_inc(ld_pos, 16)
            for q in range(PT_SEQS):
                act.dma_start(posb[q * PATCHES:(q + 1) * PATCHES, :], pos_enc[1:1 + PATCHES, :]).then_inc(ld_pos, 16)
            act.dma_start(cls_s, cls.partition_broadcast(BATCH)).then_inc(ld_pos, 16)
            act.dma_start(pos0, pos_enc[0].partition_broadcast(BATCH)).then_inc(ld_pos, 16)
            for j, r0, m, b, p in pieces:
                act.dma_start(pos_s[r0:r0 + m, j, :], pos_emb[p:p + m, :]).then_inc(ld_pos, 16)
            act.dma_start(wqk_s[:, :, :], wqk).then_inc(ld_attn, 16)
            act.dma_start(wv_s[:, :, :], wv).then_inc(ld_attn, 16)
            act.dma_start(tab_s[:, :], rel_bias.partition_broadcast(SEQ)).then_inc(ld_attn, 16)
            act.wait_ge(ld_cst, 32)

            def xt_copy(t, g, layer, d):
                act.wait_ge(pe_t, t * 2 + (d + 1))
                dst = xt[:, d, bass.ds(g * GT, GT)]
                if layer < 0:
                    act.activation(dst, bank[7][:, 0:GT], ACT.Copy).then_inc(act_xt, 1)
                else:
                    at_ = W_LN + (layer * DC + d) * 2
                    act.activation(dst, bank[7][:, 0:GT], ACT.Identity, bias=SML(at_ + 1), scale=SML(at_))\
                        .then_inc(act_xt, 1)

            with act.Fori(0, GROUPS) as g:
                for d in range(DC):
                    xt_copy(g, g, -1, d)

            def text_step(layer, g):
                s = layer * GROUPS + g
                lb, gb = back(layer, g, 1)
                lt, gt = back(layer, g, 2)
                sb_, st_ = lb * GROUPS + gb, (lt + 1) * GROUPS + gt
                if layer < LAYERS:
                    for c in range(FC):
                        act.wait_ge(pe_x, s * 4 + (c + 1))
                        wait(act, dve_conv, s * 12)
                        wait(act, act_u, s * 4)
                        act.activation(xin[:, c, :, 3:PADT], bank[c][:, 0:GT].rearrange("p (b t) -> p b t", b=GB), ACT.Copy)
                        act.activation(acc[:, c, :], bank[c][:, 0:GT], ACT.Identity,
                                       bias=SML(W_CB + layer * FC + c), scale=conv_w(layer, c, 3)).then_inc(act_x, 1)
                if 0 <= lb < LAYERS:
                    act.wait_ge(pe_b, sb_ + 1)
                    wait(act, dve_scan, sb_)
                    act.activation(bu, bank[4][0:STATE, 0:GT], ACT.Copy, scale=0.05).then_inc(act_b, 1)
                if 0 <= lt < LAYERS - 1:
                    xt_copy(st_, gt, lt, 0)
                for c in range(FC):
                    if c == 2 and 0 <= lt < LAYERS - 1:
                        xt_copy(st_, gt, lt, 1)
                    if 0 <= lb < LAYERS:
                        act.wait_ge(pe_g, sb_ * 4 + (c + 1))
                        wait(act, dve_y, sb_ * 4)
                        act.activation(sg[:, c, :], bank[(0, 1, 1, 2)[c]][:, 0:GT], ACT.Silu).then_inc(act_g, 1)
                if layer < LAYERS:
                    for c in range(FC):
                        act.wait_ge(dve_conv, s * 12 + (9 + c))
                        wait(act, dve_y, s * 4)
                        act.activation(u[:, c, :], acc[:, c, :], ACT.Silu).then_inc(act_u, 1)

            text_steps(act, text_step)

            act.wait_ge(pool_x, (LAYERS + 1) * GROUPS)
            act.wait_ge(ld_attn, 48)

            def attn_step(g, k):
                if has(g):
                    for d in range(DC):
                        act.wait_ge(a_tr, g * 2 + (d + 1))
                        wait(act, a_vm, g * 2)
                        act.activation(a_nt[:, d, :], bank[d][:, 0:GS], ACT.Copy).then_inc(a_trc, 1)
                if has(g - 1):
                    act.wait_ge(a_sa, g)
                    wait(act, a_om, (g - 1) * 2)
                    act.activation(a_w, a_arg, ACT.Gelu).then_inc(a_er, 1)
                if has(g - 2):
                    for d in range(DC):
                        act.wait_ge(m_tr, (g - 2) * 2 + (d + 1))
                        wait(act, m_lm, g - 2)
                        act.activation(m_t[:, d, :], bank[6][:, 0:GS], ACT.Copy).then_inc(m_trc, 1)
                if has(g):
                    act.wait_ge(a_qkm, g + 1)
                    wait(act, a_qkd, g)
                    act.activation(a_qk, bank[2][:, 0:GS], ACT.Silu, bias=SML(W_QK)).then_inc(a_qks, 1)
                if has(g - 2):
                    act.wait_ge(m_norm, g - 1)
                    act.activation(a_x[k][1][:, :, 0:D], a_x[k][0][:, :, 0:D], ACT.Copy).then_inc(m_row2, 1)
                    act.wait_ge(m_gap, g - 1)
                    act.activation(gap_tanh, gap, ACT.Tanh, scale=0.5).then_inc(m_wt, 1)
                if has(g):
                    act.wait_ge(a_va, g * 2 + 2)
                    wait(act, a_om, g * 2)
                    act.activation(a_v, a_vb, ACT.Silu).then_inc(a_vs, 1)

            attention_steps(act, attn_step)

            def turn(j, k):
                act.wait_ge(f_tr, j + 1)
                wait(act, f_um, j - 1)
                act.activation(x_gt[k], bank[2][:, 0:DC * P].rearrange("p (c t) -> p c t", c=DC), ACT.Copy)\
                    .then_inc(f_trc, 1)

            def gate(j):
                act.wait_ge(f_gm, j + 1)
                wait(act, f_hh, j)
                act.activation(f_sg, bank[0][:, :], ACT.Silu).then_inc(f_silu, 1)

            def back_half(j, k):
                act.wait_ge(f_dm, j + 1)
                wait(act, y_sent[k], (j - k) * 8)
                act.wait_ge(f_dest, j + 1)
                act.activation(f_y[k], bank[4 + k][:, 0:D], ACT.Copy, scale=row_wt[:, k:k + 1]).then_inc(f_yc, 1)

            def expert_step(j, k):
                gate(j)
                turn(j + 1, 1 - k)
                back_half(j - 1, 1 - k)

            act.wait_ge(tbl_ready, 2)
            turn(0, 0)
            gate(0)
            turn(1, 1)
            expert_step(1, 1)
            expert_step(2, 0)
            with act.Fori(1, BLOCKS // 2 - 1) as pair:
                expert_step(pair * 2 + 1, 1)
                expert_step(pair * 2 + 2, 0)
            gate(BLOCKS - 1)
            back_half(BLOCKS - 2, 0)
            back_half(BLOCKS - 1, 1)

        @block.gpsimd
        def _(pool):
            pool.memset(xin, 0.0).then_inc(zeroed, 1)
            pool.memset(decay, 0.95).then_inc(zeroed, 1)
            for t in (z, n, mv, emb[0], emb[1], minus_half[:, :]):
                pool.memset(t, 1.0).then_inc(zeroed, 1)
            pool.wait_ge(zeroed, 8)
            pool.memset(decay.rearrange("p (b t) -> p b t", b=GB)[:, :, 0:1], 0.0).then_inc(zeroed, 1)
            pool.memset(minus_half[:, :], -0.5).then_inc(zeroed, 1)
            pool.memset(base_m[:, :], 0.0).then_inc(zeroed, 1)
            pool.wait_ge(ld_toks, 16)
            pool.wait_ge(zeroed, 11)

            def gather(g, k, turn_):
                wait(pool, dve_n, (g - 1) * NT)
                settled(pool, pool_passed)
                pool.tensor_copy(tok_now[:, k, :], tokens_s[:, bass.ds(g * NT, NT)]).then_inc(tok_copied, 1)
                pool.wait_ge(tok_copied, g + 1)
                for j in range(NT):
                    m = TILE_ROWS[j]
                    settled(pool, pool_passed)
                    pool.indirect_dma_start(emb[k][0:m, j, :], None, tok_emb,
                                            bass.IndirectOffsetOnAxis(ap=tok_now[0:m, k, j:j + 1], axis=0))\
                        .then_inc(emb_ready[k], 16)

            def keep_embedding(g):
                pool.wait_ge(dve_n, g * NT + NT)
                settled(pool, pool_passed)
                pool.tensor_copy(group_rows(xtok, g), n).then_inc(pool_x, 1)

            gather(0, 0, 0)
            gather(1, 1, 0)
            with pool.Fori(1, GROUPS // 2) as pair:
                for k in range(2):
                    keep_embedding(pair * 2 + (k - 2))
                    pool.wait_ge(emb_ready[k], pair * (NT * 16))
                    gather(pair * 2 + k, k, pair)
            keep_embedding(GROUPS - 2)
            keep_embedding(GROUPS - 1)
            pool.wait_ge(ld_text, 80)

            def text_step(layer, g):
                lt, gt = back(layer, g, 2)
                if not 0 <= lt < LAYERS:
                    return
                s = lt * GROUPS + gt
                pool.wait_ge(dve_stats, s + 1)
                settled(pool, pool_passed)
                pool.tensor_scalar(rstd[:, 1, :], mv[:, :, 1], EPS, None, ALU.add).then_inc(pool_var, 1)
                pool.wait_ge(pool_var, s + 1)
                pool.tensor_tensor(rstd[:, 0, :], rstd[:, 1, :], minus_half[0:TR, 0:NT], ALU.pow).then_inc(pool_rstd, 1)
                pool.wait_ge(dve_n, (s + GROUPS) * NT + NT)
                gain = gb_s[:, lt, 0:1, :].broadcast_to([TR, NT, D])
                bias = gb_s[:, lt, 1:2, :].broadcast_to([TR, NT, D])
                pool.tensor_tensor(ng, n, gain, ALU.mult).then_inc(pool_ng, 1)
                pool.wait_ge(pool_ng, s + 1)
                pool.tensor_tensor(group_rows(xtok, gt), ng, bias, ALU.add).then_inc(pool_x, 1)

            text_steps(pool, text_step)

            def rsqrt(mv_, rs, stats_sem, count, chain, rstd_sem):
                pool.wait_ge(stats_sem, count)
                settled(pool, pool_passed)
                v = chain.inc(pool.tensor_scalar(rs[:, 1, :], mv_[:, :, 1], EPS, None, ALU.add))
                chain.wait(v)
                pool.tensor_tensor(rs[:, 0, :], rs[:, 1, :], minus_half[0:SEQ, 0:GB], ALU.pow).then_inc(rstd_sem, 1)

            def norm_ahead(g):
                rsqrt(a_mv, a_rs, a_stats, g + 1, Chain(pool, a_var, 1, g), a_rstd)

            def attn_step(g, k):
                if has(g + 1):
                    norm_ahead(g + 1)
                if has(g - 1):
                    rsqrt(m_mv, m_rs, m_stats, g, Chain(pool, m_var, 1, g - 1), m_rstd)
                if has(g - 2):
                    pool.wait_ge(m_row2, g - 1)
                    pool.wait_ge(m_slot, g - 1)
                    for r in range(2):
                        for b in range(GB):
                            settled(pool, pool_passed)
                            pool.indirect_dma_start(xrows, bass.IndirectOffsetOnAxis(ap=slot_i[k][:, r, b:b + 1], axis=0),
                                                    a_x[k][r][:, b, :], None).then_inc(x_sent[k], 16)

            pool.wait_ge(pool_x, (LAYERS + 1) * GROUPS)
            pool.memset(padbuf, 0.0).then_inc(pad_zero, 1)
            norm_ahead(0)
            attention_steps(pool, attn_step)

            pool.wait_ge(pad_ready, 2)
            for e in range(EXPERTS):
                pool.indirect_dma_start(xrows, bass.IndirectOffsetOnAxis(ap=padrow_i[:, e:e + 1], axis=0),
                                        padbuf[:, e, :], None).then_inc(pad_sent, 16)
            pool.dma_start(xrows[EXPERTS * REGION:XROWS, :].rearrange("(k p) d -> p k d", p=P),
                           padbuf[:, EXPERTS:EXPERTS + SPARE, :]).then_inc(spare_sent, 16)

            def send(j, k):
                pool.wait_ge(f_yc, j + 1)
                pool.wait_ge(f_dest, j + 1)
                settled(pool, pool_passed)
                pool.indirect_dma_start(yrows, bass.IndirectOffsetOnAxis(ap=dest_i[:, k:k + 1], axis=0), f_y[k], None)\
                    .then_inc(y_sent[k], 16)

            assert BLOCKS // 2 == BATCH
            pool.wait_ge(ld_late, 32)
            with pool.Fori(0, BATCH) as pair:
                for k in range(2):
                    send(pair * 2 + k, k)
                one_h = h_all[:, bass.ds(pair, 1), :]
                pool.tensor_tensor(one_h, one_h, ffn_s[:, 1:2, :], ALU.add).then_inc(h2b, 1)

            for g in range(GROUPS):
                pool.wait_ge(y_stats, g + 1)
                pool.tensor_scalar(y_rs[:, 1, :], y_mv[:, :, 1], EPS, None, ALU.add).then_inc(y_var, 1)
                pool.wait_ge(y_var, g + 1)
                pool.tensor_tensor(y_rs[:, 0, :], y_rs[:, 1, :], minus_half[0:SEQ, 0:GB], ALU.pow).then_inc(y_rstd, 1)

        @block.tensor
        def _(pe):
            def patch_tile(i, k, m, turn_):
                pe.wait_ge(ld_pat[k], turn_ * 16 + 16)
                wait(pe, pat_ready, i - 1)
                for c in range(IN_CH // P):
                    mm = pe.matmul(bank[k][0:m, 0:D], pat[k][:, c, 0:m], tokw_s[:, c, :], start=(c == 0),
                                   stop=(c == IN_CH // P - 1))
                mm.then_inc(pat_mm, 1)

            pe.wait_ge(ld_tokw, 16)
            patch_tile(0, 0, PT, 0)
            patch_tile(1, 1, PT, 0)
            with pe.Fori(1, PT_FULL // 2) as pair:
                for k in range(2):
                    patch_tile(pair * 2 + k, k, PT, pair)
            patch_tile(PT_FULL, 0, PT_TAIL, PT_FULL // 2)

            pe.wait_ge(ld_cst, 32)

            def turn(t, d):
                pe.wait_ge(dve_n, t * NT + NT)
                wait(pe, act_xt, t * 2 + d)
                for j in range(NT):
                    m = TILE_ROWS[j]
                    mm = pe.transpose(bank[7][:, TILE_AT[j]:TILE_AT[j] + m], n[0:m, j, d * P:(d + 1) * P],
                                      ident[0:m, 0:m])
                mm.then_inc(pe_t, 1)

            for d in range(DC):
                turn(0, d)
            with pe.Fori(1, GROUPS) as g:
                for d in range(DC):
                    turn(g, d)
            pe.wait_ge(ld_text, 80)

            def text_step(layer, g):
                s = layer * GROUPS + g
                lb, gb = back(layer, g, 1)
                lt, gt = back(layer, g, 2)
                sb_, st_ = lb * GROUPS + gb, (lt + 1) * GROUPS + gt
                late = 0 <= lb < LAYERS

                def in_product(l, group, c, out_):
                    for d in range(DC):
                        mm = pe.matmul(out_, win_s[:, l, d, c * P:(c + 1) * P], xt[:, d, bass.ds(group * GT, GT)],
                                       start=(d == 0), stop=(d == DC - 1))
                    return mm

                def gate_product(c, b):
                    in_product(lb, gb, FC + c, bank[b][:, 0:GT]).then_inc(pe_g, 1)

                if layer < LAYERS:
                    pe.wait_ge(act_xt, s * 2 + 2)
                    for c, (q, v) in enumerate(((dve_c, (s - 1) * 4), (act_g, (s - 2) * 4 + 3), (act_g, (s - 1) * 4),
                                                (dve_c, (s - 2) * 4 + 2))):
                        wait(pe, q, v)
                        if isinstance(s, int) and s == 1:
                            pe.wait_ge(act_x, c + 1)
                        in_product(layer, g, c, bank[c][:, 0:GT]).then_inc(pe_x, 1)
                if late:
                    for c in range(FC):
                        pe.wait_ge(act_u, sb_ * 4 + (c + 1))
                        wait(pe, dve_c, (sb_ - 1) * 4 + 3)
                        mm = pe.matmul(bank[4][0:STATE, 0:GT], wb_s[:, lb, c, :], u[:, c, :], start=(c == 0),
                                       stop=(c == FC - 1))
                    mm.then_inc(pe_b, 1)
                if 0 <= lt < LAYERS - 1:
                    turn(st_, 0)
                if late:
                    if layer < LAYERS:
                        pe.wait_ge(act_x, s * 4 + 2)
                    gate_product(0, 0)
                    gate_product(1, 1)
                if 0 <= lt < LAYERS - 1:
                    turn(st_, 1)
                if late:
                    if layer < LAYERS:
                        pe.wait_ge(act_x, s * 4 + 4)
                    pe.wait_ge(dve_scan, sb_ + 1)
                    for c, b in enumerate((2, 3, 4, 0)):
                        if c == 2:
                            pe.wait_ge(act_b, sb_ + 1)
                        if c == 3:
                            pe.wait_ge(act_g, sb_ * 4 + 1)
                        pe.matmul(bank[b][:, 0:GT], wc_s[:, lb, c * P:(c + 1) * P], hs, start=True, stop=True)\
                            .then_inc(pe_c, 1)
                    pe.wait_ge(act_g, sb_ * 4 + 2)
                    gate_product(2, 1)
                    pe.wait_ge(dve_c, sb_ * 4 + 1)
                    gate_product(3, 2)
                    for j in range(NT):
                        m = TILE_ROWS[j]
                        wait(pe, dve_z, (sb_ * 3, (sb_ - 1) * 3 + 2, sb_ * 3 + 1)[j])
                        for c in range(FC):
                            if j == 0:
                                pe.wait_ge(dve_y, sb_ * 4 + (c + 1))
                            mm = pe.matmul(bank[5 + j % 2][0:m, 0:D], yt[:, c, TILE_AT[j]:TILE_AT[j] + m],
                                           wo_s[:, lb, c, :], start=(c == 0), stop=(c == FC - 1))
                        mm.then_inc(pe_o, 1)

            text_steps(pe, text_step)

            pe.wait_ge(pool_x, (LAYERS + 1) * GROUPS)
            pe.wait_ge(ld_attn, 48)

            def values(g, half):
                wait(pe, a_va, g * 2 + half)
                for b in range(2 * half, 2 * half + 2):
                    for d in range(DC):
                        mm = pe.matmul(bank[3][0:SEQ, (b % 2) * D:(b % 2 + 1) * D], a_nt[:, d, b * SEQ:(b + 1) * SEQ],
                                       wv_s[:, d, :], start=(d == 0), stop=(d == DC - 1))
                mm.then_inc(a_vm, 1)

            def attended(g, half):
                pe.wait_ge(a_at, g + 1)
                pe.wait_ge(a_vs, g + 1)
                wait(pe, a_h2, g * 2 + half)
                for b in range(2 * half, 2 * half + 2):
                    mm = pe.matmul(bank[5][0:SEQ, (b % 2) * D:(b % 2 + 1) * D], a_w[:, b * SEQ:(b + 1) * SEQ],
                                   a_v[:, b, :], start=True, stop=True)
                mm.then_inc(a_om, 1)

            def turn_routed(g, k, d):
                pe.wait_ge(m_norm, g + 1)
                wait(pe, m_trc, g * 2 + d)
                for b in range(GB):
                    mm = pe.transpose(bank[6][:, b * SEQ:(b + 1) * SEQ], a_x[k][0][:, b, d * P:(d + 1) * P],
                                      ident[0:SEQ, 0:SEQ])
                mm.then_inc(m_tr, 1)

            def attn_step(g, k):
                if has(g - 1):
                    pe.wait_ge(a_qkd, g)
                    wait(pe, a_sa, g - 1)
                    for b in range(GB):
                        cut = slice(b * SEQ, (b + 1) * SEQ)
                        mm = pe.matmul(bank[4][0:SEQ, cut], a_k[:, cut], a_q[:, cut], start=True, stop=True)
                    mm.then_inc(a_sm, 1)
                if has(g):
                    pe.wait_ge(a_norm, g + 1)
                    for d in range(DC):
                        wait(pe, a_trc, g * 2 + (d - 1))
                        for b in range(GB):
                            mm = pe.transpose(bank[d][:, b * SEQ:(b + 1) * SEQ], a_n[:, b, d * P:(d + 1) * P],
                                              ident[0:SEQ, 0:SEQ])
                        mm.then_inc(a_tr, 1)
                if has(g - 2):
                    turn_routed(g - 2, k, 0)
                if has(g):
                    pe.wait_ge(a_trc, g * 2 + 2)
                    wait(pe, a_qks, g)
                    for d in range(DC):
                        mm = pe.matmul(bank[2][:, 0:GS], wqk_s[:, d, :], a_nt[:, d, :], start=(d == 0),
                                       stop=(d == DC - 1))
                    mm.then_inc(a_qkm, 1)
                if has(g - 2):
                    turn_routed(g - 2, k, 1)
                if has(g):
                    values(g, 0)
                if has(g - 2):
                    pe.wait_ge(m_trc, (g - 2) * 2 + 2)
                    wait(pe, m_slot, g - 2)
                    for b in range(GB):
                        for d in range(DC):
                            at_ = W_R + d * EXPERTS
                            mm = pe.matmul(bank[7][0:SEQ, b * 8:(b + 1) * 8], m_t[:, d, b * SEQ:(b + 1) * SEQ],
                                           sml[:, at_:at_ + EXPERTS], start=(d == 0), stop=(d == DC - 1))
                    mm.then_inc(m_lm, 1)
                if has(g - 1):
                    attended(g - 1, 0)
                    attended(g - 1, 1)
                if has(g):
                    values(g, 1)
                if has(g - 2):
                    pe.wait_ge(m_both, g - 1)
                    pe.matmul(bank[7][0:SEQ, 0:GB * 8], tri, both.rearrange("p k e -> p (k e)"), start=True, stop=False)
                    pe.matmul(bank[7][0:SEQ, 0:GB * 8], ones, before.rearrange("p k e -> p (k e)"), start=False,
                              stop=True).then_inc(m_rk, 1)

            attention_steps(pe, attn_step)
            pe.wait_ge(m_slot, GROUPS)
            pe.matmul(bank[7][:, 0:EXPERTS], cst[0:SEQ, C_ONE:C_ONE + P], base_m[:, :], start=True, stop=True)\
                .then_inc(cnt_mm, 1)

            pe.wait_ge(tbl_ready, 2)
            pe.wait_ge(ld_ffn, 48)

            def turn_block(j, k, turn_):
                pe.wait_ge(x_in[k], turn_ * 16 + 16)
                wait(pe, f_trc, j)
                for d in range(DC):
                    mm = pe.transpose(bank[2][:, d * P:(d + 1) * P], x_g[k][:, d * P:(d + 1) * P], ident)
                mm.then_inc(f_tr, 1)

            def gate_up(j, k):
                e = pe.value_load(expert_i[0:1, bass.ds(j, 1)], min_val=0, max_val=EXPERTS - 1)
                pe.wait_ge(f_trc, j + 1)
                for q, w, sig, free in ((0, wg_s, f_gm, f_silu), (1, wu_s, f_um, f_hh)):
                    wait(pe, free, j)
                    for d in range(DC):
                        mm = pe.matmul(bank[q][:, :], x_gt[k][:, d, :], w[:, d, bass.ds(e * FFN, FFN)], start=(d == 0),
                                       stop=(d == DC - 1))
                    mm.then_inc(sig, 1)

            def turn_hidden(j, k):
                pe.wait_ge(f_hh, j + 1)
                wait(pe, f_htc, j)
                for c in range(FC):
                    mm = pe.transpose(bank[3][:, c * P:(c + 1) * P], f_h[:, c * P:(c + 1) * P], ident)
                mm.then_inc(f_hm, 1)

            def down(j, k):
                e = pe.value_load(expert_i[0:1, bass.ds(j, 1)], min_val=0, max_val=EXPERTS - 1)
                pe.wait_ge(f_htc, j + 1)
                wait(pe, f_yc, j - 1)
                for c in range(FC):
                    mm = pe.matmul(bank[4 + k][:, 0:D], f_ht[k][:, c, :], wd_s[:, c, bass.ds(e * D, D)], start=(c == 0),
                                   stop=(c == FC - 1))
                mm.then_inc(f_dm, 1)

            def expert_step(j, k, turn_):
                gate_up(j, k)
                turn_block(j + 1, 1 - k, turn_)
                down(j - 1, 1 - k)
                turn_hidden(j, k)

            turn_block(0, 0, 0)
            gate_up(0, 0)
            turn_block(1, 1, 0)
            turn_hidden(0, 0)
            expert_step(1, 1, 1)
            expert_step(2, 0, 1)
            with pe.Fori(1, BLOCKS // 2 - 1) as pair:
                expert_step(pair * 2 + 1, 1, pair + 1)
                expert_step(pair * 2 + 2, 0, pair + 1)
            gate_up(BLOCKS - 1, 1)
            down(BLOCKS - 2, 0)
            turn_hidden(BLOCKS - 1, 1)
            down(BLOCKS - 1, 1)

        @block.vector
        def _(dve):
            dve.wait_ge(ld_pos, 16 * (3 + PT_SEQS + PIECES))
            dve.tensor_tensor(posb, posb, tokb, ALU.add).then_inc(posb_ready, 1)
            dve.tensor_tensor(cls_s, cls_s, pos0, ALU.add).then_inc(cls_ready, 1)
            dve.wait_ge(posb_ready, 1)

            def patch_tile(i, k, m, turn_):
                dve.wait_ge(pat_mm, i + 1)
                wait(dve, seq_stored[k], turn_ * (16 * PT_SEQS))
                dve.tensor_tensor(pat_out[k][0:m, :], bank[k][0:m, 0:D], posb[0:m, :], ALU.add).then_inc(pat_ready, 1)

            patch_tile(0, 0, PT, 0)
            patch_tile(1, 1, PT, 0)
            with dve.Fori(1, PT_FULL // 2) as pair:
                for k in range(2):
                    patch_tile(pair * 2 + k, k, PT, pair)
            patch_tile(PT_FULL, 0, PT_TAIL, PT_FULL // 2)

            dve.wait_ge(zeroed, 11)

            def embed(g, k, turn_):
                dve.wait_ge(emb_ready[k], turn_ * (16 * NT) + 16 * NT)
                wait(dve, pe_t, g * 2)
                wait(dve, pool_x, g)
                dve.tensor_tensor(n[:, 0:2, :], emb[k][:, 0:2, :], pos_s[:, 0:2, :], ALU.add).then_inc(dve_n, 2)
                dve.tensor_tensor(n[0:TILE_ROWS[2], 2, :], emb[k][0:TILE_ROWS[2], 2, :], pos_s[0:TILE_ROWS[2], 2, :],
                                  ALU.add).then_inc(dve_n, 1)

            embed(0, 0, 0)
            embed(1, 1, 0)
            with dve.Fori(1, GROUPS // 2) as pair:
                for k in range(2):
                    embed(pair * 2 + k, k, pair)
            dve.wait_ge(ld_cst, 32)
            dve.wait_ge(ld_attn, 48)

            HALF = SEQ // 2
            ohv = oh.rearrange("p (i b) -> p i b", b=32)
            c = Chain(dve, bias_seq, 6, 0)
            bucket = cst[0:SEQ, C_BUCKET:C_BUCKET + SEQ]
            numbers = cst[0:SEQ, C_B32:C_B32 + 32].unsqueeze(1).broadcast_to([SEQ, HALF, 32])
            for half in range(2):
                cut = slice(half * HALF, (half + 1) * HALF)
                if half:
                    c.wait(3)
                v = c.inc(dve.tensor_tensor(ohv, bucket[:, cut].unsqueeze(2).broadcast_to([SEQ, HALF, 32]), numbers,
                                            ALU.is_equal))
                c.wait(v)
                v = c.inc(dve.tensor_tensor(ohv, ohv, tab_s[:, :].unsqueeze(1).broadcast_to([SEQ, HALF, 32]), ALU.mult))
                c.wait(v)
                v = c.inc(dve.tensor_reduce(bias_t[:, cut], ohv, AX, ALU.add))
            c.wait(v)
            dve.tensor_scalar(bias_t[:, :], bias_t[:, :], QK ** 0.5 / LAP_STD, -LAP_MU / LAP_STD, ALU.mult, ALU.add)\
                .then_inc(bias_seq, 1)

            def text_step(layer, g):
                s = layer * GROUPS + g
                lb, gb = back(layer, g, 1)
                lt, gt = back(layer, g, 2)
                sb_, st_ = lb * GROUPS + gb, lt * GROUPS + gt
                late = 0 <= lb < LAYERS
                if 0 <= lt < LAYERS:
                    rows = group_rows(xtok, gt)
                    dve.wait_ge(pool_x, st_ + 1)
                    for j in range(NT):
                        m = TILE_ROWS[j]
                        dve.wait_ge(pe_o, st_ * 3 + (j + 1))
                        dve.tensor_tensor(z[0:m, j, :], bank[5 + j % 2][0:m, 0:D], rows[0:m, j, :], ALU.add)\
                            .then_inc(dve_z, 1)
                    for j in range(NT):
                        m = TILE_ROWS[j]
                        dve.wait_ge(dve_z, st_ * 3 + (j + 1))
                        settled(dve, dve_passed)
                        dve.bn_stats(stats[0:m, j, :], z[0:m, j, :]).then_inc(dve_bn, 1)
                    for j in range(NT):
                        m = TILE_ROWS[j]
                        dve.wait_ge(dve_bn, st_ * 3 + (j + 1))
                        settled(dve, dve_passed)
                        i = dve.bn_aggr(mv[0:m, j, :], stats[0:m, j, :])
                    i.then_inc(dve_stats, 1)
                if layer < LAYERS:
                    taps(layer, s, (2,), 0)
                if 0 <= lt < LAYERS:
                    dve.wait_ge(pool_rstd, st_ + 1)
                    dve.wait_ge(dve_stats, st_ + 1)
                    idx = st_ + GROUPS
                    dve.wait_ge(pe_t, idx * 2 if lt < LAYERS - 1 else ALL_T)
                    dve.wait_ge(pool_x, idx)
                    for j in range(NT):
                        m = TILE_ROWS[j]
                        dve.tensor_scalar(n[0:m, j, :], z[0:m, j, :], mv[0:m, j, 0:1], rstd[0:m, 0, j:j + 1],
                                          ALU.subtract, ALU.mult).then_inc(dve_n, 1)
                if layer < LAYERS:
                    taps(layer, s, (1,), 4)
                if late:
                    dve.wait_ge(act_b, sb_ + 1)
                    wait(dve, pe_c, sb_ * 4)
                    dve.tensor_tensor_scan(hs, decay, bu, 0.0, ALU.mult, ALU.add).then_inc(dve_scan, 1)
                if late:
                    for c in range(FC):
                        dve.wait_ge(pe_c, sb_ * 4 + (c + 1))
                        dve.wait_ge(pe_b, sb_ + 1)
                        dve.scalar_tensor_tensor(u[:, c, :], u[:, c, :], SML(W_D + lb * FC + c),
                                                 bank[(2, 3, 4, 0)[c]][:, 0:GT], ALU.mult, ALU.add).then_inc(dve_c, 1)
                    for c in range(FC):
                        dve.wait_ge(dve_c, sb_ * 4 + (c + 1))
                        dve.wait_ge(act_g, sb_ * 4 + (c + 1))
                        wait(dve, pe_o, sb_ * 3)
                        dve.tensor_tensor(yt[:, c, :], u[:, c, :], sg[:, c, :], ALU.mult).then_inc(dve_y, 1)
                if layer < LAYERS:
                    taps(layer, s, (0,), 8)

            def taps(layer, s, which, first):
                v = first
                for tap in which:
                    for c in range(FC):
                        if v < 4:
                            dve.wait_ge(act_x, s * 4 + (c + 1))
                        else:
                            dve.wait_ge(dve_conv, s * 12 + (v - 3))
                        a = acc[:, c, :].rearrange("p (b t) -> p b t", b=GB)
                        dve.scalar_tensor_tensor(a, xin[:, c, :, tap:tap + TXT], conv_w(layer, c, tap), a,
                                                 ALU.mult, ALU.add).then_inc(dve_conv, 1)
                        v += 1

            text_steps(dve, text_step)

            dve.wait_ge(pool_x, (LAYERS + 1) * GROUPS)
            rows_of = lambda g: h_all[:, bass.ds(g * GB, GB), :]

            def norm_stats(src, st, mv_, chain, stats_sem):
                for b in range(GB):
                    settled(dve, dve_passed)
                    v = chain.inc(dve.bn_stats(st[:, b, :], src[:, b, :]))
                for b in range(GB):
                    chain.wait(v - GB + 1 + b)
                    settled(dve, dve_passed)
                    i = dve.bn_aggr(mv_[:, b, :], st[:, b, :])
                i.then_inc(stats_sem, 1)

            def norm_ahead_stats(g):
                dve.wait_ge(ld_h, g * 16 + 16)
                norm_stats(rows_of(g), a_st, a_mv, Chain(dve, a_bn, 4, g), a_stats)

            def norm_ahead(g):
                h = rows_of(g)
                dve.wait_ge(a_rstd, g + 1)
                dve.wait_ge(a_stats, g + 1)
                wait(dve, a_tr, g * 2)
                for b in range(GB):
                    i = dve.tensor_scalar(a_n[:, b, :], h[:, b, :], a_mv[:, b, 0:1], a_rs[:, 0, b:b + 1],
                                          ALU.subtract, ALU.mult)
                i.then_inc(a_norm, 1)

            def value_bias(g, half):
                dve.wait_ge(a_vm, g * 2 + (half + 1))
                wait(dve, a_vs, g)
                dve.tensor_tensor(a_vb[:, 2 * half:2 * half + 2, :], bank[3][0:SEQ, :].rearrange("p (k d) -> p k d", k=2),
                                  bv_s.unsqueeze(1).broadcast_to([SEQ, 2, D]), ALU.add).then_inc(a_va, 1)

            def query_key(g):
                dve.wait_ge(a_qks, g + 1)
                wait(dve, a_sm, g)
                dve.tensor_scalar(a_q, a_qk, SML(W_QK + 1), SML(W_QK + 3), ALU.mult, ALU.add)
                dve.tensor_scalar(a_k, a_qk, SML(W_QK + 2), SML(W_QK + 4), ALU.mult, ALU.add).then_inc(a_qkd, 1)

            v3 = lambda t: t.rearrange("p (k i) -> p k i", k=GB)
            wide = lambda t: t.unsqueeze(1).broadcast_to([SEQ, GB, SEQ])

            def scale_scores(g):
                dve.wait_ge(a_sm, g + 1)
                wait(dve, a_er, g)
                wait(dve, a_at, g)
                dve.scalar_tensor_tensor(v3(a_arg), v3(bank[4][0:SEQ, 0:GS]), 1.0 / (SEQ * LAP_STD), wide(bias_t[:, :]),
                                         ALU.mult, ALU.add).then_inc(a_rec, 1)
                dve.wait_ge(a_rec, g * 3 + 1)
                dve.tensor_scalar(a_arg, a_arg, TINY, None, ALU.add).then_inc(a_sa, 1)
                dve.wait_ge(a_sa, g + 1)
                dve.reciprocal(a_rc, a_arg).then_inc(a_rec, 1)
                dve.wait_ge(a_rec, g * 3 + 2)
                dve.tensor_tensor(v3(a_rc), v3(a_rc), wide(causal), ALU.mult).then_inc(a_rec, 1)

            def weigh(g):
                dve.wait_ge(a_er, g + 1)
                dve.wait_ge(a_rec, g * 3 + 3)
                dve.tensor_tensor(a_w, a_w, a_rc, ALU.mult).then_inc(a_at, 1)

            def add_attended(g, half):
                dve.wait_ge(a_om, g * 2 + (half + 1))
                two = rows_of(g)[:, 2 * half:2 * half + 2, :]
                dve.tensor_tensor(two, bank[5][0:SEQ, :].rearrange("p (k d) -> p k d", k=2), two, ALU.add)\
                    .then_inc(a_h2, 1)

            def routed_stats(g):
                dve.wait_ge(a_h2, g * 2 + 2)
                norm_stats(rows_of(g), m_st, m_mv, Chain(dve, m_bn, 4, g), m_stats)

            def routed_norm(g, k):
                h = rows_of(g)
                dve.wait_ge(m_rstd, g + 1)
                dve.wait_ge(m_stats, g + 1)
                wait(dve, x_sent[k], (g - k) * (16 * GB))
                for b in range(GB):
                    i = dve.tensor_scalar(a_x[k][0][:, b, 0:D], h[:, b, :], m_mv[:, b, 0:1], m_rs[:, 0, b:b + 1],
                                          ALU.subtract, ALU.mult)
                i.then_inc(m_norm, 1)

            def choose(g, chain):
                dve.wait_ge(m_lm, g + 1)
                v = chain.inc(dve.tensor_copy(lg, bank[7][0:SEQ, 0:GB * 8].rearrange("p (k e) -> p k e", k=GB)))
                chain.wait(v)
                for b in range(GB):
                    settled(dve, dve_passed)
                    v = chain.inc(dve.max(top[:, b, :], lg[:, b, :]))
                for b in range(GB):
                    chain.wait(v - GB + 1 + b)
                    settled(dve, dve_passed)
                    vi = chain.inc(dve.max_index(idx_u[:, b, :], top[:, b, :], lg[:, b, :]))
                wait(dve, m_wt, g)
                dve.tensor_tensor(gap, top[:, :, 0], top[:, :, 1], ALU.subtract).then_inc(m_gap, 1)
                chain.wait(vi)
                v = chain.inc(dve.tensor_copy(idx_f, idx_u[:, :, :]))
                chain.wait(v)
                numbers = expert_no.unsqueeze(1).broadcast_to([SEQ, GB, 8])
                for r in range(2):
                    v = chain.inc(dve.tensor_tensor(one[r], idx_f[:, :, r:r + 1].broadcast_to([SEQ, GB, 8]), numbers,
                                                    ALU.is_equal))
                chain.wait(v)
                v = chain.inc(dve.tensor_tensor(both, one[0], one[1], ALU.add))
                v2 = chain.inc(dve.tensor_copy(before[:, 0, :], base_m[:, :]))
                for b in range(1, GB):
                    chain.wait(v2)
                    v2 = chain.inc(dve.tensor_tensor(before[:, b, :], before[:, b - 1, :], both[:, b - 1, :], ALU.add))
                chain.wait(v2)
                dve.tensor_tensor(base_m[:, :], before[:, GB - 1, :], both[:, GB - 1, :], ALU.add).then_inc(m_both, 1)
                return chain

            def place_rows(g, k, chain):
                dve.wait_ge(m_rk, g + 1)
                v = chain.inc(dve.tensor_tensor(place, bank[7][0:SEQ, 0:GB * 8].rearrange("p (k e) -> p k e", k=GB),
                                                cst[0:SEQ, C_BASE:C_BASE + 8].unsqueeze(1).broadcast_to([SEQ, GB, 8]),
                                                ALU.add))
                chain.wait(v)
                for r in range(2):
                    v = chain.inc(dve.tensor_tensor(picked[r], place, one[r], ALU.mult))
                for r in range(2):
                    chain.wait(v - 1 + r)
                    v3_ = chain.inc(dve.tensor_reduce(slot_f[:, r, :], picked[r], AX, ALU.add))
                chain.wait(v3_)
                dve.tensor_copy(slot_i[k][:, :, :], slot_f)
                toks = cst[0:SEQ, bass.ds(g * GB + C_TOK, GB)]
                for r in range(2):
                    dve.tensor_scalar(a_x[k][r][:, :, D], toks, float(r), None, ALU.add)
                dve.wait_ge(m_wt, g + 1)
                for r in range(2):
                    i = dve.tensor_scalar(a_x[k][r][:, :, D + 1], gap_tanh, 0.5 - r, 0.5, ALU.mult, ALU.add)
                i.then_inc(m_slot, 1)
                chain.done()

            def attn_step(g, k):
                if has(g - 1):
                    scale_scores(g - 1)
                    weigh(g - 1)
                if has(g + 1):
                    norm_ahead_stats(g + 1)
                if has(g):
                    query_key(g)
                if has(g + 1):
                    norm_ahead(g + 1)
                if has(g):
                    value_bias(g, 0)
                chain = Chain(dve, m_seq, 22, g - 2)
                if has(g - 2):
                    choose(g - 2, chain)
                if has(g - 1):
                    add_attended(g - 1, 0)
                    add_attended(g - 1, 1)
                    routed_stats(g - 1)
                if has(g - 2):
                    place_rows(g - 2, k, chain)
                if has(g):
                    value_bias(g, 1)
                if has(g - 1):
                    routed_norm(g - 1, 1 - k)

            dve.wait_ge(ld_late, 32)
            norm_ahead_stats(0)
            norm_ahead(0)
            attention_steps(dve, attn_step)

            c = Chain(dve, tb, 13, 0)
            dve.wait_ge(pad_zero, 1)
            dve.tensor_copy(padbuf[:, :, D], cst[:, C_PADDEST:C_PADDEST + EXPERTS + SPARE]).then_inc(pad_ready, 1)
            dve.wait_ge(cnt_mm, 1)
            v = c.inc(dve.tensor_copy(cnt, bank[7][:, 0:EXPERTS]))
            c.wait(v)
            v = c.inc(dve.tensor_tensor(padrow_f, cnt, cst[:, C_PADROW:C_PADROW + EXPERTS], ALU.add))
            v2 = c.inc(dve.tensor_tensor(steps_b, cnt.unsqueeze(2).broadcast_to([P, EXPERTS, COUNT_STEPS]),
                                         cst[:, C_STEPS:C_STEPS + COUNT_STEPS].unsqueeze(1)
                                         .broadcast_to([P, EXPERTS, COUNT_STEPS]), ALU.is_gt))
            c.wait(v)
            dve.tensor_copy(padrow_i[:, :], padrow_f).then_inc(pad_ready, 1)
            c.wait(v2)
            v = c.inc(dve.tensor_reduce(ntile, steps_b, AX, ALU.add))
            c.wait(v)
            v = c.inc(dve.tensor_tensor_scan(ends, cst[:, C_ONE:C_ONE + EXPERTS], ntile, 0.0, ALU.mult, ALU.add))
            v = c.inc(dve.tensor_scalar(delta, ntile, -float(P), float(REGION), ALU.mult, ALU.add))
            c.wait(v)
            v = c.inc(dve.tensor_scalar(delta[:, EXPERTS - 1:], ends[:, EXPERTS - 2:EXPERTS - 1], float(P),
                                        float(REGION - FULL_BLOCKS * P), ALU.mult, ALU.add))
            v2 = c.inc(dve.tensor_tensor(passed, cst[:, C_BLOCK:C_BLOCK + BLOCKS].unsqueeze(2)
                                         .broadcast_to([P, BLOCKS, EXPERTS]),
                                         ends.unsqueeze(1).broadcast_to([P, BLOCKS, EXPERTS]), ALU.is_ge))
            c.wait(v2)
            v = c.inc(dve.tensor_tensor(shifts, passed, delta.unsqueeze(1).broadcast_to([P, BLOCKS, EXPERTS]), ALU.mult))
            v2 = c.inc(dve.tensor_reduce(expert_f, passed, AX, ALU.add))
            c.wait(v)
            v = c.inc(dve.tensor_reduce(row_f, shifts, AX, ALU.add))
            c.wait(v)
            v = c.inc(dve.scalar_tensor_tensor(row_f, cst[:, C_BLOCK:C_BLOCK + BLOCKS], float(P), row_f, ALU.mult, ALU.add))
            v2 = c.inc(dve.tensor_scalar(expert_f, expert_f, float(EXPERTS - 1), None, ALU.min))
            c.wait(v2)
            dve.tensor_copy(row_i[:, :], row_f).then_inc(tbl_ready, 1)
            dve.tensor_copy(expert_i[:, :], expert_f).then_inc(tbl_ready, 1)
            c.done()
            dve.wait_ge(tbl_ready, 2)

            def hidden(j, k):
                dve.wait_ge(f_silu, j + 1)
                dve.wait_ge(f_um, j + 1)
                wait(dve, f_hm, j)
                dve.tensor_tensor(f_h, bank[1][:, :], f_sg, ALU.mult).then_inc(f_hh, 1)

            def destinations(j, k):
                dve.wait_ge(f_tr, j + 1)
                wait(dve, f_yc, j - 1)
                wait(dve, y_sent[k], (j - k) * 8)
                dve.tensor_copy(row_wt[:, k:k + 1], x_g[k][:, D + 1:D + 2])
                dve.tensor_copy(dest_i[:, k:k + 1], x_g[k][:, D:D + 1]).then_inc(f_dest, 1)

            def hidden_turned(j, k):
                dve.wait_ge(f_hm, j + 1)
                wait(dve, f_dm, j - 1)
                dve.tensor_copy(f_ht[k], bank[3][:, :].rearrange("p (c t) -> p c t", c=FC)).then_inc(f_htc, 1)

            for j in range(2):
                hidden(j, j)
                destinations(j, j)
                hidden_turned(j, j)
            with dve.Fori(1, BLOCKS // 2) as pair:
                for k in range(2):
                    hidden(pair * 2 + k, k)
                    destinations(pair * 2 + k, k)
                    hidden_turned(pair * 2 + k, k)

            for g in range(GROUPS):
                k = g % 2
                c = Chain(dve, yf, 10, g)
                dve.wait_ge(y_in[k], 16 * (g // 2 + 1))
                v = c.inc(dve.tensor_tensor(y_sum, y12[k][:, :, 0:D], y12[k][:, :, D:2 * D], ALU.add))
                c.wait(v)
                norm_stats(y_sum, y_st, y_mv, c, y_stats)
                dve.wait_ge(y_rstd, g + 1)
                dve.wait_ge(y_stats, g + 1)
                for b in range(GB):
                    v = c.inc(dve.tensor_scalar(y_n[:, b, :], y_sum[:, b, :], y_mv[:, b, 0:1], y_rs[:, 0, b:b + 1],
                                                ALU.subtract, ALU.mult))
                c.wait(v)
                v = c.inc(dve.tensor_tensor(y_g, y_n, ffn_s[0:SEQ, 0:1, :].broadcast_to([SEQ, GB, D]), ALU.mult))
                wait(dve, out_sent[k], 16 * (g // 2))
                dve.wait_ge(h2b, BATCH)
                c.wait(v)
                dve.tensor_tensor(y_out[k], y_g, h_all[:, g * GB:(g + 1) * GB, :], ALU.add).then_inc(y_done, 1)
                c.done()


def constants():
    import math

    import numpy as np
    c = np.zeros((P, CONSTS), np.float32)
    p = np.arange(P)[:, None]
    i = np.arange(P)[None, :]
    c[:, C_ID:C_ID + P] = p == i
    c[:, C_TRI:C_TRI + P] = p < i
    c[:, C_CAUSAL:C_CAUSAL + P] = p <= i
    c[:, C_ONE:C_ONE + P] = 1
    dist = np.maximum(i - p, 0)
    large = 16 + (np.log(np.maximum(dist, 1).astype(np.float32) / 16) / math.log(128 / 16) * 16).astype(np.int32)
    c[:, C_BUCKET:C_BUCKET + P] = np.where(dist < 16, dist, np.minimum(large, 31))
    e = np.arange(EXPERTS)
    c[:, C_EXP:C_EXP + EXPERTS] = e
    c[:, C_BASE:C_BASE + EXPERTS] = e * REGION
    c[:, C_PADROW:C_PADROW + EXPERTS] = e * REGION + p
    k = np.arange(EXPERTS + SPARE)
    c[:, C_PADDEST:C_PADDEST + EXPERTS + SPARE] = 2 * TOKENS + k * P + p
    c[:, C_TOK:C_TOK + BATCH] = 2 * (np.arange(BATCH) * SEQ + p)
    c[:, C_STEPS:C_STEPS + COUNT_STEPS] = P * np.arange(COUNT_STEPS)
    c[:, C_BLOCK:C_BLOCK + BLOCKS] = np.arange(BLOCKS)
    c[:, C_B32:C_B32 + 32] = np.arange(32)
    return c


def kernel(**inputs):
    import concourse.bacc as bacc
    import numpy as np
    from concourse.bass_utils import run_bass_kernel_spmd

    a = {k: np.asarray(v) for k, v in inputs.items()}
    rows = lambda w, chunks: w.reshape(chunks, P, -1).transpose(1, 0, 2)

    x = a["x"].reshape(BATCH, 3, 6, 16, 6, 16).transpose(1, 3, 5, 0, 2, 4).reshape(IN_CH // P, P, BATCH * PATCHES)
    full = PT_FULL * PT
    patches = x[:, :, :full].reshape(IN_CH // P, P, PT_FULL, PT).transpose(2, 1, 0, 3)
    tail = x[:, :, full:].transpose(1, 0, 2)
    toks = a["x_txt"].reshape(GROUPS, GT)
    tokens = np.zeros((TR, GROUPS * NT), np.int32)
    for j, (t, m) in enumerate(zip(TILE_AT, TILE_ROWS)):
        tokens[:m, j::NT] = toks[:, t:t + m].T

    per_layer = lambda w, chunks: np.stack([rows(w[l].T, chunks) for l in range(LAYERS)], 1)
    small = np.zeros((P, SMALL), np.float32)
    small[:, W_CONV:W_CB] = a["L0_txt_conv_w"].reshape(LAYERS, FC, P, 4).transpose(2, 0, 1, 3).reshape(P, -1)
    small[:, W_CB:W_D] = a["L0_txt_conv_b"].reshape(LAYERS * FC, P).T
    small[:, W_D:W_LN] = a["L0_txt_D_vec"].reshape(LAYERS * FC, P).T
    small[:, W_LN:W_QK:2] = a["L0_txt_ln_g"].reshape(LAYERS * DC, P).T
    small[:, W_LN + 1:W_QK:2] = a["L0_txt_ln_b"].reshape(LAYERS * DC, P).T
    small[:, W_QK] = a["L0_attn_bqk"]
    small[:, W_QK + 1:W_QK + 3] = a["L0_attn_gamma"].T
    small[:, W_QK + 3:W_QK + 5] = a["L0_attn_beta"].T
    small[:, W_R:] = rows(a["L0_ffn_w_router"].T, DC).reshape(P, -1)

    experts = lambda w, chunks: w.transpose(2, 0, 1).reshape(chunks, P, -1).transpose(1, 0, 2)
    arrays = {
        "patches": patches, "patches_tail": tail, "tokens": tokens,
        "tok_w": rows(a["L0_tok_W"].T, IN_CH // P), "tok_b": a["L0_tok_b"], "cls": a["L0_tok_cls_token"].reshape(D),
        "pos_enc": a["L0_tok_pos_enc"].reshape(1 + PATCHES, D), "tok_emb": a["L0_txt_tok_emb"],
        "pos_emb": a["L0_txt_pos_emb"], "w_in": per_layer(a["L0_txt_W_in"], DC),
        "w_b": per_layer(a["L0_txt_W_B"], FC), "w_c": a["L0_txt_W_C"].transpose(2, 0, 1),
        "w_out": per_layer(a["L0_txt_W_out"], FC), "small": small,
        "ln_gb": np.stack([a["L0_txt_ln_g"], a["L0_txt_ln_b"]], 1),
        "wqk": rows(a["L0_attn_wqk"], DC), "wv": rows(a["L0_attn_wv"], DC), "bv": a["L0_attn_bv"],
        "rel_bias": a["L0_attn_rel_bias"],
        "w_gate": experts(a["L0_ffn_w_gate"], DC), "w_up": experts(a["L0_ffn_w_up"], DC),
        "w_down": experts(a["L0_ffn_w_down"], FC),
        "ffn_gb": np.stack([a["L0_ffn_ln_gamma"], a["L0_ffn_ln_beta"]]), "consts": constants(),
    }
    nc = bacc.Bacc("TRN2", target_bir_lowering=False, num_devices=1)
    arrays = {f"in_{k}": np.ascontiguousarray(v) for k, v in arrays.items()}
    aps = [nc.dram_tensor(k, v.shape, mybir.dt.from_np(v.dtype), kind="ExternalInput").ap() for k, v in arrays.items()]
    aps.append(nc.dram_tensor("out_0", (BATCH, SEQ, D), F32, kind="ExternalOutput").ap())
    build(nc, *aps)
    r = run_bass_kernel_spmd(nc, [arrays], core_ids=[0])
    return r.results[0]["out_0"]
```

```python
from contextlib import ExitStack

import concourse.bass as bass
from concourse import mybir

F32 = mybir.dt.float32
F32R = mybir.dt.float32r
I32 = mybir.dt.int32
U32 = mybir.dt.uint32
ACT = mybir.ActivationFunctionType
ALU = mybir.AluOpType
AX = mybir.AxisListType.X

P = 128
BATCH, TXT, PATCHES = 32, 77, 36
SEQ = 1 + PATCHES + TXT
D = 256
DC = D // P
IN_CH = 768
INNER, STATE, LAYERS = 512, 64, 4
FC = INNER // P
GB = 4
GROUPS = BATCH // GB
GT = GB * TXT
TILE_ROWS = (104, 104, 100)
TILE_AT = (0, 104, 208)
TR = TILE_ROWS[0]
NT = len(TILE_ROWS)
PADT = TXT + 3
PT_SEQS = 3
PT = PT_SEQS * PATCHES
PT_FULL = BATCH // PT_SEQS
PT_TAIL = (BATCH - PT_FULL * PT_SEQS) * PATCHES
QK = 128
GS = GB * SEQ
EXPERTS, FFN = 8, 512
TOKENS = BATCH * SEQ
REGION = TOKENS + P + (-TOKENS) % P
FULL_BLOCKS = 2 * TOKENS // P
BLOCKS = FULL_BLOCKS + EXPERTS - 1
BLOCKS += BLOCKS % 2
SPARE = BLOCKS - FULL_BLOCKS
XROWS = EXPERTS * REGION + SPARE * P
YROWS = 2 * TOKENS + (EXPERTS + SPARE) * P
ROW = D + 2
BIAS_CUT = SEQ // 3
COUNT_STEPS = -(-TOKENS // P)
EPS = 1e-5
LAP_MU = 0.5 ** 0.5
LAP_STD = (0.25 * 3.141592653589793) ** 0.5
TINY = 1e-30

C_ID = 0
C_TRI = C_ID + P
C_CAUSAL = C_TRI + P
C_ONE = C_CAUSAL + P
C_BUCKET = C_ONE + P
C_EXP = C_BUCKET + P
C_BASE = C_EXP + EXPERTS
C_PADDEST = C_BASE + EXPERTS
C_TOK = C_PADDEST + EXPERTS + SPARE
C_STEPS = C_TOK + BATCH
C_BLOCK = C_STEPS + COUNT_STEPS
C_B32 = C_BLOCK + BLOCKS
CONSTS = C_B32 + 32

W_CONV = 0
W_CB = W_CONV + LAYERS * FC * 4
W_D = W_CB + LAYERS * FC
W_LN = W_D + LAYERS * FC
W_QK = W_LN + LAYERS * DC * 2
W_R = W_QK + 5
SMALL = W_R + DC * EXPERTS


class Chain:

    def __init__(self, eng, sem, per, iteration):
        self.eng, self.sem, self.base, self.n, self.per = eng, sem, iteration * per, 0, per

    def inc(self, instruction):
        instruction.then_inc(self.sem, 1)
        self.n += 1
        assert self.n <= self.per
        return self.n

    def wait(self, n):
        self.eng.wait_ge(self.sem, self.base + n)

    def done(self):
        assert self.n == self.per, self.n


def wait(eng, sem, value):
    if not (isinstance(value, int) and value <= 0):
        eng.wait_ge(sem, value)


def settled(eng, sem):
    eng.sem_inc(sem, 1)


def text_steps(eng, body, before_last=None):
    for layer in range(LAYERS):
        body(layer, 0)
        body(layer, 1)
        with eng.Fori(2, GROUPS) as g:
            body(layer, g)
    body(LAYERS, 0)
    if before_last:
        before_last()
    body(LAYERS, 1)


def back(layer, g, k):
    if isinstance(g, int) and g < k:
        return layer - 1, g + GROUPS - k
    return layer, g - k


def group_steps(eng, body, pairs):
    body(0, 0)
    body(1, 1)
    with eng.Fori(1, pairs + 1) as pair:
        for k in range(2):
            body(pair * 2 + k, k)
    for g in range(2 * pairs + 2, GROUPS + 2):
        body(g, g % 2)


def has(g):
    return not isinstance(g, int) or 0 <= g < GROUPS


def build(nc, patches, patches_tail, tokens, tok_w, tok_b, cls, pos_enc, tok_emb, pos_emb, w_in, w_b, w_c, w_out,
          small, ln_gb, wqk, wv, bv, rel_bias, w_gate, w_up, w_down, ffn_gb, consts, out):
    ctx = ExitStack()
    with ctx:
        def sb(name, shape, dt=F32):
            return ctx.enter_context(nc.sbuf_tensor(name, shape, dt))

        def sem(name):
            return ctx.enter_context(nc.semaphore(name))

        seq = nc.dram_tensor("seq", (TOKENS, D), F32, kind="Internal").ap()
        xrows = nc.dram_tensor("xrows", (XROWS, ROW), F32, kind="Internal").ap()
        yrows = nc.dram_tensor("yrows", (YROWS, D), F32, kind="Internal").ap()

        cst = sb("cst", [P, CONSTS])
        sml = sb("sml", [P, SMALL])
        ident = cst[:, C_ID:C_ID + P]
        tri = cst[0:SEQ, C_TRI:C_TRI + SEQ]
        causal = cst[0:SEQ, C_CAUSAL:C_CAUSAL + SEQ]
        ones = cst[0:SEQ, C_ONE:C_ONE + SEQ]
        expert_no = cst[0:SEQ, C_EXP:C_EXP + EXPERTS]
        bias_t = sb("bias_t", [SEQ, SEQ])
        wqk_s = sb("wqk_s", [P, DC, QK])
        wv_s = sb("wv_s", [P, DC, D])
        minus_half = sb("minus_half", [P, GB])
        tab_s = sb("tab_s", [SEQ, 32])
        base_m = sb("base_m", [SEQ, EXPERTS])
        bv_s = sb("bv_s", [SEQ, D])[:, :]
        dest_i = sb("dest_i", [P, 2], I32)
        idx_u = sb("idx_u", [SEQ, GB, 8], U32)
        slot_i = [sb(f"slot_i{k}", [SEQ, 2, GB], I32) for k in range(2)]
        padrow_i = sb("padrow_i", [1, EXPERTS], I32)
        expert_i = sb("expert_i", [P, BLOCKS], I32)
        row_i = sb("row_i", [P, BLOCKS], I32)
        a_rc = sb("a_rc", [SEQ, GS])[:, :]
        a_st = sb("a_st", [SEQ, GB, 6])
        a_mv = sb("a_mv", [SEQ, GB, 2])
        a_rs = sb("a_rs", [SEQ, 2, GB])
        row_wt = sb("row_wt", [P, 2])

        def part(arena, cols, shape=None, rows=P):
            v = arena[0:rows, at[0]:at[0] + cols]
            at[0] += cols
            assert at[0] <= arena.shape[1], (at[0], arena.shape)
            return v

        at = [0]

        arena_b = sb("arena_b", [P, 10240])
        at[0] = 0
        xin = part(arena_b, FC * GB * PADT).rearrange("p (c b t) -> p c b t", c=FC, b=GB)
        acc = part(arena_b, FC * GT).rearrange("p (c t) -> p c t", c=FC)
        u = part(arena_b, FC * GT).rearrange("p (c t) -> p c t", c=FC)
        sg = part(arena_b, FC * GT).rearrange("p (c t) -> p c t", c=FC)
        bu = part(arena_b, GT)
        hs = part(arena_b, GT)
        decay = part(arena_b, GT)
        z = part(arena_b, NT * D, rows=TR).rearrange("p (j d) -> p j d", j=NT)
        n = part(arena_b, NT * D, rows=TR).rearrange("p (j d) -> p j d", j=NT)
        ng = z
        stats = part(arena_b, NT * 6, rows=TR).rearrange("p (j s) -> p j s", j=NT)
        mv = part(arena_b, NT * 2, rows=TR).rearrange("p (j s) -> p j s", j=NT)
        rstd = part(arena_b, 2 * NT, rows=TR).rearrange("p (k j) -> p k j", k=2)
        x_full = [part(arena_b, GT) for _ in range(DC)]
        pos_s = arena_b[0:TR, at[0]:at[0] + NT * D].rearrange("p (j d) -> p j d", j=NT)
        one_hot = part(arena_b, BIAS_CUT * 32, rows=SEQ).rearrange("p (i b) -> p i b", b=32)
        tokens_s = sb("tokens_s", [TR, GROUPS * NT], I32)
        with ExitStack() as text_memory:
            def text_sb(name, shape, dt=F32):
                return text_memory.enter_context(nc.sbuf_tensor(name, shape, dt))

            TEXT_COLS = GROUPS * NT * D + LAYERS * FC * P + LAYERS * 2 * D
            text_a = text_sb("text_a", [P, TEXT_COLS])
            at[0] = 0
            xtok = part(text_a, GROUPS * NT * D, rows=TR)
            wb_s = part(text_a, LAYERS * FC * P).rearrange("p (l c n) -> p l c n", l=LAYERS, c=FC)
            gb_s = part(text_a, LAYERS * 2 * D, rows=TR).rearrange("p (l s d) -> p l s d", l=LAYERS, s=2)
            xt_hi = text_sb("xt_hi", [P, DC, BATCH * TXT], F32R)
            xt_lo = text_sb("xt_lo", [P, DC, BATCH * TXT], F32R)
            hs_halves = text_sb("hs_halves", [P, 2, GT], F32R)
            hs_hi, hs_lo = hs_halves[:, 0, :], hs_halves[0:STATE, 1, :]
            wc_halves = [text_sb(f"wc_halves{k}", [P, INNER], F32R) for k in range(2)]
            wc_raw = text_sb("wc_raw", [P, INNER])
            y_hi = text_sb("y_hi", [P, FC, GT], F32R)
            y_lo = text_sb("y_lo", [P, FC, GT], F32R)
            WIN_COLS, WOUT_COLS = DC * 2 * INNER, FC * D
            W_COLS = WIN_COLS + WOUT_COLS
            w_raw = text_sb("w_raw", [P, W_COLS])
            w_hi, w_lo = [], []
            for k in range(2):
                w_hi.append(text_sb(f"w_hi{k}", [P, W_COLS], F32R))
                w_lo.append(text_sb(f"w_lo{k}", [P, W_COLS], F32R))

        FFN_COLS = DC * EXPERTS * FFN * 2 + FC * EXPERTS * D + 2 * D
        BEFORE_HALVES = TEXT_COLS + 2 * DC * BATCH * TXT + 2 * GT + 3 * INNER + 2 * FC * GT + W_COLS
        assert FFN_COLS <= BEFORE_HALVES
        arena_a = sb("arena_a", [P, BEFORE_HALVES])
        h_all = sb("h_all", [SEQ, BATCH, D])
        padbuf = sb("padbuf", [P, EXPERTS + SPARE, ROW])
        at[0] = 0
        wg_s = part(arena_a, DC * EXPERTS * FFN).rearrange("p (c n) -> p c n", c=DC)
        wu_s = part(arena_a, DC * EXPERTS * FFN).rearrange("p (c n) -> p c n", c=DC)
        wd_s = part(arena_a, FC * EXPERTS * D).rearrange("p (c n) -> p c n", c=FC)
        ffn_s = part(arena_a, 2 * D, rows=SEQ).rearrange("p (s d) -> p s d", s=2)
        m_t = part(arena_a, DC * GS).rearrange("p (c t) -> p c t", c=DC)

        H2 = 2 * W_COLS
        h_flat = h_all[:, :, :].rearrange("p b d -> p (b d)")
        at[0] = FC * GB * PADT
        tokw_s = part(arena_b, IN_CH // P * D).rearrange("p (c d) -> p c d", c=IN_CH // P)
        pat = [part(arena_b, IN_CH // P * PT).rearrange("p (c t) -> p c t", c=IN_CH // P) for _ in range(2)]
        pat_out = [h_flat[0:PT, H2 + k * D:H2 + (k + 1) * D] for k in range(2)]
        posb = h_flat[0:PT, H2 + 2 * D:H2 + 3 * D]
        tokb = h_flat[0:PT, H2 + 3 * D:H2 + 4 * D]
        cls_s = h_flat[0:BATCH, H2 + 4 * D:H2 + 5 * D]
        pos0 = h_flat[0:BATCH, H2 + 5 * D:H2 + 6 * D]

        at[0] = 0
        a_n = part(arena_b, GB * D, rows=SEQ).rearrange("p (k d) -> p k d", k=GB)
        a_nt = part(arena_b, DC * GS).rearrange("p (c t) -> p c t", c=DC)
        a_qk = part(arena_b, GS)
        a_q = part(arena_b, GS)
        a_k = part(arena_b, GS)
        a_v = part(arena_b, GB * D, rows=SEQ).rearrange("p (k d) -> p k d", k=GB)
        a_arg = part(arena_b, GS, rows=SEQ)
        a_w = part(arena_b, GS, rows=SEQ)
        a_x = [[part(arena_b, GB * ROW, rows=SEQ).rearrange("p (k d) -> p k d", k=GB) for _ in range(2)]
               for _ in range(2)]
        m_st = part(arena_b, GB * 6, rows=SEQ).rearrange("p (k s) -> p k s", k=GB)
        m_mv = part(arena_b, GB * 2, rows=SEQ).rearrange("p (k s) -> p k s", k=GB)
        m_rs = part(arena_b, GB * 2, rows=SEQ).rearrange("p (s k) -> p s k", s=2)
        lg = part(arena_b, GB * 8, rows=SEQ).rearrange("p (k e) -> p k e", k=GB)
        top = part(arena_b, GB * 8, rows=SEQ).rearrange("p (k e) -> p k e", k=GB)
        idx_f = part(arena_b, GB * 8, rows=SEQ).rearrange("p (k e) -> p k e", k=GB)
        one = [part(arena_b, GB * 8, rows=SEQ).rearrange("p (k e) -> p k e", k=GB) for _ in range(2)]
        both = part(arena_b, GB * 8, rows=SEQ).rearrange("p (k e) -> p k e", k=GB)
        before = part(arena_b, GB * 8, rows=SEQ).rearrange("p (k e) -> p k e", k=GB)
        place = part(arena_b, GB * 8, rows=SEQ).rearrange("p (k e) -> p k e", k=GB)
        picked = [part(arena_b, GB * 8, rows=SEQ).rearrange("p (k e) -> p k e", k=GB) for _ in range(2)]
        slot_f = part(arena_b, 2 * GB, rows=SEQ).rearrange("p (r k) -> p r k", r=2)
        gap = part(arena_b, GB, rows=SEQ)
        gap_tanh = part(arena_b, GB, rows=SEQ)
        at[0] = 0
        cnt = part(arena_b, EXPERTS)
        padrow_f = part(arena_b, EXPERTS)
        steps_b = part(arena_b, EXPERTS * COUNT_STEPS).rearrange("p (e k) -> p e k", e=EXPERTS)
        ntile = part(arena_b, EXPERTS)
        ends = part(arena_b, EXPERTS)
        delta = part(arena_b, EXPERTS)
        passed = part(arena_b, BLOCKS * EXPERTS).rearrange("p (j e) -> p j e", e=EXPERTS)
        shifts = part(arena_b, BLOCKS * EXPERTS).rearrange("p (j e) -> p j e", e=EXPERTS)
        expert_f = part(arena_b, BLOCKS)
        row_f = part(arena_b, BLOCKS)

        at[0] = 0
        x_g = [part(arena_b, ROW) for _ in range(2)]
        x_gt = [part(arena_b, DC * P).rearrange("p (c t) -> p c t", c=DC) for _ in range(2)]
        f_sg = part(arena_b, FFN)
        f_h = part(arena_b, FFN)
        f_ht = [part(arena_b, FFN).rearrange("p (c t) -> p c t", c=FC) for _ in range(2)]
        f_y = [part(arena_b, D) for _ in range(2)]
        at[0] = 0
        y12 = [part(arena_a, GB * 2 * D, rows=SEQ).rearrange("p (k d) -> p k d", k=GB) for _ in range(2)]
        y_sum = [part(arena_a, GB * D, rows=SEQ).rearrange("p (k d) -> p k d", k=GB) for _ in range(2)]
        y_n = [part(arena_a, GB * D, rows=SEQ).rearrange("p (k d) -> p k d", k=GB) for _ in range(2)]
        y_st = part(arena_a, GB * 6, rows=SEQ).rearrange("p (k s) -> p k s", k=GB)
        y_mv = [part(arena_a, GB * 2, rows=SEQ).rearrange("p (k s) -> p k s", k=GB) for _ in range(2)]
        y_rs = [part(arena_a, GB * 4, rows=SEQ).rearrange("p (s k) -> p s k", s=4) for _ in range(2)]

        bank = [ctx.enter_context(nc.psum_tensor(f"bank{k}", [P, 512], F32)) for k in range(8)]

        ld_cst = sem("ld_cst")
        ld_text = sem("ld_text")
        ld_text_rest = sem("ld_text_rest")
        ld_layer, split_hi, split_lo = sem("ld_layer"), sem("split_hi"), sem("split_lo")
        split_c_hi, split_c = sem("split_c_hi"), sem("split_c")
        xt_split = sem("xt_split")
        ld_tokw = sem("ld_tokw")
        ld_attn = sem("ld_attn")
        ld_pos, ld_txt_pos = sem("ld_pos"), sem("ld_txt_pos")
        ld_late = sem("ld_late")
        ld_toks = sem("ld_toks")
        ld_pat = [sem(f"ld_pat{k}") for k in range(2)]
        ld_ffn = sem("ld_ffn")
        ld_h = sem("ld_h")
        seq_stored = [sem(f"seq_stored{k}") for k in range(3)]
        posb_ready = sem("posb_ready")
        cls_ready = sem("cls_ready")
        pat_mm = sem("pat_mm")
        pat_ready = sem("pat_ready")
        zeroed = sem("zeroed")
        bias_seq = sem("bias_seq")
        emb_ready = [sem(f"emb_ready{k}") for k in range(2)]
        pe_x, act_x = sem("pe_x"), sem("act_x")
        pe_g, act_g = sem("pe_g"), sem("act_g")
        pe_b, act_b = sem("pe_b"), sem("act_b")
        pe_c, dve_c = sem("pe_c"), sem("dve_c")
        dve_gated, act_y, pool_y = sem("dve_gated"), sem("act_y"), sem("pool_y")
        dve_scan, act_u, dve_conv = sem("dve_scan"), sem("act_u"), sem("dve_conv")
        act_hs, dve_hs = sem("act_hs"), sem("dve_hs")
        pe_o, dve_z, dve_bn, dve_stats = sem("pe_o"), sem("dve_z"), sem("dve_bn"), sem("dve_stats")
        pool_var, pool_rstd, dve_n = sem("pool_var"), sem("pool_rstd"), sem("dve_n")
        pe_t, act_xt, pool_ng, x_kept = sem("pe_t"), sem("act_xt"), sem("pool_ng"), sem("x_kept")
        dve_passed, pool_passed, sp_passed, act_passed = (
            sem("dve_passed"), sem("pool_passed"), sem("sp_passed"), sem("act_passed"))
        a_bn, a_var, m_bn, m_var, m_seq = sem("a_bn"), sem("a_var"), sem("m_bn"), sem("m_var"), sem("m_seq")
        a_stats, a_rstd, a_norm = sem("a_stats"), sem("a_rstd"), sem("a_norm")
        a_tr, a_trc, a_qkm, a_qks, a_qkd = sem("a_tr"), sem("a_trc"), sem("a_qkm"), sem("a_qks"), sem("a_qkd")
        a_vm, a_vs = sem("a_vm"), sem("a_vs")
        a_sm, a_sa, a_er, a_at = sem("a_sm"), sem("a_sa"), sem("a_er"), sem("a_at")
        a_rec = sem("a_rec")
        a_om, a_h2 = sem("a_om"), sem("a_h2")
        m_stats, m_rstd, m_norm, m_tr, m_trc = sem("m_stats"), sem("m_rstd"), sem("m_norm"), sem("m_tr"), sem("m_trc")
        m_lm, m_gap, m_wt, m_both, m_rk = sem("m_lm"), sem("m_gap"), sem("m_wt"), sem("m_both"), sem("m_rk")
        m_slot, m_row2, pad_zero = sem("m_slot"), sem("m_row2"), sem("pad_zero")
        x_sent = [sem(f"x_sent{k}") for k in range(2)]
        cnt_mm, tb, tbl_ready, pad_ready, pad_sent, spare_sent = (
            sem("cnt_mm"), sem("tb"), sem("tbl_ready"), sem("pad_ready"), sem("pad_sent"), sem("spare_sent"))
        x_in = [sem(f"x_in{k}") for k in range(2)]
        f_tr, f_trc, f_gm, f_um, f_silu, f_hh = sem("f_tr"), sem("f_trc"), sem("f_gm"), sem("f_um"), sem("f_silu"), sem("f_hh")
        f_hm, f_htc, f_dm, f_yc, f_dest = sem("f_hm"), sem("f_htc"), sem("f_dm"), sem("f_yc"), sem("f_dest")
        y_sent = [sem(f"y_sent{k}") for k in range(2)]
        h2b = sem("h2b")
        y_in = [sem(f"y_in{k}") for k in range(2)]
        y_summed, y_bn, y_stats, y_var, y_rstd, y_normed, y_gained, y_done, out_sent = (
            sem("y_summed"), sem("y_bn"), sem("y_stats"), sem("y_var"), sem("y_rstd"), sem("y_normed"),
            sem("y_gained"), sem("y_done"), sem("out_sent"))

        SML = lambda at_, *_: sml[:, at_:at_ + 1]
        seq_b = seq.rearrange("(b s) d -> b s d", s=SEQ)

        def conv_w(layer, c, tap):
            return SML(W_CONV + (layer * FC + c) * 4 + tap)

        def group_rows(tile, g):
            return tile[:, bass.ds(g * (NT * D), NT * D)].rearrange("p (j d) -> p j d", j=NT)

        N_STEPS = LAYERS * GROUPS
        ZEROED = 8
        ALL_T = 2 * N_STEPS
        pieces = []
        for j in range(NT):
            t = TILE_AT[j]
            while t < TILE_AT[j] + TILE_ROWS[j]:
                b, p = divmod(t, TXT)
                m = min(TXT - p, TILE_AT[j] + TILE_ROWS[j] - t)
                pieces.append((j, t - TILE_AT[j], m, b, p))
                t += m
        PIECES = len(pieces)

        text_weights = ((wb_s[:, :, :, 0:STATE], w_b), (wb_s[:, :, :, STATE:P], w_b))

        def load_layer(eng, layer):
            for dst, src in ((w_raw[:, 0:WIN_COLS].rearrange("p (c n) -> p c n", c=DC), w_in[:, layer]),
                             (w_raw[:, WIN_COLS:].rearrange("p (c n) -> p c n", c=FC), w_out[:, layer]),
                             (wc_raw[0:STATE, :], w_c[:, layer]), (wc_raw[STATE:P, :], w_c[:, layer])):
                eng.dma_start(dst, src).then_inc(ld_layer, 16)

        SPLITS = GROUPS - 2
        SPLIT_COLS = W_COLS // SPLITS
        assert SPLIT_COLS * SPLITS == W_COLS

        def split_part(g):
            return bass.ds(g * SPLIT_COLS - 2 * SPLIT_COLS, SPLIT_COLS)

        def in_half(half, layer, d, cut):
            return half[layer % 2][:, d * 2 * INNER + cut.start:d * 2 * INNER + cut.stop]

        def out_half(half, layer, c):
            return half[layer % 2][:, WIN_COLS + c * D:WIN_COLS + (c + 1) * D]

        OUT_BANKS = (5, 6, 4)
        block = ctx.enter_context(nc.Block())

        @block.sync
        def _(sp):
            sp.dma_start(tokw_s[:, :, :], tok_w).then_inc(ld_tokw, 16)
            for k in range(2):
                sp.dma_start(pat[k][:, :, :], patches[k]).then_inc(ld_pat[k], 16)
            sp.dma_start(cst[:, :], consts).then_inc(ld_cst, 16)
            sp.dma_start(sml[:, :], small).then_inc(ld_cst, 16)

            def store_patches(i, k, seqs=PT_SEQS):
                sp.wait_ge(pat_ready, i + 1)
                for q in range(seqs):
                    sp.dma_start(seq_b[bass.ds(i * PT_SEQS + q, 1), 1:1 + PATCHES, :].rearrange("b s d -> (b s) d"),
                                 pat_out[k][q * PATCHES:(q + 1) * PATCHES, :]).then_inc(seq_stored[k], 16)

            with sp.Fori(0, PT_FULL // 2 - 1) as pair:
                for k in range(2):
                    i = pair * 2 + k
                    sp.wait_ge(pat_mm, i + 1)
                    sp.dma_start(pat[k][:, :, :], patches[bass.ds(i + 2, 1)].rearrange("a p c t -> (a p) c t"))\
                        .then_inc(ld_pat[k], 16)
                    store_patches(i, k)
            sp.wait_ge(pat_mm, PT_FULL - 1)
            sp.dma_start(pat[0][:, :, 0:PT_TAIL], patches_tail).then_inc(ld_pat[0], 16)
            store_patches(PT_FULL - 2, 0)
            store_patches(PT_FULL - 1, 1)
            store_patches(PT_FULL, 0, PT_TAIL // PATCHES)
            sp.wait_ge(cls_ready, 1)
            sp.dma_start(seq_b[:, 0, :], cls_s).then_inc(seq_stored[1], 16)
            for dst, src in text_weights:
                sp.dma_start(dst[:, 1:LAYERS], src[:, 1:LAYERS]).then_inc(ld_text_rest, 16)
            sp.wait_ge(seq_stored[0], 16 * (PT_SEQS * (PT_FULL // 2) + PT_TAIL // PATCHES))
            sp.wait_ge(seq_stored[1], 16 * (PT_SEQS * (PT_FULL // 2) + 1))
            for layer in range(1, LAYERS):
                sp.wait_ge(split_lo, layer * SPLITS)
                sp.wait_ge(split_c, layer)
                load_layer(sp, layer)

            def store_text(g):
                sp.wait_ge(x_kept, g + (LAYERS * GROUPS + 1))
                settled(sp, sp_passed)
                rows = group_rows(xtok, g)
                for j, r0, m, b, p in pieces:
                    sp.dma_start(seq_b[bass.ds(g * GB + b, 1), 1 + PATCHES + p:1 + PATCHES + p + m, :]
                                 .rearrange("b s d -> (b s) d"), rows[r0:r0 + m, j, :]).then_inc(seq_stored[2], 16)

            def load_fused(g):
                sp.wait_ge(seq_stored[2], g * (16 * PIECES) + 16 * PIECES)
                settled(sp, sp_passed)
                wait(sp, ld_h, g * 16)
                settled(sp, sp_passed)
                sp.dma_start(h_all[:, bass.ds(g * GB, GB), :],
                             seq_b[bass.ds(g * GB, GB)].rearrange("b s d -> s b d")).then_inc(ld_h, 16)

            store_text(0)
            load_fused(0)
            with sp.Fori(1, GROUPS // 2) as g:
                store_text(g)
                load_fused(g)
            with sp.Fori(GROUPS // 2, GROUPS) as g:
                store_text(g)
            sp.wait_ge(seq_stored[2], 16 * PIECES * GROUPS)
            with sp.Fori(GROUPS // 2, GROUPS) as g:
                load_fused(g)
            sp.dma_start(ffn_s, ffn_gb.partition_broadcast(SEQ)).then_inc(ld_late, 16)
            for dst, src in ((wg_s, w_gate), (wu_s, w_up), (wd_s, w_down)):
                sp.dma_start(dst, src).then_inc(ld_ffn, 16)

            sp.wait_ge(pad_ready, 1)
            sp.dma_start(xrows[EXPERTS * REGION:XROWS, :].rearrange("(k p) d -> p k d", p=P),
                         padbuf[:, EXPERTS:EXPERTS + SPARE, :]).then_inc(spare_sent, 16)
            sp.wait_ge(pad_ready, 2)
            for e in range(EXPERTS):
                row = sp.value_load(padrow_i[0:1, e:e + 1], min_val=e * REGION, max_val=e * REGION + TOKENS)
                sp.dma_start(xrows[bass.ds(row, P), :], padbuf[:, e, :]).then_inc(pad_sent, 16)

            sp.wait_ge(pad_sent, 16 * EXPERTS)
            sp.wait_ge(spare_sent, 16)
            for k in range(2):
                sp.wait_ge(x_sent[k], 16 * 2 * GB * (GROUPS // 2))
            sp.wait_ge(tbl_ready, 2)

            def load_block(j, k):
                row = sp.value_load(row_i[0:1, bass.ds(j, 1)], min_val=0, max_val=XROWS - P)
                sp.dma_start(x_g[k], xrows[bass.ds(row, P), :]).then_inc(x_in[k], 16)

            load_block(0, 0)
            load_block(1, 1)
            with sp.Fori(1, BLOCKS // 2) as pair:
                for k in range(2):
                    j = pair * 2 + k
                    sp.wait_ge(f_tr, j - 1)
                    sp.wait_ge(f_dest, j - 1)
                    load_block(j, k)

            for k in range(2):
                sp.wait_ge(y_sent[k], 16 * (BLOCKS // 2))

            def final_step(g, k):
                if has(g):
                    wait(sp, y_summed, g - 1)
                    settled(sp, sp_passed)
                    sp.dma_start(y12[k], yrows[bass.ds(g * (2 * GS), 2 * GS)]
                                 .rearrange("(b s r) d -> s b (r d)", s=SEQ, r=2)).then_inc(y_in[k], 16)

            group_steps(sp, final_step, GROUPS // 2 - 1)
            sp.wait_ge(out_sent, 16 * GROUPS)

        @block.scalar
        def _(act):
            act.dma_start(tokens_s[:, :], tokens).then_inc(ld_toks, 16)
            act.dma_start(tokb, tok_b.partition_broadcast(PT)).then_inc(ld_pos, 16)
            for q in range(PT_SEQS):
                act.dma_start(posb[q * PATCHES:(q + 1) * PATCHES, :], pos_enc[1:1 + PATCHES, :]).then_inc(ld_pos, 16)
            act.dma_start(cls_s, cls.partition_broadcast(BATCH)).then_inc(ld_pos, 16)
            act.dma_start(pos0, pos_enc[0].partition_broadcast(BATCH)).then_inc(ld_pos, 16)
            for j, r0, m, b, p in pieces:
                act.dma_start(pos_s[r0:r0 + m, j, :], pos_emb[p:p + m, :]).then_inc(ld_txt_pos, 16)
            load_layer(act, 0)
            for dst, src in text_weights:
                act.dma_start(dst[:, 0:1], src[:, 0:1]).then_inc(ld_text, 16)
            act.dma_start(gb_s[:, :, :, :], ln_gb.partition_broadcast(TR)).then_inc(ld_text, 16)
            act.dma_start(wqk_s[:, :, :], wqk).then_inc(ld_attn, 16)
            act.dma_start(wv_s[:, :, :], wv).then_inc(ld_attn, 16)
            act.dma_start(tab_s[:, :], rel_bias.partition_broadcast(SEQ)).then_inc(ld_attn, 16)
            act.dma_start(bv_s, bv.partition_broadcast(SEQ)).then_inc(ld_attn, 16)
            act.wait_ge(ld_cst, 32)

            def xt_copy(t, g, layer, d):
                act.wait_ge(pe_t, t * 2 + (d + 1))
                wait(act, xt_split, t * 2 + (d - 1))
                hi = xt_hi[:, d, bass.ds(g * GT, GT)]
                if layer < 0:
                    act.activation(x_full[d], bank[7 - d][:, 0:GT], ACT.Copy)
                    act.activation(hi, bank[7 - d][:, 0:GT], ACT.Copy).then_inc(act_xt, 1)
                else:
                    gain, bias = (SML(W_LN + (layer * DC + d) * 2 + k) for k in range(2))
                    act.activation(x_full[d], bank[7][:, 0:GT], ACT.Identity, bias=bias, scale=gain)
                    act.activation(hi, bank[7][:, 0:GT], ACT.Identity, bias=bias, scale=gain).then_inc(act_xt, 1)

            def split_w_c(layer):
                act.wait_ge(ld_layer, 64 * (layer + 1))
                if layer >= 2:
                    act.wait_ge(pe_c, (layer - 1) * GROUPS * FC)
                act.activation(wc_halves[layer % 2][:, :], wc_raw[:, :], ACT.Copy).then_inc(split_c_hi, 1)

            def split_weights(layer, part, parts=1):
                if layer >= 2:
                    act.wait_ge(pe_o, (layer - 1) * GROUPS * NT)
                act.activation(w_hi[layer % 2][:, part], w_raw[:, part], ACT.Copy).then_inc(split_hi, parts)

            for d in range(DC):
                xt_copy(0, 0, -1, d)
            with act.Fori(1, GROUPS // 2) as g:
                for d in range(DC):
                    xt_copy(g, g, -1, d)
            split_w_c(0)
            split_weights(0, slice(0, W_COLS), SPLITS)
            with act.Fori(GROUPS // 2, GROUPS) as g:
                for d in range(DC):
                    xt_copy(g, g, -1, d)

            def upper_half(step, c):
                act.wait_ge(dve_gated, step * 4 + (c + 1))
                wait(act, pe_o, step * 3)
                act.activation(y_hi[:, c, :], u[:, c, :], ACT.Copy).then_inc(act_y, 1)

            def text_step(layer, g):
                s = layer * GROUPS + g
                lb, gb = back(layer, g, 1)
                lt, gt = back(layer, g, 2)
                sb_, st_ = lb * GROUPS + gb, (lt + 1) * GROUPS + gt
                if layer < LAYERS:
                    for c in range(FC):
                        act.wait_ge(pe_x, s * 4 + (c + 1))
                        wait(act, dve_conv, s * 12)
                        wait(act, act_u, s * 4)
                        act.activation(xin[:, c, :, 3:PADT], bank[c][:, 0:GT].rearrange("p (b t) -> p b t", b=GB), ACT.Copy)
                        act.activation(acc[:, c, :], bank[c][:, 0:GT], ACT.Identity,
                                       bias=SML(W_CB + layer * FC + c), scale=conv_w(layer, c, 3)).then_inc(act_x, 1)
                if layer < LAYERS - 1 and not isinstance(g, int):
                    split_weights(layer + 1, split_part(g))
                if 0 <= lb < LAYERS:
                    act.wait_ge(pe_b, sb_ + 1)
                    wait(act, dve_scan, sb_)
                    act.activation(bu, bank[4][:, 0:GT], ACT.Copy, scale=0.05).then_inc(act_b, 1)
                for c in range(FC):
                    if c == 2 and 0 <= lt < LAYERS - 1:
                        xt_copy(st_, gt, lt, 0)
                        xt_copy(st_, gt, lt, 1)
                    if 0 <= lb < LAYERS:
                        act.wait_ge(pe_g, sb_ * 4 + (c + 1))
                        wait(act, dve_gated, sb_ * 4)
                        act.activation(sg[:, c, :], bank[(0, 1, 1, 2)[c]][:, 0:GT], ACT.Silu).then_inc(act_g, 1)
                    if 0 <= lb < LAYERS and c == 0:
                        act.wait_ge(dve_scan, sb_ + 1)
                        wait(act, pe_c, sb_ * 4)
                        act.activation(hs_hi, hs, ACT.Copy).then_inc(act_hs, 1)
                    if 0 <= lb < LAYERS and c == 2:
                        upper_half(sb_, 0)
                if 0 <= lb < LAYERS:
                    for c in range(1, FC):
                        upper_half(sb_, c)
                if layer < LAYERS - 1 and isinstance(g, int) and g == 1:
                    split_w_c(layer + 1)
                if layer < LAYERS:
                    for c in range(FC):
                        act.wait_ge(dve_conv, s * 12 + (9 + c))
                        if not isinstance(s, int) or s > 0:
                            act.wait_ge(pool_y, s * 4 + (c - 3))
                        act.activation(u[:, c, :], acc[:, c, :], ACT.Silu).then_inc(act_u, 1)
            act.wait_ge(zeroed, ZEROED)
            text_steps(act, text_step)

            act.wait_ge(ld_attn, 64)

            def gate_values(g, half):
                act.wait_ge(a_vm, g * 2 + (half + 1))
                wait(act, a_om, g * 2 - 1 + half)
                act.activation(a_v[:, 2 * half:2 * half + 2, :],
                               bank[3][0:SEQ, :].rearrange("p (k d) -> p k d", k=2), ACT.Silu).then_inc(a_vs, 1)

            def attn_step(g, k):
                if has(g):
                    for d in range(DC):
                        act.wait_ge(a_tr, g * 2 + (d + 1))
                        wait(act, a_vm, g * 2)
                        act.activation(a_nt[:, d, :], bank[d][:, 0:GS], ACT.Copy).then_inc(a_trc, 1)
                if has(g - 2):
                    for d in range(DC):
                        act.wait_ge(m_tr, (g - 2) * 2 + (d + 1))
                        wait(act, m_lm, g - 2)
                        act.activation(m_t[:, d, :], bank[(6, 0)[d]][:, 0:GS], ACT.Copy).then_inc(m_trc, 1)
                if has(g - 1):
                    act.wait_ge(a_sa, g)
                    wait(act, a_om, (g - 1) * 2)
                    act.activation(a_w, a_arg, ACT.Gelu).then_inc(a_er, 1)
                if has(g):
                    act.wait_ge(a_qkm, g + 1)
                    wait(act, a_qkd, g)
                    act.activation(a_qk, bank[2][:, 0:GS], ACT.Silu, bias=SML(W_QK)).then_inc(a_qks, 1)
                    act.wait_ge(a_qks, g + 1)
                    wait(act, a_sm, g)
                    act.activation(a_q, a_qk, ACT.Identity, bias=SML(W_QK + 3), scale=SML(W_QK + 1))
                    act.activation(a_k, a_qk, ACT.Identity, bias=SML(W_QK + 4), scale=SML(W_QK + 2))\
                        .then_inc(a_qkd, 1)
                if has(g - 2):
                    act.wait_ge(m_norm, g - 1)
                    act.activation(a_x[k][1][:, :, 0:D], a_x[k][0][:, :, 0:D], ACT.Copy).then_inc(m_row2, 1)
                if has(g):
                    gate_values(g, 0)
                if has(g - 2):
                    act.wait_ge(m_gap, g - 1)
                    act.activation(gap_tanh, gap, ACT.Tanh, scale=0.5).then_inc(m_wt, 1)
                if has(g):
                    gate_values(g, 1)

            group_steps(act, attn_step, GROUPS // 2 - 2)

            def turn(j, k):
                act.wait_ge(f_tr, j + 1)
                wait(act, f_um, j - 1)
                act.activation(x_gt[k], bank[2][:, 0:DC * P].rearrange("p (c t) -> p c t", c=DC), ACT.Copy)\
                    .then_inc(f_trc, 1)

            def gate(j):
                act.wait_ge(f_gm, j + 1)
                wait(act, f_hh, j)
                act.activation(f_sg, bank[0][:, :], ACT.Silu).then_inc(f_silu, 1)

            def back_half(j, k):
                act.wait_ge(f_dm, j + 1)
                wait(act, y_sent[k], (j - k) * 8)
                act.wait_ge(f_dest, j + 1)
                act.activation(f_y[k], bank[4 + k][:, 0:D], ACT.Copy, scale=row_wt[:, k:k + 1]).then_inc(f_yc, 1)

            def expert_step(j, k):
                gate(j)
                turn(j + 1, 1 - k)
                back_half(j - 1, 1 - k)

            act.wait_ge(tbl_ready, 2)
            turn(0, 0)
            gate(0)
            turn(1, 1)
            expert_step(1, 1)
            expert_step(2, 0)
            with act.Fori(1, BLOCKS // 2 - 1) as pair:
                expert_step(pair * 2 + 1, 1)
                expert_step(pair * 2 + 2, 0)
            gate(BLOCKS - 1)
            back_half(BLOCKS - 2, 0)
            back_half(BLOCKS - 1, 1)

            def final_step(g, k):
                if has(g - 2):
                    act.wait_ge(y_done, g - 1)
                    settled(act, act_passed)
                    act.dma_start(out[bass.ds(g * GB - 2 * GB, GB)].rearrange("b s d -> s b d"),
                                  h_all[:, bass.ds(g * GB - 2 * GB, GB), :]).then_inc(out_sent, 16)
                if has(g):
                    act.wait_ge(y_rstd, g + 1)
                    wait(act, y_done, g - 1)
                    for b in range(GB):
                        i = act.activation(y_n[k][:, b, :], y_sum[k][:, b, :], ACT.Identity, bias=y_rs[k][:, 3, b:b + 1],
                                           scale=y_rs[k][:, 0, b:b + 1])
                    i.then_inc(y_normed, 1)

            group_steps(act, final_step, GROUPS // 2 - 1)

        @block.gpsimd
        def _(pool):
            pool.wait_ge(ld_toks, 16)
            for g in range(GROUPS):
                wait(pool, emb_ready[g % 2], g // 2 * (16 * NT))
                for j in range(NT):
                    m = TILE_ROWS[j]
                    pool.indirect_dma_start(group_rows(xtok, g)[0:m, j, :], None, tok_emb,
                                            bass.IndirectOffsetOnAxis(ap=tokens_s[0:m, g * NT + j:g * NT + j + 1], axis=0))\
                        .then_inc(emb_ready[g % 2], 16)
                if g == 0:
                    for t in (z, n, mv):
                        pool.memset(t, 1.0).then_inc(zeroed, 1)
            pool.memset(xin, 0.0).then_inc(zeroed, 1)
            pool.memset(decay, 0.95).then_inc(zeroed, 1)
            pool.wait_ge(zeroed, 5)
            pool.memset(decay.rearrange("p (b t) -> p b t", b=GB)[:, :, 0:1], 0.0).then_inc(zeroed, 1)
            pool.memset(minus_half[:, :], -0.5).then_inc(zeroed, 1)
            pool.memset(base_m[:, :], 0.0).then_inc(zeroed, 1)
            pool.wait_ge(zeroed, ZEROED)

            def split_weights(layer, part, upto, parts=1):
                pool.wait_ge(split_hi, upto)
                pool.tensor_tensor(w_lo[layer % 2][:, part], w_raw[:, part], w_hi[layer % 2][:, part].bitcast(F32),
                                   ALU.subtract).then_inc(split_lo, parts)

            split_weights(0, slice(0, W_COLS), SPLITS, SPLITS)
            pool.wait_ge(ld_text, 48)

            def text_step(layer, g):
                lt, gt = back(layer, g, 2)
                if 0 <= lt < LAYERS:
                    finish_rows(lt, gt, layer, g)
                lb, gb = back(layer, g, 1)
                if 0 <= lb < LAYERS:
                    sb_ = lb * GROUPS + gb
                    for c in range(FC):
                        pool.wait_ge(act_y, sb_ * 4 + (c + 1))
                        pool.tensor_tensor(y_lo[:, c, :], u[:, c, :], y_hi[:, c, :].bitcast(F32), ALU.subtract)\
                            .then_inc(pool_y, 1)
            def finish_rows(lt, gt, layer, g):
                s = lt * GROUPS + gt
                pool.wait_ge(dve_stats, s + 1)
                settled(pool, pool_passed)
                pool.tensor_scalar(rstd[:, 1, :], mv[:, :, 1], EPS, None, ALU.add).then_inc(pool_var, 1)
                pool.wait_ge(pool_var, s + 1)
                pool.tensor_tensor(rstd[:, 0, :], rstd[:, 1, :], minus_half[0:TR, 0:NT], ALU.pow).then_inc(pool_rstd, 1)
                if layer < LAYERS - 1 and not isinstance(g, int):
                    split_weights(layer + 1, split_part(g), g + ((layer + 1) * SPLITS - 1))
                pool.wait_ge(dve_n, (s + GROUPS) * NT + NT)
                gain = gb_s[:, lt, 0:1, :].broadcast_to([TR, NT, D])
                bias = gb_s[:, lt, 1:2, :].broadcast_to([TR, NT, D])
                pool.tensor_tensor(ng, n, gain, ALU.mult).then_inc(pool_ng, 1)
                pool.wait_ge(pool_ng, s + 1)
                pool.tensor_tensor(group_rows(xtok, gt), ng, bias, ALU.add).then_inc(x_kept, 1)
                if lt < LAYERS - 1:
                    t = s + GROUPS
                    for d in range(DC):
                        pool.wait_ge(act_xt, t * 2 + (d + 1))
                        cols = bass.ds(gt * GT, GT)
                        pool.tensor_tensor(xt_lo[:, d, cols], x_full[d], xt_hi[:, d, cols].bitcast(F32), ALU.subtract)\
                            .then_inc(xt_split, 1)

            def rsqrt(mv_, rs, stats_sem, count, chain, rstd_sem):
                pool.wait_ge(stats_sem, count)
                settled(pool, pool_passed)
                v = chain.inc(pool.tensor_scalar(rs[:, 1, :], mv_[:, :, 1], EPS, None, ALU.add))
                chain.wait(v)
                pool.tensor_tensor(rs[:, 0, :], rs[:, 1, :], minus_half[0:SEQ, 0:GB], ALU.pow).then_inc(rstd_sem, 1)

            def norm_ahead(g):
                rsqrt(a_mv, a_rs, a_stats, g + 1, Chain(pool, a_var, 1, g), a_rstd)

            text_steps(pool, text_step, lambda: norm_ahead(0))

            def attn_step(g, k):
                if isinstance(g, int) and g == 0:
                    pool.wait_ge(x_kept, (LAYERS + 1) * GROUPS)
                    pool.memset(padbuf[:, :, :], 0.0).then_inc(pad_zero, 1)
                if has(g - 1):
                    rsqrt(m_mv, m_rs, m_stats, g, Chain(pool, m_var, 1, g - 1), m_rstd)
                if has(g + 2):
                    norm_ahead(g + 2)
                if has(g - 2):
                    pool.wait_ge(m_row2, g - 1)
                    pool.wait_ge(m_slot, g - 1)
                    for r in range(2):
                        for b in range(GB):
                            settled(pool, pool_passed)
                            pool.indirect_dma_start(xrows, bass.IndirectOffsetOnAxis(ap=slot_i[k][:, r, b:b + 1], axis=0),
                                                    a_x[k][r][:, b, :], None).then_inc(x_sent[k], 16)

            norm_ahead(1)
            group_steps(pool, attn_step, GROUPS // 2 - 2)

            def send(j, k):
                pool.wait_ge(f_yc, j + 1)
                pool.wait_ge(f_dest, j + 1)
                settled(pool, pool_passed)
                pool.indirect_dma_start(yrows, bass.IndirectOffsetOnAxis(ap=dest_i[:, k:k + 1], axis=0), f_y[k], None)\
                    .then_inc(y_sent[k], 16)

            assert BLOCKS // 2 == BATCH
            pool.wait_ge(ld_late, 16)
            with pool.Fori(0, BATCH) as pair:
                for k in range(2):
                    send(pair * 2 + k, k)
                one_h = h_all[:, bass.ds(pair, 1), :]
                pool.tensor_tensor(one_h, one_h, ffn_s[:, 1:2, :], ALU.add).then_inc(h2b, 1)

            def final_step(g, k):
                if has(g):
                    pool.wait_ge(y_stats, g + 1)
                    settled(pool, pool_passed)
                    chain, rs = Chain(pool, y_var, 3, g), y_rs[k]
                    v = chain.inc(pool.tensor_scalar(rs[:, 1, :], y_mv[k][:, :, 1], EPS, None, ALU.add))
                    chain.wait(v)
                    v = chain.inc(pool.tensor_tensor(rs[:, 0, :], rs[:, 1, :], minus_half[0:SEQ, 0:GB], ALU.pow))
                    chain.wait(v)
                    v = chain.inc(pool.tensor_tensor(rs[:, 2, :], rs[:, 0, :], y_mv[k][:, :, 0], ALU.mult))
                    chain.wait(v)
                    settled(pool, pool_passed)
                    pool.tensor_scalar(rs[:, 3, :], rs[:, 2, :], -1.0, None, ALU.mult).then_inc(y_rstd, 1)
                if has(g - 1):
                    pool.wait_ge(y_normed, g)
                    n_ = y_n[1 - k]
                    pool.tensor_tensor(n_, n_, ffn_s[0:SEQ, 0:1, :].broadcast_to([SEQ, GB, D]), ALU.mult)\
                        .then_inc(y_gained, 1)

            group_steps(pool, final_step, GROUPS // 2 - 1)

        @block.tensor
        def _(pe):
            def patch_tile(i, k, m, turn_):
                pe.wait_ge(ld_pat[k], turn_ * 16 + 16)
                wait(pe, pat_ready, i - 1)
                for c in range(IN_CH // P):
                    mm = pe.matmul(bank[k][0:m, 0:D], pat[k][:, c, 0:m], tokw_s[:, c, :], start=(c == 0),
                                   stop=(c == IN_CH // P - 1))
                mm.then_inc(pat_mm, 1)

            def turn_embedding(g):
                for d in range(DC):
                    pe.wait_ge(dve_n, g * NT + NT)
                    wait(pe, act_xt, g * 2 + (d - 1))
                    for j in range(NT):
                        m = TILE_ROWS[j]
                        mm = pe.transpose(bank[7 - d][:, TILE_AT[j]:TILE_AT[j] + m], n[0:m, j, d * P:(d + 1) * P],
                                          ident[0:m, 0:m])
                    mm.then_inc(pe_t, 1)

            pe.wait_ge(ld_tokw, 16)
            patch_tile(0, 0, PT, 0)
            patch_tile(1, 1, PT, 0)
            pe.wait_ge(ld_cst, 32)
            for i in (2, 3):
                turn_embedding(i - 2)
                patch_tile(i, i % 2, PT, 1)
            with pe.Fori(2, PT_FULL // 2) as pair:
                for k in range(2):
                    turn_embedding(pair * 2 + (k - 2))
                    patch_tile(pair * 2 + k, k, PT, pair)
            patch_tile(PT_FULL, 0, PT_TAIL, PT_FULL // 2)

            def turn(t, d):
                pe.wait_ge(dve_n, t * NT + NT)
                wait(pe, act_xt, t * 2 + d)
                for j in range(NT):
                    m = TILE_ROWS[j]
                    mm = pe.transpose(bank[7][:, TILE_AT[j]:TILE_AT[j] + m], n[0:m, j, d * P:(d + 1) * P],
                                      ident[0:m, 0:m])
                mm.then_inc(pe_t, 1)

            pe.wait_ge(pat_ready, PT_FULL + 1)
            pe.wait_ge(act_xt, 2 * GROUPS)
            pe.wait_ge(ld_text, 48)

            def text_step(layer, g):
                s = layer * GROUPS + g
                lb, gb = back(layer, g, 1)
                lt, gt = back(layer, g, 2)
                sb_, st_ = lb * GROUPS + gb, (lt + 1) * GROUPS + gt
                late = 0 <= lb < LAYERS
                if layer < LAYERS and isinstance(g, int) and g == 0:
                    pe.wait_ge(split_lo, (layer + 1) * SPLITS)
                if layer == 1 and isinstance(g, int) and g == 0:
                    pe.wait_ge(ld_text_rest, 32)

                def in_product(l, group, c, out_):
                    pairs = [(w, x, d) for d in range(DC) for w, x in ((w_hi, xt_hi), (w_lo, xt_hi), (w_hi, xt_lo))]
                    for i, (w, x, d) in enumerate(pairs):
                        mm = pe.matmul(out_, in_half(w, l, d, slice(c * P, (c + 1) * P)), x[:, d, bass.ds(group * GT, GT)],
                                       start=(i == 0), stop=(i == len(pairs) - 1))
                    return mm

                def out_product(j, y, w, c, start=False, stop=False):
                    m = TILE_ROWS[j]
                    return pe.matmul(bank[OUT_BANKS[j]][0:m, 0:D], y[:, c, TILE_AT[j]:TILE_AT[j] + m], out_half(w, lt, c),
                                     start=start, stop=stop)

                def out_products(so):
                    for j in range(NT):
                        for c in range(FC):
                            if j == 0:
                                pe.wait_ge(act_y, so * 4 + (c + 1))
                            for w in (w_hi, w_lo):
                                out_product(j, y_hi, w, c, start=(c == 0 and w is w_hi))
                    for j in range(NT):
                        for c in range(FC):
                            if j == 0:
                                pe.wait_ge(pool_y, so * 4 + (c + 1))
                            mm = out_product(j, y_lo, w_hi, c, stop=(c == FC - 1))
                        mm.then_inc(pe_o, 1)

                def gate_product(c, b):
                    in_product(lb, gb, FC + c, bank[b][:, 0:GT]).then_inc(pe_g, 1)

                def input_chunk(c):
                    wait(pe, *((dve_c, (s - 1) * 4), (act_g, (s - 2) * 4 + 3), (act_g, (s - 1) * 4),
                               (dve_c, (s - 2) * 4 + 2))[c])
                    if isinstance(s, int) and s == 1:
                        pe.wait_ge(act_x, c + 1)
                    in_product(layer, g, c, bank[c][:, 0:GT]).then_inc(pe_x, 1)

                if layer < LAYERS:
                    pe.wait_ge(xt_split, s * 2 + 2)
                    input_chunk(0)
                    input_chunk(1)
                if 0 <= lt < LAYERS:
                    out_products(lt * GROUPS + gt)
                if layer < LAYERS:
                    input_chunk(2)
                    input_chunk(3)
                if late:
                    for c in range(FC):
                        pe.wait_ge(act_u, sb_ * 4 + (c + 1))
                        wait(pe, dve_z, sb_ * 3)
                        mm = pe.matmul(bank[4][:, 0:GT], wb_s[:, lb, c, :], u[:, c, :], start=(c == 0),
                                       stop=(c == FC - 1))
                    mm.then_inc(pe_b, 1)
                    if layer < LAYERS:
                        pe.wait_ge(act_x, s * 4 + 2)
                    gate_product(0, 0)
                    gate_product(1, 1)
                if 0 <= lt < LAYERS - 1:
                    turn(st_, 0)
                if late:
                    if layer < LAYERS:
                        pe.wait_ge(act_x, s * 4 + 4)
                    if layer < LAYERS and isinstance(g, int) and g == 1:
                        pe.wait_ge(split_c, layer + 1)
                    pe.wait_ge(act_hs, sb_ + 1)
                    for c, b in enumerate((2, 3, 4, 0)):
                        if c == 2:
                            pe.wait_ge(act_b, sb_ + 1)
                        if c == 3:
                            pe.wait_ge(act_g, sb_ * 4 + 1)
                        pe.matmul(bank[b][:, 0:GT], wc_halves[lb % 2][:, c * P:(c + 1) * P], hs_hi,
                                  start=True, stop=False)
                    pe.wait_ge(dve_hs, sb_ + 1)
                    for c, b in enumerate((2, 3, 4, 0)):
                        pe.matmul(bank[b][:, 0:GT], wc_halves[lb % 2][0:STATE, c * P:(c + 1) * P], hs_lo,
                                  start=False, stop=True).then_inc(pe_c, 1)
                if 0 <= lt < LAYERS - 1:
                    turn(st_, 1)
                if late:
                    pe.wait_ge(act_g, sb_ * 4 + 2)
                    gate_product(2, 1)
                    pe.wait_ge(dve_c, sb_ * 4 + 1)
                    gate_product(3, 2)

            text_steps(pe, text_step)

            pe.wait_ge(ld_attn, 64)

            def values(g, half):
                wait(pe, a_vs, g * 2 + half)
                for b in range(2 * half, 2 * half + 2):
                    for d in range(DC):
                        pe.matmul(bank[3][0:SEQ, (b % 2) * D:(b % 2 + 1) * D], a_nt[:, d, b * SEQ:(b + 1) * SEQ],
                                  wv_s[:, d, :], start=(d == 0), stop=False)
                    mm = pe.matmul(bank[3][0:SEQ, (b % 2) * D:(b % 2 + 1) * D], ones[0:1, :], bv_s[0:1, :], start=False,
                                   stop=True)
                mm.then_inc(a_vm, 1)

            def attended(g, half):
                pe.wait_ge(a_at, g + 1)
                pe.wait_ge(a_vs, g * 2 + 2)
                if half == 0:
                    wait(pe, a_h2, g * 2 - 1)
                elif has(g + 1):
                    pe.wait_ge(a_qks, g + 2)
                for b in range(2 * half, 2 * half + 2):
                    mm = pe.matmul(bank[(5, 2)[half]][0:SEQ, (b % 2) * D:(b % 2 + 1) * D], a_w[:, b * SEQ:(b + 1) * SEQ],
                                   a_v[:, b, :], start=True, stop=True)
                mm.then_inc(a_om, 1)

            def turn_routed(g, k, d):
                pe.wait_ge(m_norm, g + 1)
                if d == 1 and has(g + 2):
                    pe.wait_ge(a_trc, (g + 2) * 2 + 1)
                for b in range(GB):
                    mm = pe.transpose(bank[(6, 0)[d]][:, b * SEQ:(b + 1) * SEQ], a_x[k][0][:, b, d * P:(d + 1) * P],
                                      ident[0:SEQ, 0:SEQ])
                mm.then_inc(m_tr, 1)

            def attn_step(g, k):
                if has(g - 1):
                    pe.wait_ge(a_qkd, g)
                    wait(pe, a_sa, g - 1)
                    for b in range(GB):
                        cut = slice(b * SEQ, (b + 1) * SEQ)
                        mm = pe.matmul(bank[4][0:SEQ, cut], a_k[:, cut], a_q[:, cut], start=True, stop=True)
                    mm.then_inc(a_sm, 1)
                if has(g):
                    pe.wait_ge(a_norm, g + 1)
                    for d in range(DC):
                        wait(pe, a_trc, g * 2 + (d - 1))
                        for b in range(GB):
                            mm = pe.transpose(bank[d][:, b * SEQ:(b + 1) * SEQ], a_n[:, b, d * P:(d + 1) * P],
                                              ident[0:SEQ, 0:SEQ])
                        mm.then_inc(a_tr, 1)
                if has(g):
                    pe.wait_ge(a_trc, g * 2 + 2)
                    wait(pe, a_h2, g * 2 - 2)
                    for d in range(DC):
                        mm = pe.matmul(bank[2][:, 0:GS], wqk_s[:, d, :], a_nt[:, d, :], start=(d == 0),
                                       stop=(d == DC - 1))
                    mm.then_inc(a_qkm, 1)
                if has(g - 2):
                    turn_routed(g - 2, k, 0)
                    turn_routed(g - 2, k, 1)
                if has(g):
                    values(g, 0)
                if has(g - 2):
                    pe.wait_ge(m_trc, (g - 2) * 2 + 2)
                    wait(pe, m_slot, g - 2)
                    for b in range(GB):
                        for d in range(DC):
                            at_ = W_R + d * EXPERTS
                            mm = pe.matmul(bank[7][0:SEQ, b * 8:(b + 1) * 8], m_t[:, d, b * SEQ:(b + 1) * SEQ],
                                           sml[:, at_:at_ + EXPERTS], start=(d == 0), stop=(d == DC - 1))
                    mm.then_inc(m_lm, 1)
                if has(g - 1):
                    attended(g - 1, 0)
                    attended(g - 1, 1)
                if has(g):
                    values(g, 1)
                if has(g - 2):
                    pe.wait_ge(m_both, g - 1)
                    pe.matmul(bank[7][0:SEQ, 0:GB * 8], tri, both.rearrange("p k e -> p (k e)"), start=True, stop=False)
                    pe.matmul(bank[7][0:SEQ, 0:GB * 8], ones, before.rearrange("p k e -> p (k e)"), start=False,
                              stop=True).then_inc(m_rk, 1)

            group_steps(pe, attn_step, GROUPS // 2 - 2)
            pe.wait_ge(m_slot, GROUPS)
            pe.matmul(bank[7][:, 0:EXPERTS], cst[0:SEQ, C_ONE:C_ONE + P], base_m[:, :], start=True, stop=True)\
                .then_inc(cnt_mm, 1)

            pe.wait_ge(tbl_ready, 2)
            pe.wait_ge(ld_ffn, 48)

            def turn_block(j, k, turn_):
                pe.wait_ge(x_in[k], turn_ * 16 + 16)
                wait(pe, f_trc, j)
                for d in range(DC):
                    mm = pe.transpose(bank[2][:, d * P:(d + 1) * P], x_g[k][:, d * P:(d + 1) * P], ident)
                mm.then_inc(f_tr, 1)

            def gate_up(j, k):
                e = pe.value_load(expert_i[0:1, bass.ds(j, 1)], min_val=0, max_val=EXPERTS - 1)
                pe.wait_ge(f_trc, j + 1)
                for q, w, sig, free in ((0, wg_s, f_gm, f_silu), (1, wu_s, f_um, f_hh)):
                    wait(pe, free, j)
                    for d in range(DC):
                        mm = pe.matmul(bank[q][:, :], x_gt[k][:, d, :], w[:, d, bass.ds(e * FFN, FFN)], start=(d == 0),
                                       stop=(d == DC - 1))
                    mm.then_inc(sig, 1)

            def turn_hidden(j, k):
                pe.wait_ge(f_hh, j + 1)
                wait(pe, f_htc, j)
                for c in range(FC):
                    mm = pe.transpose(bank[3][:, c * P:(c + 1) * P], f_h[:, c * P:(c + 1) * P], ident)
                mm.then_inc(f_hm, 1)

            def down(j, k):
                e = pe.value_load(expert_i[0:1, bass.ds(j, 1)], min_val=0, max_val=EXPERTS - 1)
                pe.wait_ge(f_htc, j + 1)
                wait(pe, f_yc, j - 1)
                for c in range(FC):
                    mm = pe.matmul(bank[4 + k][:, 0:D], f_ht[k][:, c, :], wd_s[:, c, bass.ds(e * D, D)], start=(c == 0),
                                   stop=(c == FC - 1))
                mm.then_inc(f_dm, 1)

            def expert_step(j, k, turn_):
                gate_up(j, k)
                turn_block(j + 1, 1 - k, turn_)
                down(j - 1, 1 - k)
                turn_hidden(j, k)

            turn_block(0, 0, 0)
            gate_up(0, 0)
            turn_block(1, 1, 0)
            turn_hidden(0, 0)
            expert_step(1, 1, 1)
            expert_step(2, 0, 1)
            with pe.Fori(1, BLOCKS // 2 - 1) as pair:
                expert_step(pair * 2 + 1, 1, pair + 1)
                expert_step(pair * 2 + 2, 0, pair + 1)
            gate_up(BLOCKS - 1, 1)
            down(BLOCKS - 2, 0)
            turn_hidden(BLOCKS - 1, 1)
            down(BLOCKS - 1, 1)

        @block.vector
        def _(dve):
            dve.wait_ge(ld_pos, 16 * (3 + PT_SEQS))
            dve.tensor_tensor(posb, posb, tokb, ALU.add).then_inc(posb_ready, 1)
            dve.tensor_tensor(cls_s, cls_s, pos0, ALU.add).then_inc(cls_ready, 1)
            dve.wait_ge(posb_ready, 1)

            def patch_tile(i, k, m, turn_):
                dve.wait_ge(pat_mm, i + 1)
                wait(dve, seq_stored[k], turn_ * (16 * PT_SEQS))
                dve.tensor_tensor(pat_out[k][0:m, :], bank[k][0:m, 0:D], posb[0:m, :], ALU.add).then_inc(pat_ready, 1)

            def embed(g, k, turn_):
                rows = group_rows(xtok, g)
                dve.wait_ge(emb_ready[k], turn_ * (16 * NT) + 16 * NT)
                wait(dve, pe_t, g * 2)
                cuts = (slice(0, TR), slice(0, 2)), (slice(0, TILE_ROWS[2]), slice(2, 3))
                for (p, j), count in zip(cuts, (2, 1)):
                    dve.tensor_tensor(n[p, j, :], rows[p, j, :], pos_s[p, j, :], ALU.add).then_inc(dve_n, count)
                dve.wait_ge(dve_n, g * NT + NT)
                for p, j in cuts:
                    i = dve.tensor_tensor(rows[p, j, :], rows[p, j, :], pos_s[p, j, :], ALU.add)
                i.then_inc(x_kept, 1)

            def split_input(g):
                cols = bass.ds(g * GT, GT)
                for d in range(DC):
                    dve.wait_ge(act_xt, g * 2 + (d + 1))
                    dve.tensor_tensor(xt_lo[:, d, cols], x_full[d], xt_hi[:, d, cols].bitcast(F32), ALU.subtract)\
                        .then_inc(xt_split, 1)

            bias_chain = Chain(dve, bias_seq, 3 * 3 + 1, 0)

            def bias_part(third):
                c = bias_chain
                cut = slice(third * BIAS_CUT, (third + 1) * BIAS_CUT)
                numbers = cst[0:SEQ, C_B32:C_B32 + 32].unsqueeze(1).broadcast_to([SEQ, BIAS_CUT, 32])
                bucket = cst[0:SEQ, C_BUCKET + cut.start:C_BUCKET + cut.stop].unsqueeze(2)\
                    .broadcast_to([SEQ, BIAS_CUT, 32])
                if third:
                    c.wait(c.n)
                else:
                    dve.wait_ge(ld_attn, 64)
                    dve.wait_ge(x_kept, GROUPS)
                v = c.inc(dve.tensor_tensor(one_hot, bucket, numbers, ALU.is_equal))
                c.wait(v)
                v = c.inc(dve.tensor_tensor(one_hot, one_hot, tab_s[:, :].unsqueeze(1).broadcast_to([SEQ, BIAS_CUT, 32]),
                                            ALU.mult))
                c.wait(v)
                v = c.inc(dve.tensor_reduce(bias_t[:, cut], one_hot, AX, ALU.add))
                if third == 2:
                    c.wait(v)
                    v = c.inc(dve.tensor_scalar(bias_t[:, :], bias_t[:, :], QK ** 0.5 / LAP_STD, -LAP_MU / LAP_STD,
                                            ALU.mult, ALU.add))
                    c.wait(v)
                    c.done()

            patch_tile(0, 0, PT, 0)
            dve.wait_ge(ld_txt_pos, 16 * PIECES)
            dve.wait_ge(zeroed, 3)
            for i in (2, 3):
                embed(i - 2, i % 2, 0)
                patch_tile(i - 1, 1 - i % 2, PT, i // 3)
                split_input(i - 2)
            with dve.Fori(2, PT_FULL // 2) as pair:
                for k in range(2):
                    embed(pair * 2 + (k - 2), k, pair - 1)
                    patch_tile(pair * 2 + (k - 1), 1 - k, PT, pair + (k - 1))
                    split_input(pair * 2 + (k - 2))
            bias_part(0)
            patch_tile(PT_FULL - 1, 1, PT, PT_FULL // 2 - 1)
            patch_tile(PT_FULL, 0, PT_TAIL, PT_FULL // 2)
            dve.wait_ge(zeroed, ZEROED)

            def split_w_c(layer):
                dve.wait_ge(split_c_hi, layer + 1)
                low = wc_halves[layer % 2][STATE:P, :]
                dve.tensor_tensor(low, wc_raw[STATE:P, :], low.bitcast(F32), ALU.subtract).then_inc(split_c, 1)

            def text_step(layer, g):
                s = layer * GROUPS + g
                lb, gb = back(layer, g, 1)
                lt, gt = back(layer, g, 2)
                sb_, st_ = lb * GROUPS + gb, lt * GROUPS + gt
                late = 0 <= lb < LAYERS
                if isinstance(g, int) and g == 0 and layer < LAYERS:
                    split_w_c(layer)
                if 0 <= lt < LAYERS:
                    rows = group_rows(xtok, gt)
                    dve.wait_ge(x_kept, st_ + GROUPS)
                    for j in range(NT):
                        m = TILE_ROWS[j]
                        dve.wait_ge(pe_o, st_ * 3 + (j + 1))
                        dve.tensor_tensor(z[0:m, j, :], bank[OUT_BANKS[j]][0:m, 0:D], rows[0:m, j, :], ALU.add)\
                            .then_inc(dve_z, 1)
                    if layer == LAYERS and g == 1:
                        norm_ahead(0)
                    for j in range(NT):
                        m = TILE_ROWS[j]
                        dve.wait_ge(dve_z, st_ * 3 + (j + 1))
                        settled(dve, dve_passed)
                        dve.bn_stats(stats[0:m, j, :], z[0:m, j, :]).then_inc(dve_bn, 1)
                    for j in range(NT):
                        m = TILE_ROWS[j]
                        dve.wait_ge(dve_bn, st_ * 3 + (j + 1))
                        settled(dve, dve_passed)
                        i = dve.bn_aggr(mv[0:m, j, :], stats[0:m, j, :])
                    i.then_inc(dve_stats, 1)
                if layer < LAYERS:
                    taps(layer, s, (2,), 0)
                if 0 <= lt < LAYERS:
                    dve.wait_ge(pool_rstd, st_ + 1)
                    dve.wait_ge(dve_stats, st_ + 1)
                    idx = st_ + GROUPS
                    dve.wait_ge(pe_t, idx * 2 if lt < LAYERS - 1 else ALL_T)
                    for j in range(NT):
                        m = TILE_ROWS[j]
                        dve.tensor_scalar(n[0:m, j, :], z[0:m, j, :], mv[0:m, j, 0:1], rstd[0:m, 0, j:j + 1],
                                          ALU.subtract, ALU.mult).then_inc(dve_n, 1)
                if late:
                    dve.wait_ge(act_b, sb_ + 1)
                    wait(dve, act_hs, sb_)
                    dve.tensor_tensor_scan(hs, decay, bu, 0.0, ALU.mult, ALU.add).then_inc(dve_scan, 1)
                if layer < LAYERS:
                    taps(layer, s, (1,), 4, (0, 1))
                if late:
                    dve.wait_ge(act_hs, sb_ + 1)
                    wait(dve, pe_c, sb_ * 4)
                    dve.tensor_tensor(hs_lo, hs[0:STATE, :], hs_hi[0:STATE, :].bitcast(F32), ALU.subtract)\
                        .then_inc(dve_hs, 1)
                if layer < LAYERS:
                    taps(layer, s, (1,), 6, (2,))
                if late:
                    for c in range(FC):
                        dve.wait_ge(pe_c, sb_ * 4 + (c + 1))
                        dve.wait_ge(pe_b, sb_ + 1)
                        dve.scalar_tensor_tensor(u[:, c, :], u[:, c, :], SML(W_D + lb * FC + c),
                                                 bank[(2, 3, 4, 0)[c]][:, 0:GT], ALU.mult, ALU.add).then_inc(dve_c, 1)
                    for c in range(FC):
                        dve.wait_ge(dve_c, sb_ * 4 + (c + 1))
                        dve.wait_ge(act_g, sb_ * 4 + (c + 1))
                        dve.tensor_tensor(u[:, c, :], u[:, c, :], sg[:, c, :], ALU.mult).then_inc(dve_gated, 1)
                if layer < LAYERS:
                    taps(layer, s, (1,), 7, (3,))
                    taps(layer, s, (0,), 8)
                if layer == 0 and isinstance(g, int) and g == 0:
                    bias_part(1)

            def taps(layer, s, which, first, chunks=range(FC)):
                v = first
                for tap in which:
                    for c in chunks:
                        if v < 4:
                            dve.wait_ge(act_x, s * 4 + (c + 1))
                        else:
                            dve.wait_ge(dve_conv, s * 12 + (v - 3))
                        a = acc[:, c, :].rearrange("p (b t) -> p b t", b=GB)
                        dve.scalar_tensor_tensor(a, xin[:, c, :, tap:tap + TXT], conv_w(layer, c, tap), a,
                                                 ALU.mult, ALU.add).then_inc(dve_conv, 1)
                        v += 1

            rows_of = lambda g: h_all[:, bass.ds(g * GB, GB), :]

            def norm_stats(src, st, mv_, chain, stats_sem):
                for b in range(GB):
                    settled(dve, dve_passed)
                    v = chain.inc(dve.bn_stats(st[:, b, :], src[:, b, :]))
                for b in range(GB):
                    chain.wait(v - GB + 1 + b)
                    settled(dve, dve_passed)
                    i = dve.bn_aggr(mv_[:, b, :], st[:, b, :])
                i.then_inc(stats_sem, 1)

            def norm_ahead_stats(g):
                dve.wait_ge(ld_h, g * 16 + 16)
                norm_stats(rows_of(g), a_st, a_mv, Chain(dve, a_bn, 4, g), a_stats)

            def norm_ahead(g):
                h = rows_of(g)
                dve.wait_ge(a_rstd, g + 1)
                dve.wait_ge(a_stats, g + 1)
                wait(dve, a_tr, g * 2)
                for b in range(GB):
                    i = dve.tensor_scalar(a_n[:, b, :], h[:, b, :], a_mv[:, b, 0:1], a_rs[:, 0, b:b + 1],
                                          ALU.subtract, ALU.mult)
                i.then_inc(a_norm, 1)

            v3 = lambda t: t.rearrange("p (k i) -> p k i", k=GB)
            wide = lambda t: t.unsqueeze(1).broadcast_to([SEQ, GB, SEQ])

            def scale_scores(g):
                dve.wait_ge(a_sm, g + 1)
                wait(dve, a_er, g)
                wait(dve, a_at, g)
                dve.scalar_tensor_tensor(v3(a_arg), v3(bank[4][0:SEQ, 0:GS]), 1.0 / (SEQ * LAP_STD), wide(bias_t[:, :]),
                                         ALU.mult, ALU.add).then_inc(a_rec, 1)
                dve.wait_ge(a_rec, g * 3 + 1)
                dve.tensor_scalar(a_arg, a_arg, TINY, None, ALU.add).then_inc(a_sa, 1)
                dve.wait_ge(a_sa, g + 1)
                dve.reciprocal(a_rc, a_arg).then_inc(a_rec, 1)
                dve.wait_ge(a_rec, g * 3 + 2)
                dve.tensor_tensor(v3(a_rc), v3(a_rc), wide(causal), ALU.mult).then_inc(a_rec, 1)

            def weigh(g):
                dve.wait_ge(a_er, g + 1)
                dve.wait_ge(a_rec, g * 3 + 3)
                dve.tensor_tensor(a_w, a_w, a_rc, ALU.mult).then_inc(a_at, 1)

            def add_attended(g, half):
                dve.wait_ge(a_om, g * 2 + (half + 1))
                two = rows_of(g)[:, 2 * half:2 * half + 2, :]
                dve.tensor_tensor(two, bank[(5, 2)[half]][0:SEQ, :].rearrange("p (k d) -> p k d", k=2), two, ALU.add)\
                    .then_inc(a_h2, 1)

            def routed_stats(g):
                dve.wait_ge(a_h2, g * 2 + 2)
                norm_stats(rows_of(g), m_st, m_mv, Chain(dve, m_bn, 4, g), m_stats)

            def routed_norm(g, k):
                h = rows_of(g)
                dve.wait_ge(m_rstd, g + 1)
                dve.wait_ge(m_stats, g + 1)
                wait(dve, x_sent[k], (g - k) * (16 * GB))
                for b in range(GB):
                    i = dve.tensor_scalar(a_x[k][0][:, b, 0:D], h[:, b, :], m_mv[:, b, 0:1], m_rs[:, 0, b:b + 1],
                                          ALU.subtract, ALU.mult)
                i.then_inc(m_norm, 1)

            def choose(g, chain):
                dve.wait_ge(m_lm, g + 1)
                v = chain.inc(dve.tensor_copy(lg, bank[7][0:SEQ, 0:GB * 8].rearrange("p (k e) -> p k e", k=GB)))
                chain.wait(v)
                for b in range(GB):
                    settled(dve, dve_passed)
                    v = chain.inc(dve.max(top[:, b, :], lg[:, b, :]))
                for b in range(GB):
                    chain.wait(v - GB + 1 + b)
                    settled(dve, dve_passed)
                    vi = chain.inc(dve.max_index(idx_u[:, b, :], top[:, b, :], lg[:, b, :]))
                wait(dve, m_wt, g)
                dve.tensor_tensor(gap, top[:, :, 0], top[:, :, 1], ALU.subtract).then_inc(m_gap, 1)
                chain.wait(vi)
                v = chain.inc(dve.tensor_copy(idx_f, idx_u[:, :, :]))
                chain.wait(v)
                numbers = expert_no.unsqueeze(1).broadcast_to([SEQ, GB, 8])
                for r in range(2):
                    v = chain.inc(dve.tensor_tensor(one[r], idx_f[:, :, r:r + 1].broadcast_to([SEQ, GB, 8]), numbers,
                                                    ALU.is_equal))
                chain.wait(v)
                v = chain.inc(dve.tensor_tensor(both, one[0], one[1], ALU.add))
                v2 = chain.inc(dve.tensor_copy(before[:, 0, :], base_m[:, :]))
                for b in range(1, GB):
                    chain.wait(v2)
                    v2 = chain.inc(dve.tensor_tensor(before[:, b, :], before[:, b - 1, :], both[:, b - 1, :], ALU.add))
                chain.wait(v2)
                dve.tensor_tensor(base_m[:, :], before[:, GB - 1, :], both[:, GB - 1, :], ALU.add).then_inc(m_both, 1)
                return chain

            def place_rows(g, k, chain):
                dve.wait_ge(m_rk, g + 1)
                v = chain.inc(dve.tensor_tensor(place, bank[7][0:SEQ, 0:GB * 8].rearrange("p (k e) -> p k e", k=GB),
                                                cst[0:SEQ, C_BASE:C_BASE + 8].unsqueeze(1).broadcast_to([SEQ, GB, 8]),
                                                ALU.add))
                chain.wait(v)
                for r in range(2):
                    v = chain.inc(dve.tensor_tensor(picked[r], place, one[r], ALU.mult))
                for r in range(2):
                    chain.wait(v - 1 + r)
                    v3_ = chain.inc(dve.tensor_reduce(slot_f[:, r, :], picked[r], AX, ALU.add))
                chain.wait(v3_)
                dve.tensor_copy(slot_i[k][:, :, :], slot_f)
                toks = cst[0:SEQ, bass.ds(g * GB + C_TOK, GB)]
                for r in range(2):
                    dve.tensor_scalar(a_x[k][r][:, :, D], toks, float(r), None, ALU.add)
                dve.wait_ge(m_wt, g + 1)
                for r in range(2):
                    i = dve.tensor_scalar(a_x[k][r][:, :, D + 1], gap_tanh, 0.5 - r, 0.5, ALU.mult, ALU.add)
                i.then_inc(m_slot, 1)
                chain.done()

            def attn_step(g, k):
                if isinstance(g, int) and g == 1:
                    bias_part(2)
                if has(g - 1):
                    scale_scores(g - 1)
                    weigh(g - 1)
                if has(g + 1):
                    norm_ahead(g + 1)
                chain = Chain(dve, m_seq, 22, g - 2)
                if has(g - 2):
                    choose(g - 2, chain)
                if has(g - 1):
                    add_attended(g - 1, 0)
                    add_attended(g - 1, 1)
                    routed_stats(g - 1)
                if has(g - 2):
                    place_rows(g - 2, k, chain)
                if has(g + 2):
                    norm_ahead_stats(g + 2)
                if isinstance(g, int) and g == 1:
                    dve.wait_ge(pad_zero, 1)
                    dve.tensor_copy(padbuf[:, :, D], cst[:, C_PADDEST:C_PADDEST + EXPERTS + SPARE])\
                        .then_inc(pad_ready, 1)
                    dve.wait_ge(x_kept, (LAYERS + 1) * GROUPS)
                if has(g - 1):
                    routed_norm(g - 1, 1 - k)

            text_steps(dve, text_step, lambda: norm_ahead_stats(0))
            norm_ahead_stats(1)
            group_steps(dve, attn_step, GROUPS // 2 - 2)

            c = Chain(dve, tb, 13, 0)
            dve.wait_ge(cnt_mm, 1)
            v = c.inc(dve.tensor_copy(cnt, bank[7][:, 0:EXPERTS]))
            c.wait(v)
            v = c.inc(dve.tensor_tensor(padrow_f[0:1, :], cnt[0:1, :], cst[0:1, C_BASE:C_BASE + EXPERTS], ALU.add))
            v2 = c.inc(dve.tensor_tensor(steps_b, cnt.unsqueeze(2).broadcast_to([P, EXPERTS, COUNT_STEPS]),
                                         cst[:, C_STEPS:C_STEPS + COUNT_STEPS].unsqueeze(1)
                                         .broadcast_to([P, EXPERTS, COUNT_STEPS]), ALU.is_gt))
            c.wait(v)
            dve.tensor_copy(padrow_i[:, :], padrow_f[0:1, :]).then_inc(pad_ready, 1)
            c.wait(v2)
            v = c.inc(dve.tensor_reduce(ntile, steps_b, AX, ALU.add))
            c.wait(v)
            v = c.inc(dve.tensor_tensor_scan(ends, cst[:, C_ONE:C_ONE + EXPERTS], ntile, 0.0, ALU.mult, ALU.add))
            v = c.inc(dve.tensor_scalar(delta, ntile, -float(P), float(REGION), ALU.mult, ALU.add))
            c.wait(v)
            v = c.inc(dve.tensor_scalar(delta[:, EXPERTS - 1:], ends[:, EXPERTS - 2:EXPERTS - 1], float(P),
                                        float(REGION - FULL_BLOCKS * P), ALU.mult, ALU.add))
            v2 = c.inc(dve.tensor_tensor(passed, cst[:, C_BLOCK:C_BLOCK + BLOCKS].unsqueeze(2)
                                         .broadcast_to([P, BLOCKS, EXPERTS]),
                                         ends.unsqueeze(1).broadcast_to([P, BLOCKS, EXPERTS]), ALU.is_ge))
            c.wait(v2)
            v = c.inc(dve.tensor_tensor(shifts, passed, delta.unsqueeze(1).broadcast_to([P, BLOCKS, EXPERTS]), ALU.mult))
            v2 = c.inc(dve.tensor_reduce(expert_f, passed, AX, ALU.add))
            c.wait(v)
            v = c.inc(dve.tensor_reduce(row_f, shifts, AX, ALU.add))
            c.wait(v)
            v = c.inc(dve.scalar_tensor_tensor(row_f, cst[:, C_BLOCK:C_BLOCK + BLOCKS], float(P), row_f, ALU.mult, ALU.add))
            v2 = c.inc(dve.tensor_scalar(expert_f, expert_f, float(EXPERTS - 1), None, ALU.min))
            c.wait(v2)
            dve.tensor_copy(row_i[:, :], row_f).then_inc(tbl_ready, 1)
            dve.tensor_copy(expert_i[:, :], expert_f).then_inc(tbl_ready, 1)
            c.done()
            dve.wait_ge(tbl_ready, 2)

            def hidden(j, k):
                dve.wait_ge(f_silu, j + 1)
                dve.wait_ge(f_um, j + 1)
                wait(dve, f_hm, j)
                dve.tensor_tensor(f_h, bank[1][:, :], f_sg, ALU.mult).then_inc(f_hh, 1)

            def destinations(j, k):
                dve.wait_ge(f_tr, j + 1)
                wait(dve, f_yc, j - 1)
                wait(dve, y_sent[k], (j - k) * 8)
                dve.tensor_copy(row_wt[:, k:k + 1], x_g[k][:, D + 1:D + 2])
                dve.tensor_copy(dest_i[:, k:k + 1], x_g[k][:, D:D + 1]).then_inc(f_dest, 1)

            def hidden_turned(j, k):
                dve.wait_ge(f_hm, j + 1)
                wait(dve, f_dm, j - 1)
                dve.tensor_copy(f_ht[k], bank[3][:, :].rearrange("p (c t) -> p c t", c=FC)).then_inc(f_htc, 1)

            for j in range(2):
                hidden(j, j)
                destinations(j, j)
                hidden_turned(j, j)
            with dve.Fori(1, BLOCKS // 2) as pair:
                for k in range(2):
                    hidden(pair * 2 + k, k)
                    destinations(pair * 2 + k, k)
                    hidden_turned(pair * 2 + k, k)

            def final_step(g, k):
                if has(g):
                    if isinstance(g, int):
                        dve.wait_ge(y_in[k], 16 * (g // 2 + 1))
                    else:
                        dve.wait_ge(y_in[k], (g - k) * 8 + 16)
                    wait(dve, y_normed, g - 1)
                    dve.tensor_tensor(y_sum[k], y12[k][:, :, 0:D], y12[k][:, :, D:2 * D], ALU.add).then_inc(y_summed, 1)
                    dve.wait_ge(y_summed, g + 1)
                    norm_stats(y_sum[k], y_st, y_mv[k], Chain(dve, y_bn, 4, g), y_stats)
                if has(g - 2):
                    dve.wait_ge(y_gained, g - 1)
                    rows = h_all[:, bass.ds(g * GB - 2 * GB, GB), :]
                    dve.tensor_tensor(rows, rows, y_n[k], ALU.add).then_inc(y_done, 1)

            dve.wait_ge(h2b, BATCH)
            group_steps(dve, final_step, GROUPS // 2 - 1)


def constants():
    import math

    import numpy as np
    c = np.zeros((P, CONSTS), np.float32)
    p = np.arange(P)[:, None]
    i = np.arange(P)[None, :]
    c[:, C_ID:C_ID + P] = p == i
    c[:, C_TRI:C_TRI + P] = p < i
    c[:, C_CAUSAL:C_CAUSAL + P] = p <= i
    c[:, C_ONE:C_ONE + P] = 1
    dist = np.maximum(i - p, 0)
    large = 16 + (np.log(np.maximum(dist, 1).astype(np.float32) / 16) / math.log(128 / 16) * 16).astype(np.int32)
    c[:, C_BUCKET:C_BUCKET + P] = np.where(dist < 16, dist, np.minimum(large, 31))
    e = np.arange(EXPERTS)
    c[:, C_EXP:C_EXP + EXPERTS] = e
    c[:, C_BASE:C_BASE + EXPERTS] = e * REGION
    k = np.arange(EXPERTS + SPARE)
    c[:, C_PADDEST:C_PADDEST + EXPERTS + SPARE] = 2 * TOKENS + k * P + p
    c[:, C_TOK:C_TOK + BATCH] = 2 * (np.arange(BATCH) * SEQ + p)
    c[:, C_STEPS:C_STEPS + COUNT_STEPS] = P * np.arange(COUNT_STEPS)
    c[:, C_BLOCK:C_BLOCK + BLOCKS] = np.arange(BLOCKS)
    c[:, C_B32:C_B32 + 32] = np.arange(32)
    return c


def kernel(**inputs):
    import concourse.bacc as bacc
    import numpy as np
    from concourse.bass_utils import run_bass_kernel_spmd

    a = {k: np.asarray(v) for k, v in inputs.items()}
    rows = lambda w, chunks: w.reshape(chunks, P, -1).transpose(1, 0, 2)

    x = a["x"].reshape(BATCH, 3, 6, 16, 6, 16).transpose(1, 3, 5, 0, 2, 4).reshape(IN_CH // P, P, BATCH * PATCHES)
    full = PT_FULL * PT
    patches = x[:, :, :full].reshape(IN_CH // P, P, PT_FULL, PT).transpose(2, 1, 0, 3)
    tail = x[:, :, full:].transpose(1, 0, 2)
    toks = a["x_txt"].reshape(GROUPS, GT)
    tokens = np.zeros((TR, GROUPS * NT), np.int32)
    for j, (t, m) in enumerate(zip(TILE_AT, TILE_ROWS)):
        tokens[:m, j::NT] = toks[:, t:t + m].T

    per_layer = lambda w, chunks: np.stack([rows(w[l].T, chunks) for l in range(LAYERS)], 1)
    small = np.zeros((P, SMALL), np.float32)
    small[:, W_CONV:W_CB] = a["L0_txt_conv_w"].reshape(LAYERS, FC, P, 4).transpose(2, 0, 1, 3).reshape(P, -1)
    small[:, W_CB:W_D] = a["L0_txt_conv_b"].reshape(LAYERS * FC, P).T
    small[:, W_D:W_LN] = a["L0_txt_D_vec"].reshape(LAYERS * FC, P).T
    small[:, W_LN:W_QK:2] = a["L0_txt_ln_g"].reshape(LAYERS * DC, P).T
    small[:, W_LN + 1:W_QK:2] = a["L0_txt_ln_b"].reshape(LAYERS * DC, P).T
    small[:, W_QK] = a["L0_attn_bqk"]
    small[:, W_QK + 1:W_QK + 3] = a["L0_attn_gamma"].T
    small[:, W_QK + 3:W_QK + 5] = a["L0_attn_beta"].T
    small[:, W_R:] = rows(a["L0_ffn_w_router"].T, DC).reshape(P, -1)

    experts = lambda w, chunks: w.transpose(2, 0, 1).reshape(chunks, P, -1).transpose(1, 0, 2)
    arrays = {
        "patches": patches, "patches_tail": tail, "tokens": tokens,
        "tok_w": rows(a["L0_tok_W"].T, IN_CH // P), "tok_b": a["L0_tok_b"], "cls": a["L0_tok_cls_token"].reshape(D),
        "pos_enc": a["L0_tok_pos_enc"].reshape(1 + PATCHES, D), "tok_emb": a["L0_txt_tok_emb"],
        "pos_emb": a["L0_txt_pos_emb"], "w_in": per_layer(a["L0_txt_W_in"], DC),
        "w_b": per_layer(a["L0_txt_W_B"], FC), "w_c": a["L0_txt_W_C"].transpose(2, 0, 1),
        "w_out": per_layer(a["L0_txt_W_out"], FC), "small": small,
        "ln_gb": np.stack([a["L0_txt_ln_g"], a["L0_txt_ln_b"]], 1),
        "wqk": rows(a["L0_attn_wqk"], DC), "wv": rows(a["L0_attn_wv"], DC), "bv": a["L0_attn_bv"],
        "rel_bias": a["L0_attn_rel_bias"],
        "w_gate": experts(a["L0_ffn_w_gate"], DC), "w_up": experts(a["L0_ffn_w_up"], DC),
        "w_down": experts(a["L0_ffn_w_down"], FC),
        "ffn_gb": np.stack([a["L0_ffn_ln_gamma"], a["L0_ffn_ln_beta"]]), "consts": constants(),
    }
    nc = bacc.Bacc("TRN2", target_bir_lowering=False, num_devices=1)
    arrays = {f"in_{k}": np.ascontiguousarray(v) for k, v in arrays.items()}
    aps = [nc.dram_tensor(k, v.shape, mybir.dt.from_np(v.dtype), kind="ExternalInput").ap() for k, v in arrays.items()]
    aps.append(nc.dram_tensor("out_0", (BATCH, SEQ, D), F32, kind="ExternalOutput").ap())
    build(nc, *aps)
    r = run_bass_kernel_spmd(nc, [arrays], core_ids=[0])
    return r.results[0]["out_0"]
```
